# Optimizing a Trainium2 kernel written in Bass

```python
import numpy as np
import jax
import jax.numpy as jnp

def _softmax(x, axis=-1):
    return jax.nn.softmax(x, axis=axis)

def _gelu(x):
    return jax.nn.gelu(x, approximate=True)

def _silu(x):
    return jax.nn.silu(x)

def _sigmoid(x):
    return jax.nn.sigmoid(x)

def _layernorm(x, axis=-1, eps=1e-05):
    m = jnp.mean(x, axis=axis, keepdims=True)
    v = jnp.var(x, axis=axis, keepdims=True)
    return (x - m) / jnp.sqrt(v + eps)

def _scatter_add(tgt, idx, src, axis=0):
    return tgt.at[idx].add(src)

def _segment_sum(src, seg, n):
    return jax.ops.segment_sum(src, seg, n)
kernel_name = 'mk_seq_postln_d1_jaxref_r4_af8b33'

def setup_inputs(seed: int=0):
    np.random.seed(seed)
    _w = jnp.asarray

    def _L0_attn_setup():
        import jax, jax.numpy as jnp
        import numpy as np
        import math
        B, T, C = (2, 512, 256)
        H = 16
        HS = C // H
        NC = 2 * HS
        G = min(32, NC)
        LAMBDA_INIT = 0.8 - 0.6 * math.exp(-0.3 * (12 - 1))
        EPS = 1e-05

        def _heads(x, W, d):
            b, t, _ = x.shape
            return jnp.einsum('btc,oc->bto', x, W).reshape(b, t, H, d).transpose(0, 2, 1, 3)
        key = jax.random.key(seed)
        ks = jax.random.split(key, 12)
        s = 0.02
        return {'x': jax.random.normal(ks[0], (B, T, C), jnp.float32), 'Wq1': jax.random.normal(ks[1], (C, C), jnp.float32) * s, 'Wq2': jax.random.normal(ks[2], (C, C), jnp.float32) * s, 'Wk1': jax.random.normal(ks[3], (C, C), jnp.float32) * s, 'Wk2': jax.random.normal(ks[4], (C, C), jnp.float32) * s, 'Wv': jax.random.normal(ks[5], (2 * C, C), jnp.float32) * s, 'Wc': jax.random.normal(ks[6], (C, 2 * C), jnp.float32) * s, 'gn_w': jnp.ones((NC,), jnp.float32), 'gn_b': jnp.zeros((NC,), jnp.float32), 'gamma': jnp.ones((NC,), jnp.float32), 'lq1': jnp.full((H, 1, 1), 0.1, jnp.float32), 'lk1': jnp.full((H, 1, 1), 0.1, jnp.float32), 'lq2': jnp.full((H, 1, 1), 0.1, jnp.float32), 'lk2': jnp.full((H, 1, 1), 0.1, jnp.float32)}
    _L0_attn_in = _L0_attn_setup()

    def _L0_ffn_setup():
        import jax, jax.numpy as jnp
        import numpy as np
        DIM = 256
        DEPTH = 2
        HEADS = 8
        DIM_HEAD = 64
        WINDOW = 128
        INNER = HEADS * DIM_HEAD
        HID = int(DIM * 4 * 2 / 3)
        B, N = (2, 2048)
        QK_SCALE = 8.0

        def shift_token(t):
            t1, t2 = jnp.split(t, 2, axis=-1)
            t2 = jnp.pad(t2, ((0, 0), (1, 0), (0, 0)))[:, :-1]
            return jnp.concatenate([t1, t2], axis=-1)

        def l2norm(t):
            return t / jnp.clip(jnp.linalg.norm(t, axis=-1, keepdims=True), 1e-12)

        def rotate_half(x):
            x1, x2 = jnp.split(x, 2, axis=-1)
            return jnp.concatenate([-x2, x1], axis=-1)

        def rotary_xpos(q, k):
            n = q.shape[-2]
            half_idx = jnp.arange(0, DIM_HEAD, 2, dtype=jnp.float32)
            inv_freq = 1.0 / 10000.0 ** (half_idx / DIM_HEAD)
            t = jnp.arange(n, dtype=jnp.float32)
            freqs = t[:, None] * inv_freq[None, :]
            freqs = jnp.concatenate([freqs, freqs], axis=-1)
            base = (half_idx + 0.4 * DIM_HEAD) / (1.4 * DIM_HEAD)
            power = (t - n // 2) / float(WINDOW // 2)
            scale = base[None, :] ** power[:, None]
            scale = jnp.concatenate([scale, scale], axis=-1)
            cos, sin = (jnp.cos(freqs), jnp.sin(freqs))
            q = q * cos * scale + rotate_half(q) * sin * scale
            k = k * cos / scale + rotate_half(k) * sin / scale
            return (q, k)

        def local_attention(q, k, v):
            b, h, n, d = q.shape
            w = n // WINDOW
            bq = q.reshape(b, h, w, WINDOW, d) * QK_SCALE
            bk = k.reshape(b, h, w, WINDOW, d)
            bv = v.reshape(b, h, w, WINDOW, d)

            def look_around(t):
                p = jnp.pad(t, ((0, 0), (0, 0), (1, 0), (0, 0), (0, 0)))
                return jnp.concatenate([p[:, :, :w], p[:, :, 1:]], axis=3)
            bk, bv = (look_around(bk), look_around(bv))
            bt = jnp.arange(n).reshape(w, WINDOW)
            btp = jnp.pad(bt, ((1, 0), (0, 0)), constant_values=-1)
            btk = jnp.concatenate([btp[:w], btp[1:]], axis=1)
            sim = jnp.einsum('bhwid,bhwjd->bhwij', bq, bk)
            i = bt[:, :, None]
            j = btk[:, None, :]
            mask = (i < j) | (i > j + WINDOW) | (j == -1)
            sim = jnp.where(mask, -jnp.finfo(sim.dtype).max, sim)
            attn = jax.nn.softmax(sim, axis=-1)
            out = jnp.einsum('bhwij,bhwjd->bhwid', attn, bv)
            return out.reshape(b, h, n, d)

        def _layer(x, wqkv, qs, ksc, wo, lg, lb, w1, b1, w2, b2):
            b, n, _ = x.shape
            h = shift_token(x)
            qkv = h @ wqkv
            q, k, v = jnp.split(qkv, 3, axis=-1)
            to_heads = lambda t: t.reshape(b, n, HEADS, DIM_HEAD).transpose(0, 2, 1, 3)
            q, k, v = (to_heads(q), to_heads(k), to_heads(v))
            q = l2norm(q) * qs
            k = l2norm(k) * ksc
            q, k = rotary_xpos(q, k)
            o = local_attention(q, k, v)
            o = o.transpose(0, 2, 1, 3).reshape(b, n, INNER)
            x = x + o @ wo
            h = shift_token(x)
            mu = h.mean(-1, keepdims=True)
            var = h.var(-1, keepdims=True)
            h = (h - mu) / jnp.sqrt(var + 1e-05) * lg + lb
            h = h @ w1 + b1
            a, g = jnp.split(h, 2, axis=-1)
            h = a * jax.nn.gelu(g, approximate=False)
            x = x + h @ w2 + b2
            return x
        key = jax.random.key(seed)
        ks = jax.random.split(key, 6)
        return {'x': jax.random.normal(ks[0], (B, N, DIM), jnp.float32), 'wqkv': jax.random.normal(ks[1], (DEPTH, DIM, 3 * INNER), jnp.float32) * 0.02, 'q_scale': jnp.ones((DEPTH, DIM_HEAD), jnp.float32), 'k_scale': jnp.ones((DEPTH, DIM_HEAD), jnp.float32), 'wo': jax.random.normal(ks[2], (DEPTH, INNER, DIM), jnp.float32) * 0.02, 'ln_g': jnp.ones((DEPTH, DIM), jnp.float32), 'ln_b': jnp.zeros((DEPTH, DIM), jnp.float32), 'w1': jax.random.normal(ks[3], (DEPTH, DIM, 2 * HID), jnp.float32) * 0.02, 'b1': jnp.zeros((DEPTH, 2 * HID), jnp.float32), 'w2': jax.random.normal(ks[4], (DEPTH, HID, DIM), jnp.float32) * 0.02, 'b2': jnp.zeros((DEPTH, DIM), jnp.float32)}
    _L0_ffn_in = _L0_ffn_setup()
    _d = {'L0_attn_x': _L0_attn_in['x'], 'L0_attn_Wq1': _L0_attn_in['Wq1'], 'L0_attn_Wq2': _L0_attn_in['Wq2'], 'L0_attn_Wk1': _L0_attn_in['Wk1'], 'L0_attn_Wk2': _L0_attn_in['Wk2'], 'L0_attn_Wv': _L0_attn_in['Wv'], 'L0_attn_Wc': _L0_attn_in['Wc'], 'L0_attn_gn_w': _L0_attn_in['gn_w'], 'L0_attn_gn_b': _L0_attn_in['gn_b'], 'L0_attn_gamma': _L0_attn_in['gamma'], 'L0_attn_lq1': _L0_attn_in['lq1'], 'L0_attn_lk1': _L0_attn_in['lk1'], 'L0_attn_lq2': _L0_attn_in['lq2'], 'L0_attn_lk2': _L0_attn_in['lk2'], 'L0_ffn_wqkv': _L0_ffn_in['wqkv'], 'L0_ffn_q_scale': _L0_ffn_in['q_scale'], 'L0_ffn_k_scale': _L0_ffn_in['k_scale'], 'L0_ffn_wo': _L0_ffn_in['wo'], 'L0_ffn_ln_g': _L0_ffn_in['ln_g'], 'L0_ffn_ln_b': _L0_ffn_in['ln_b'], 'L0_ffn_w1': _L0_ffn_in['w1'], 'L0_ffn_b1': _L0_ffn_in['b1'], 'L0_ffn_w2': _L0_ffn_in['w2'], 'L0_ffn_b2': _L0_ffn_in['b2']}
    _x0 = _d['L0_attn_x']
    _d['L0_attn_x'] = jax.random.normal(jax.random.fold_in(jax.random.key(seed), 1), (8, 1024, 256), dtype=_x0.dtype)
    del _x0
    return _d

def reference(L0_attn_x, L0_attn_Wq1, L0_attn_Wq2, L0_attn_Wk1, L0_attn_Wk2, L0_attn_Wv, L0_attn_Wc, L0_attn_gn_w, L0_attn_gn_b, L0_attn_gamma, L0_attn_lq1, L0_attn_lk1, L0_attn_lq2, L0_attn_lk2, L0_ffn_wqkv, L0_ffn_q_scale, L0_ffn_k_scale, L0_ffn_wo, L0_ffn_ln_g, L0_ffn_ln_b, L0_ffn_w1, L0_ffn_b1, L0_ffn_w2, L0_ffn_b2):

    def _L0_attn_ref(x, Wq1, Wq2, Wk1, Wk2, Wv, Wc, gn_w, gn_b, gamma, lq1, lk1, lq2, lk2):
        import jax, jax.numpy as jnp
        import numpy as np
        import math
        B, T, C = (2, 512, 256)
        H = 16
        HS = C // H
        NC = 2 * HS
        G = min(32, NC)
        LAMBDA_INIT = 0.8 - 0.6 * math.exp(-0.3 * (12 - 1))
        EPS = 1e-05

        def _heads(x, W, d):
            b, t, _ = x.shape
            return jnp.einsum('btc,oc->bto', x, W).reshape(b, t, H, d).transpose(0, 2, 1, 3)
        b, t, c = x.shape
        q1 = _heads(x, Wq1, HS)
        q2 = _heads(x, Wq2, HS)
        k1 = _heads(x, Wk1, HS)
        k2 = _heads(x, Wk2, HS)
        v = _heads(x, Wv, 2 * HS)
        scale = 1.0 / math.sqrt(HS)
        mask = jnp.tril(jnp.ones((t, t), bool))
        neg = jnp.float32(-jnp.inf)
        att1 = jnp.einsum('bhqd,bhkd->bhqk', q1, k1) * scale
        att2 = jnp.einsum('bhqd,bhkd->bhqk', q2, k2) * scale
        att1 = jax.nn.softmax(jnp.where(mask, att1, neg), axis=-1)
        att2 = jax.nn.softmax(jnp.where(mask, att2, neg), axis=-1)
        lam1 = jax.nn.sigmoid(lq1 * lk1)
        lam2 = jax.nn.sigmoid(lq2 * lk2)
        lam = lam1 - lam2 + LAMBDA_INIT
        att = att1 - lam[None] * att2
        y = jnp.einsum('bhqk,bhkd->bhqd', att, v)
        yr = y.reshape(b, H, t, G, NC // G)
        mean = yr.mean(axis=(2, 4), keepdims=True)
        var = ((yr - mean) ** 2).mean(axis=(2, 4), keepdims=True)
        yn = ((yr - mean) * jax.lax.rsqrt(var + EPS)).reshape(b, H, t, NC)
        yn = yn * gn_w + gn_b
        yn = yn * gamma
        yn = yn * (1.0 - LAMBDA_INIT)
        y2 = yn.transpose(0, 2, 1, 3).reshape(b, t, 2 * c)
        out = jnp.einsum('btf,of->bto', y2, Wc)
        return out

    def _L0_ffn_ref(x, wqkv, q_scale, k_scale, wo, ln_g, ln_b, w1, b1, w2, b2):
        import jax, jax.numpy as jnp
        import numpy as np
        DIM = 256
        DEPTH = 2
        HEADS = 8
        DIM_HEAD = 64
        WINDOW = 128
        INNER = HEADS * DIM_HEAD
        HID = int(DIM * 4 * 2 / 3)
        B, N = (2, 2048)
        QK_SCALE = 8.0

        def shift_token(t):
            t1, t2 = jnp.split(t, 2, axis=-1)
            t2 = jnp.pad(t2, ((0, 0), (1, 0), (0, 0)))[:, :-1]
            return jnp.concatenate([t1, t2], axis=-1)

        def l2norm(t):
            return t / jnp.clip(jnp.linalg.norm(t, axis=-1, keepdims=True), 1e-12)

        def rotate_half(x):
            x1, x2 = jnp.split(x, 2, axis=-1)
            return jnp.concatenate([-x2, x1], axis=-1)

        def rotary_xpos(q, k):
            n = q.shape[-2]
            half_idx = jnp.arange(0, DIM_HEAD, 2, dtype=jnp.float32)
            inv_freq = 1.0 / 10000.0 ** (half_idx / DIM_HEAD)
            t = jnp.arange(n, dtype=jnp.float32)
            freqs = t[:, None] * inv_freq[None, :]
            freqs = jnp.concatenate([freqs, freqs], axis=-1)
            base = (half_idx + 0.4 * DIM_HEAD) / (1.4 * DIM_HEAD)
            power = (t - n // 2) / float(WINDOW // 2)
            scale = base[None, :] ** power[:, None]
            scale = jnp.concatenate([scale, scale], axis=-1)
            cos, sin = (jnp.cos(freqs), jnp.sin(freqs))
            q = q * cos * scale + rotate_half(q) * sin * scale
            k = k * cos / scale + rotate_half(k) * sin / scale
            return (q, k)

        def local_attention(q, k, v):
            b, h, n, d = q.shape
            w = n // WINDOW
            bq = q.reshape(b, h, w, WINDOW, d) * QK_SCALE
            bk = k.reshape(b, h, w, WINDOW, d)
            bv = v.reshape(b, h, w, WINDOW, d)

            def look_around(t):
                p = jnp.pad(t, ((0, 0), (0, 0), (1, 0), (0, 0), (0, 0)))
                return jnp.concatenate([p[:, :, :w], p[:, :, 1:]], axis=3)
            bk, bv = (look_around(bk), look_around(bv))
            bt = jnp.arange(n).reshape(w, WINDOW)
            btp = jnp.pad(bt, ((1, 0), (0, 0)), constant_values=-1)
            btk = jnp.concatenate([btp[:w], btp[1:]], axis=1)
            sim = jnp.einsum('bhwid,bhwjd->bhwij', bq, bk)
            i = bt[:, :, None]
            j = btk[:, None, :]
            mask = (i < j) | (i > j + WINDOW) | (j == -1)
            sim = jnp.where(mask, -jnp.finfo(sim.dtype).max, sim)
            attn = jax.nn.softmax(sim, axis=-1)
            out = jnp.einsum('bhwij,bhwjd->bhwid', attn, bv)
            return out.reshape(b, h, n, d)

        def _layer(x, wqkv, qs, ksc, wo, lg, lb, w1, b1, w2, b2):
            b, n, _ = x.shape
            h = shift_token(x)
            qkv = h @ wqkv
            q, k, v = jnp.split(qkv, 3, axis=-1)
            to_heads = lambda t: t.reshape(b, n, HEADS, DIM_HEAD).transpose(0, 2, 1, 3)
            q, k, v = (to_heads(q), to_heads(k), to_heads(v))
            q = l2norm(q) * qs
            k = l2norm(k) * ksc
            q, k = rotary_xpos(q, k)
            o = local_attention(q, k, v)
            o = o.transpose(0, 2, 1, 3).reshape(b, n, INNER)
            x = x + o @ wo
            h = shift_token(x)
            mu = h.mean(-1, keepdims=True)
            var = h.var(-1, keepdims=True)
            h = (h - mu) / jnp.sqrt(var + 1e-05) * lg + lb
            h = h @ w1 + b1
            a, g = jnp.split(h, 2, axis=-1)
            h = a * jax.nn.gelu(g, approximate=False)
            x = x + h @ w2 + b2
            return x
        for l in range(DEPTH):
            x = _layer(x, wqkv[l], q_scale[l], k_scale[l], wo[l], ln_g[l], ln_b[l], w1[l], b1[l], w2[l], b2[l])
        return x
    x = L0_attn_x
    x = _layernorm(x + _L0_attn_ref(x, L0_attn_Wq1, L0_attn_Wq2, L0_attn_Wk1, L0_attn_Wk2, L0_attn_Wv, L0_attn_Wc, L0_attn_gn_w, L0_attn_gn_b, L0_attn_gamma, L0_attn_lq1, L0_attn_lk1, L0_attn_lq2, L0_attn_lk2), axis=-1)
    x = _layernorm(x + _L0_ffn_ref(x, L0_ffn_wqkv, L0_ffn_q_scale, L0_ffn_k_scale, L0_ffn_wo, L0_ffn_ln_g, L0_ffn_ln_b, L0_ffn_w1, L0_ffn_b1, L0_ffn_w2, L0_ffn_b2), axis=-1)
    return x

_drawn_inputs = setup_inputs


def setup_inputs(seed=0):
    import zlib

    import numpy as np

    out = dict(_drawn_inputs(seed))
    spreads = {'L0_attn_gn_w': (1.0, 0.6),
     'L0_attn_gn_b': (0.0, 0.8),
     'L0_attn_gamma': (1.0, 0.6),
     'L0_attn_lq1': (0.10000000149011612, 0.6),
     'L0_attn_lk1': (0.10000000149011612, 0.6),
     'L0_attn_lq2': (0.10000000149011612, 0.6),
     'L0_attn_lk2': (0.10000000149011612, 0.6),
     'L0_ffn_q_scale': (1.0, 0.6),
     'L0_ffn_k_scale': (1.0, 0.6),
     'L0_ffn_ln_g': (1.0, 0.6),
     'L0_ffn_ln_b': (0.0, 0.8),
     'L0_ffn_b1': (0.0, 0.8),
     'L0_ffn_b2': (0.0, 0.1)}
    factors = {'L0_ffn_wqkv': 3.114, 'L0_ffn_wo': 3.101}
    for name, (base, spread) in spreads.items():
        noise = np.random.default_rng([zlib.crc32(name.encode()), seed]).standard_normal(out[name].shape)
        drawn = base * np.exp(spread * noise) if base else spread * noise
        out[name] = jnp.asarray(drawn.astype(out[name].dtype))
    for name, factor in factors.items():
        out[name] = (out[name] * factor).astype(out[name].dtype)
    return out
```

```python
import math
from contextlib import ExitStack

import concourse.bass as bass
from concourse import mybir

F32 = mybir.dt.float32
BF16 = mybir.dt.bfloat16
ALU = mybir.AluOpType
ACT = mybir.ActivationFunctionType
AX_X = mybir.AxisListType.X

P = 128
EPS = 1e-5
NEG = -3.0e38
START = 64

HEADS = 16
HS = 16
VC = 2 * HS
LAMBDA_INIT = 0.8 - 0.6 * math.exp(-0.3 * (12 - 1))
SCALE = 1.0 / math.sqrt(HS)
Q_PARTS = (0, 0, 0, 1, 1, 2)
K_PARTS = (0, 1, 2, 0, 1, 0)
KDIM = HS * len(Q_PARTS)
KALL = KDIM + 2
UNROLL = 4


LAYERS = 2
LHEADS = 8
LD = 64
WIN = 8
HID = 682
HB = 6
HP = -(-HID // HB)
NORM_SHIFT = 10


def done(n):
    return n + START


def sent(n):
    return 16 * n + START


def max_pieces():
    out = []
    for r in range(8):
        for c0 in range(0, (r + 1) * P, 512):
            c1 = min(c0 + 512, (r + 1) * P)
            out.append((r, c0, c1 - c0, c1 == (r + 1) * P))
    return out


def halves(kb):
    out = []
    for half in range(2):
        lo, hi = max(kb * P, half * 512), (half + 1) * 512
        if lo < hi:
            out.append((half, lo, hi))
    return out


PIECES = max_pieces()
SLOTS = 2 * len(PIECES) + 1
QKV_SLOTS = 24


def program(nc, d, nb):
    with ExitStack() as ctx:
        top = [nc.sbuf_base]

        def sb(name, shape, dt):
            n = 2 if dt == BF16 else 4
            for x in shape[1:]:
                n *= x
            at = (top[0] + 31) // 32 * 32
            top[0] = at + n
            return nc.alloc_sbuf_tensor_at(name, shape, dt, offset=at)

        def sem(name):
            s = ctx.enter_context(nc.semaphore(name))
            counters.append(s)
            return s

        counters = []
        ps = ctx.enter_context(nc.psum_tensor("ps", [P, 8, 512], F32))
        psb = ps[:, :, :].bitcast(BF16)

        ones = sb("ones", [P, VC], F32)
        mean_w = sb("mean_w", [P, P], F32)
        eps_c = sb("eps_c", [P, 1], F32)
        sq = sb("sq", [P, 2, 512], F32)
        rl = sb("rl", [P, 512], F32)
        identf = sb("identf", [P, P], F32)
        base_ab = top[0]
        ident_b = sb("ident_b", [P, P], BF16)
        causal = sb("causal", [P, 512], F32)
        wqk = sb("wqk", [P, 2, 4, 2, P], F32)
        wv = sb("wv", [P, 2, 512], F32)
        wc = sb("wc", [P, 4, 256], F32)
        gnp = sb("gnp", [P, 3], F32)
        gsc = sb("gsc", [P, 2], F32)
        lam_in = sb("lam_in", [P, 4, HEADS], F32)
        lam_t = sb("lam_t", [P, 2, HEADS], F32)
        nlam = sb("nlam", [P, HEADS, VC], F32)
        xt = sb("xt", [P, 2, 1024], F32)
        part = sb("part", [P, 3, 4, 2, 1024], BF16)
        rest = sb("rest", [P, 2, 512], F32)
        qt = sb("qt", [P, UNROLL, 2, 1024], BF16)
        kt = sb("kt", [P, UNROLL, 2, 1024], BF16)
        va = sb("va", [P, 8, 512], F32)
        vs = sb("vs", [P, 2, 8, 2, VC], F32)
        pt = sb("pt", [P, 2, 2, 1024], F32)
        junk = sb("junk", [P, 2, 512], BF16)
        mc = sb("mc", [P, 2, 2, 8], F32)
        mm = sb("mm", [P, 2, 8], F32)
        nm = sb("nm", [P, 2, 2, 8], BF16)
        mt = sb("mt", [32, P], BF16)
        ev = sb("ev", [P, 1024], F32)
        rb = sb("rb", [64, 1024], F32)
        wy = sb("wy", [64, 2, 1024], F32)
        ya = sb("ya", [P, 4, 1024], F32)
        yb = sb("yb", [P, 4, 1024], F32)
        bs = sb("bs", [P, 4, 2, 6], F32)
        mv = sb("mv", [P, 4, 2], F32)
        gl = sb("gl", [P, 4], F32)
        ga = sb("ga", [P, 4], F32)
        gb = sb("gb", [P, 4], F32)
        z = yb[:, 0:2, :]

        top[0] = base_ab
        window = sb("window", [P, 2, 256], F32)
        wqkv = sb("wqkv", [P, 2, 1536], F32)
        wo = sb("wo", [P, 4, 256], F32)
        w1 = sb("w1", [P, 2, 2, HB, HP], F32)
        w2 = sb("w2", [HP, HB, 256], F32)
        tabc = sb("tabc", [P, WIN, 4, LD], F32)
        tab = sb("tab", [P, WIN, 4, LD], F32)
        scl = sb("scl", [P, 4, LD], F32)
        lnp = sb("lnp", [P, 2, 2], F32)
        b1 = sb("b1", [HP, 2, HB], F32)
        b2 = sb("b2", [P, 2], F32)
        xin = sb("xin", [P, 2, 1024], F32)
        xs = sb("xs", [P, 2, 1025], F32)
        xw = sb("xw", [P, 2, 2, P], F32)
        sqw = sb("sqw", [P, 1024], F32)
        ra = sb("ra", [P, 2, LHEADS, LD], F32)
        rr = sb("rr", [P, 2, LHEADS, LD], F32)
        rn = sb("rn", [P, 2 * LHEADS], F32)
        rn2 = sb("rn2", [P, 2 * LHEADS], F32)
        qp = sb("qp", [P, 2, 4, P], F32)
        kp = sb("kp", [P, 4, 2, P], F32)
        vt = sb("vt", [P, 2, 512], F32)
        sm = sb("sm", [P, 2, 2, 256], F32)
        mxw = sb("mxw", [P, 4, 2], F32)
        sumw = sb("sumw", [P, 4, 2], F32)
        ptw = sb("ptw", [P, 2, 4, P], F32)
        ot = sb("ot", [P, 4, 1024], F32)
        cn = sb("cn", [P, 2, 1024], F32)
        sqf = sb("sqf", [P, 2, 512], F32)
        rlf = sb("rlf", [P, 512], F32)
        ge = sb("ge", [HP, 2, 512], F32)
        hh = sb("hh", [HP, 2, HB, 512], F32)
        xo = sb("xo", [P, 2, 1024], F32)
        zc = xo

        const_ready = sem("const_ready")
        w_ready = sem("w_ready")
        x_ready = sem("x_ready")
        ident_ready = sem("ident_ready")
        lam_ready = sem("lam_ready")
        proj_full = sem("proj_full")
        high_done = sem("high_done")
        rest_done = sem("rest_done")
        mid_done = sem("mid_done")
        low_done = sem("low_done")
        v_done = sem("v_done")
        op_ready = [sem(f"op_ready{u}") for u in range(UNROLL)]
        max_full = sem("max_full")
        max_free = sem("max_free")
        mc_done = sem("mc_done")
        mx_done = sem("mx_done")
        nm_done = sem("nm_done")
        mrow_ready = sem("mrow_ready")
        st_full = sem("st_full")
        exp_done = sem("exp_done")
        masked = sem("masked")
        vs_ready = sem("vs_ready")
        pv_done = sem("pv_done")
        ev_done = sem("ev_done")
        ln_done = sem("ln_done")
        rb_done = sem("rb_done")
        wy_done = sem("wy_done")
        y_ready = [sem(f"y_ready{p}") for p in range(2)]
        ysum_done = sem("ysum_done")
        bn_done = sem("bn_done")
        bnag_done = sem("bnag_done")
        gl_done = sem("gl_done")
        gr_done = sem("gr_done")
        ga_done = sem("ga_done")
        gt_done = sem("gt_done")
        gb_done = sem("gb_done")
        yn_done = sem("yn_done")
        yn2_done = sem("yn2_done")
        out_full = sem("out_full")
        z_done = sem("z_done")
        mean_full = sem("mean_full")
        cen_done = sem("cen_done")
        sq_done = sem("sq_done")
        var_full = sem("var_full")
        lv_done = sem("lv_done")
        rs_done = sem("rs_done")
        norm_done = sem("norm_done")
        stored = sem("stored")

        wl_ready = sem("wl_ready")
        k2_ready = sem("k2_ready")
        tab_done = sem("tab_done")
        xin_ready = sem("xin_ready")
        xs_ready = sem("xs_ready")
        xw_ready = sem("xw_ready")
        qk_full = sem("qk_full")
        v_full = sem("v_full")
        vt_done = sem("vt_done")
        sqw_done = sem("sqw_done")
        ssq_done = sem("ssq_done")
        ssc_done = sem("ssc_done")
        lnq_done = sem("lnq_done")
        rn_done = sem("rn_done")
        ra_done = sem("ra_done")
        rr_done = sem("rr_done")
        rsum_done = sem("rsum_done")
        rot_done = sem("rot_done")
        tq_full = sem("tq_full")
        tq_read = sem("tq_read")
        s_full = sem("s_full")
        s_read = sem("s_read")
        e_done = sem("e_done")
        rc_done = sem("rc_done")
        p_ready = sem("p_ready")
        t_full = sem("t_full")
        t_read = sem("t_read")
        o_full = sem("o_full")
        o_read = sem("o_read")
        wo_full = sem("wo_full")
        xm_done = sem("xm_done")
        fm_full = sem("fm_full")
        fc_done = sem("fc_done")
        fs_done = sem("fs_done")
        fv_full = sem("fv_full")
        fl_done = sem("fl_done")
        fr_done = sem("fr_done")
        fn_done = sem("fn_done")
        hn_done = sem("hn_done")
        g_full = sem("g_full")
        a_full = sem("a_full")
        ge_done = sem("ge_done")
        hh_done = sem("hh_done")
        w2_full = sem("w2_full")
        xo_done = sem("xo_done")
        storedb = sem("storedb")
        z_ready = sem("z_ready")
        zsum_done = sem("zsum_done")
        storedc = sem("storedc")
        pe_passed = sem("pe_passed")
        dve_passed = sem("dve_passed")
        pool_passed = sem("pool_passed")

        N_W = 6
        N_L = 9
        block = ctx.enter_context(nc.Block())

        @block.sync
        def _(sp):
            sp.dma_start(wqk[:], d["wqk"]).then_inc(w_ready, 16)
            sp.dma_start(wv[:], d["wv"]).then_inc(w_ready, 16)
            sp.dma_start(lam_in[:], d["lam"]).then_inc(w_ready, 16)
            sp.dma_start(gnp[:], d["gnp"]).then_inc(w_ready, 16)
            sp.dma_start(identf[:], d["identf"]).then_inc(w_ready, 16)
            sp.dma_start(wc[:], d["wc"]).then_inc(w_ready, 16)
            with sp.Fori(0, nb) as b:
                sp.wait_ge(z_done, done(b * 4))
                sp.dma_start(xt[:], d["x"][bass.ds(b, 1)].rearrange("a c p t -> p (a c) t")).then_inc(x_ready, 16)

                def operands(h):
                    u, c, p0 = h % UNROLL, h // 8, HS * (h % 8)
                    sp.wait_ge(low_done, done(b * 16 + 8 * c + 8))
                    sp.wait_ge(st_full, done((b * 16 + h - 3) * 16))
                    for s in range(6):
                        for t, parts, n in ((qt, Q_PARTS, 0), (kt, K_PARTS, 2)):
                            sp.dma_start(t[HS * s:HS * (s + 1), u, :, :],
                                         part[p0:p0 + HS, parts[s], n:n + 2, c, :]).then_inc(op_ready[u], 16)

                def max_rows(h):
                    sp.wait_ge(max_free, done((b * 16 + h + 1) * SLOTS))
                    for a in range(2):
                        sp.dma_start(qt[KDIM + a:KDIM + a + 1, h % UNROLL, :, :].rearrange("p i (k q) -> p (i k) q", q=P),
                                     mt[16 * a:16 * a + 16, :]).then_inc(mrow_ready, 16)

                def values_out(h):
                    sp.wait_ge(wy_done, done(b * 16 + h + 1))
                    if h == 0:
                        sp.wait_ge(norm_done, done(b * 2))
                        sp.wait_ge(stored, sent(b * 2))
                    for a, t in ((0, ya), (1, yb)):
                        sp.dma_start(t[VC * (h % 4):VC * (h % 4 + 1), h // 4, :],
                                     wy[32 * a:32 * a + 32, h % 2, :]).then_inc(y_ready[h % 2], 16)

                operands(0)
                operands(1)
                max_rows(0)
                for h in range(HEADS):
                    if h + 2 < HEADS:
                        operands(h + 2)
                    if h + 1 < HEADS:
                        max_rows(h + 1)
                    if h:
                        values_out(h - 1)
                values_out(HEADS - 1)
                for half in range(2):
                    sp.wait_ge(norm_done, done(b * 2 + half + 1))
                    sp.dma_start(d["sx"][bass.ds(b, 1), :, :, half * 512:half * 512 + 512].rearrange("a c p t -> p (a c) t"),
                                 z[:, :, half * 512:half * 512 + 512]).then_inc(stored, 16)
            sp.wait_ge(stored, sent(nb * 2))

            with sp.Fori(0, LAYERS) as l:
                sp.wait_ge(storedb, sent(l * (nb * 2)))
                for t, name in ((wqkv, "wqkv"), (tabc, "tabc"), (scl, "scl"), (wo, "wo"), (w1, "w1"), (w2, "w2"),
                                (lnp, "lnp"), (b1, "b1"), (b2, "b2")):
                    src = d[name] if name == "tabc" else d[name][bass.ds(l, 1)].rearrange("a p n -> p (a n)")
                    if name != "tabc" and len(t.shape) > 2:
                        axes = "ijkm"[:len(t.shape) - 1]
                        src = src.rearrange(f"p ({' '.join(axes)}) -> p {' '.join(axes)}", **dict(zip(axes[1:], t.shape[2:])))
                    sp.dma_start(t[:], src).then_inc(wl_ready, 16)

                def load(b):
                    lb = l * nb + b
                    sp.wait_ge(xs_ready, done(lb))
                    sp.dma_start(xin[:], d["sx"][bass.ds(lb, 1)].rearrange("a c p t -> p (a c) t")).then_inc(xin_ready, 16)

                def store(b):
                    lb = l * nb + b
                    for half in range(2):
                        sp.wait_ge(xo_done, done(lb * 4 + 2 * half + 2))
                        sp.dma_start(d["sx"][bass.ds(lb + nb, 1), :, :, half * 512:half * 512 + 512].rearrange("a c p t -> p (a c) t"),
                                     xo[:, :, half * 512:half * 512 + 512]).then_inc(storedb, 16)

                load(0)
                with sp.Fori(0, nb - 1) as b:
                    load(b + 1)
                    store(b)
                store(nb - 1)
            sp.wait_ge(storedb, sent(LAYERS * nb * 2))

            with sp.Fori(0, nb) as b:
                sp.wait_ge(storedc, sent(b * 2))
                sp.dma_start(zc[:], d["sx"][bass.ds(b + LAYERS * nb, 1)].rearrange("a c p t -> p (a c) t")).then_inc(z_ready, 16)
                sp.dma_start(xin[:], d["sx"][bass.ds(b, 1)].rearrange("a c p t -> p (a c) t")).then_inc(z_ready, 16)
                for half in range(2):
                    sp.wait_ge(norm_done, done(nb * 2 + b * 2 + half + 1))
                    sp.dma_start(d["out"][bass.ds(b, 1), :, :, half * 512:half * 512 + 512].rearrange("a c p t -> p (a c) t"),
                                 zc[:, :, half * 512:half * 512 + 512]).then_inc(storedc, 16)
            sp.wait_ge(storedc, sent(nb * 2))

        @block.tensor
        def _(pe):
            pe.wait_ge(w_ready, sent(N_W))
            pe.wait_ge(const_ready, done(8))
            pe.wait_ge(ident_ready, done(1))

            def feature_norm(k, src, ready):
                for half in range(2):
                    ready(half)
                    for c in range(2):
                        mmi = pe.matmul(ps[:, 4 + half, :], mean_w[:], src[:, c, half * 512:half * 512 + 512],
                                        start=c == 0, stop=c == 1)
                    mmi.then_inc(mean_full, 1)
                for half in range(2):
                    pe.wait_ge(sq_done, done(k * 2 + half + 1))
                    for c in range(2):
                        mmi = pe.matmul(ps[:, 6 + half, :], mean_w[:], sq[:, c, :], start=c == 0, stop=c == 1)
                    mmi.then_inc(var_full, 1)

            with pe.Fori(0, nb) as b:
                h0 = pe.snap(b * HEADS)

                pe.wait_ge(x_ready, sent(b + 1))
                pe.wait_ge(norm_done, done(b * 2))
                for s in range(QKV_SLOTS):
                    k = s if s < 8 else s - 8
                    if s >= 4:
                        o = s - 4
                        if 8 <= o < 16:
                            pe.wait_ge(v_done, done(b * 8 + o - 8 + 1))
                        else:
                            pe.wait_ge(rest_done, done(b * 16 + (o if o < 8 else o - 8) + 1))
                    for kc in range(2):
                        if 8 <= s < 16:
                            blk = s - 8
                            mmi = pe.matmul(ps[:, s % 4, :], xt[:, kc, blk * P:(blk + 1) * P], wv[:, kc, :],
                                            start=kc == 0, stop=kc == 1)
                        else:
                            c, n, half = k // 8, k % 8 // 2, k % 2
                            mmi = pe.matmul(ps[:, s % 4, :], wqk[:, kc, n, c, :], xt[:, kc, half * 512:half * 512 + 512],
                                            start=kc == 0, stop=kc == 1)
                    mmi.then_inc(proj_full, 1)

                def maxima(g, slot0, u, ks):
                    for k in ks:
                        r, c0, w, _ = PIECES[k % 12]
                        i = k // 12
                        if k == 0:
                            pe.wait_ge(op_ready[u], sent((g - u) * 3 + 12))
                        pe.wait_ge(max_free, done(slot0 + k - 1))
                        pe.matmul(ps[:, 6 + (u + k) % 2, 0:w], qt[0:KDIM, u, i, r * P:(r + 1) * P],
                                  kt[0:KDIM, u, i, c0:c0 + w], start=True, stop=True).then_inc(max_full, 1)

                def max_transpose(g, slot0, u):
                    pe.wait_ge(nm_done, done(g + 1))
                    pe.wait_ge(max_free, done(slot0 + 24 - 1))
                    pe.transpose(psb[0:32, 6 + u % 2, 0:P], nm[:, :, :, :].rearrange("p a i k -> p (a i k)"),
                                 ident_b[:]).then_inc(max_full, 1)

                def scores(g, u, kb, i):
                    if kb == 0 and i == 0:
                        pe.wait_ge(mrow_ready, sent(2 * g + 2))
                    pe.wait_ge(exp_done, done(g * 16 + 2 * kb + i - 1))
                    for half, lo, hi in halves(kb):
                        mmi = pe.matmul(ps[:, 2 * i + half, lo - half * 512:hi - half * 512],
                                        kt[0:KALL, u, i, kb * P:(kb + 1) * P], qt[0:KALL, u, i, lo:hi],
                                        start=True, stop=True)
                    mmi.then_inc(st_full, 1)

                def values(g, u, kb):
                    if kb == 0:
                        pe.wait_ge(ev_done, done(g))
                        pe.wait_ge(vs_ready, done(g + 1))
                    pe.wait_ge(masked, done(g * 8 + kb + 1))
                    for half, lo, hi in halves(kb):
                        for q in range(4):
                            i = q % 2
                            w = vs[:, u % 2, kb, i, :] if q < 2 else ones[:]
                            mmi = pe.matmul(ps[32 * q:32 * q + 32, 4 + half, lo - half * 512:hi - half * 512], w,
                                            pt[:, kb % 2, i, lo:hi], start=kb == 0, stop=kb == 4 * half + 3)
                    mmi.then_inc(pv_done, 1)

                def group(g0, slots, last):
                    for u in range(UNROLL):
                        g, more = g0 + u, not (last and u == UNROLL - 1)
                        nxt, un, sn = g + 1, (u + 1) % UNROLL, slots + (u + 1) * SLOTS
                        for kb in range(8):
                            if more and kb < 4:
                                maxima(nxt, sn, un, range(6 * kb, 6 * kb + 3))
                            if more and kb == 5:
                                max_transpose(nxt, sn, un)
                            if kb < 7:
                                scores(g, u, kb + 1, 0)
                            elif more:
                                scores(nxt, un, 0, 0)
                            if more and kb < 4:
                                maxima(nxt, sn, un, range(6 * kb + 3, 6 * kb + 6))
                            if kb < 7:
                                scores(g, u, kb + 1, 1)
                            elif more:
                                scores(nxt, un, 0, 1)
                            values(g, u, kb)

                maxima(h0, h0 * SLOTS, 0, range(24))
                max_transpose(h0, h0 * SLOTS, 0)
                scores(h0, 0, 0, 0)
                scores(h0, 0, 0, 1)
                with pe.Fori(0, HEADS // UNROLL - 1) as j:
                    g0 = pe.snap(b * HEADS + j * UNROLL)
                    group(g0, pe.snap(g0 * SLOTS), False)
                g0 = pe.snap(b * HEADS + HEADS - UNROLL)
                group(g0, pe.snap(g0 * SLOTS), True)

                for n, (oc, half) in enumerate([(0, 0), (1, 0), (0, 1), (1, 1)]):
                    if n == 0:
                        pe.wait_ge(yn_done, done(b * 4 + 4))
                    for f in range(4):
                        mmi = pe.matmul(ps[:, n, :], wc[:, f, oc * P:(oc + 1) * P], ya[:, f, half * 512:half * 512 + 512],
                                        start=f == 0, stop=f == 3)
                    mmi.then_inc(out_full, 1)
                feature_norm(b, z, lambda half: pe.wait_ge(z_done, done(b * 4 + 2 * half + 2)))

            with pe.Fori(0, LAYERS) as l:
                pe.wait_ge(k2_ready, done(4))
                pe.wait_ge(wl_ready, sent((l + 1) * N_L))
                pe.sem_inc(pe_passed, 1)
                with pe.Fori(0, nb) as b:
                    lb = pe.snap(l * nb + b)

                    def project(par, n):
                        for kc in range(2):
                            mmi = pe.matmul(ps[:, n, :], xw[:, par, kc, :], wqkv[:, kc, n * 512:n * 512 + 512],
                                            start=kc == 0, stop=kc == 1)
                        return mmi

                    def queries_keys(W, par):
                        pe.wait_ge(xw_ready, done(W + 1))
                        pe.wait_ge(ra_done, done(W * 3))
                        project(par, 0)
                        project(par, 1).then_inc(qk_full, 1)

                    def values(W, par):
                        pe.wait_ge(vt_done, done(W))
                        project(par, 2).then_inc(v_full, 1)

                    def transpose_qk(W, par):
                        pe.wait_ge(rot_done, done(W + 1))
                        for hp in range(4):
                            mmi = pe.transpose(ps[:, 3, hp * P:(hp + 1) * P],
                                               rr[:, 0, 2 * hp:2 * hp + 2, :].rearrange("p h e -> p (h e)"), identf[:])
                        mmi.then_inc(tq_full, 1)
                        pe.wait_ge(t_read, done(W * 5))
                        for hp in range(4):
                            mmi = pe.transpose(ps[:, 6, hp * P:(hp + 1) * P],
                                               rr[:, 1, 2 * hp:2 * hp + 2, :].rearrange("p h e -> p (h e)"), identf[:])
                        mmi.then_inc(t_full, 1)

                    def scores(W, par, hp, first):
                        if hp == 0:
                            pe.wait_ge(tq_read, done(W + 1))
                            pe.wait_ge(t_read, done(W * 5 + 1))
                        pe.wait_ge(s_read, done(W * 4 + hp - 1))
                        n = P if first else 256
                        for q in range(2):
                            mmi = pe.matmul(ps[:, 4 + hp % 2, q * 256:q * 256 + n], qp[:, q, hp, :],
                                            kp[:, hp, :, :].rearrange("p a k -> p (a k)")[:, 0:n], start=True, stop=True)
                        mmi.then_inc(s_full, 1)

                    def transpose_p(W, par, hp, first):
                        pe.wait_ge(p_ready, done(W * 4 + hp + 1))
                        pe.wait_ge(t_read, done(W * 5 + hp + 1))
                        for q in range(2):
                            for a in range(1 if first else 2):
                                mmi = pe.transpose(ps[:, 6, (2 * q + a) * P:(2 * q + a + 1) * P],
                                                   sm[:, hp % 2, q, a * P:(a + 1) * P], identf[:])
                        mmi.then_inc(t_full, 1)

                    def weigh(W, par, hp, first):
                        if hp == 0:
                            pe.wait_ge(vt_done, done(W + 1))
                            pe.wait_ge(o_read, done(W))
                        pe.wait_ge(t_read, done(W * 5 + hp + 2))
                        for a in range(1 if first else 2):
                            for q in range(2):
                                mmi = pe.matmul(ps[64 * q:64 * q + 64, 7, hp * P:(hp + 1) * P],
                                                vt[:, a, (2 * hp + q) * LD:(2 * hp + q + 1) * LD],
                                                ptw[:, hp % 2, 2 * q + a, :], start=a == 0, stop=first or a == 1)
                        mmi.then_inc(o_full, 1)

                    def attend(W, par, first=False, last=False):
                        if not last:
                            queries_keys(W + 1, 1 - par)
                        scores(W, par, 0, first)
                        scores(W, par, 1, first)
                        if not last:
                            values(W + 1, 1 - par)
                        transpose_p(W, par, 0, first)
                        scores(W, par, 2, first)
                        weigh(W, par, 0, first)
                        transpose_p(W, par, 1, first)
                        scores(W, par, 3, first)
                        weigh(W, par, 1, first)
                        transpose_p(W, par, 2, first)
                        weigh(W, par, 2, first)
                        transpose_p(W, par, 3, first)
                        weigh(W, par, 3, first)
                        if not last:
                            transpose_qk(W + 1, 1 - par)

                    W0 = pe.snap(lb * WIN)
                    queries_keys(W0, 0)
                    values(W0, 0)
                    transpose_qk(W0, 0)
                    attend(W0, 0, first=True)
                    with pe.Fori(0, WIN // 2 - 1) as j:
                        W1 = pe.snap(W0 + j * 2 + 1)
                        attend(W1, 1)
                        attend(W1 + 1, 0)
                    attend(W0 + (WIN - 1), 1, last=True)

                    for n, (oc, half) in enumerate([(0, 0), (1, 0), (0, 1), (1, 1)]):
                        if n == 0:
                            pe.wait_ge(o_read, done(W0 + WIN))
                            pe.wait_ge(tq_read, done(W0 + WIN))
                        for f in range(4):
                            mmi = pe.matmul(ps[:, n, :], wo[:, f, oc * P:(oc + 1) * P], ot[:, f, half * 512:half * 512 + 512],
                                            start=f == 0, stop=f == 3)
                        mmi.then_inc(wo_full, 1)
                    for half in range(2):
                        pe.wait_ge(xm_done, done(lb * 4 + 2 * half + 2))
                        for kc in range(2):
                            mmi = pe.matmul(ps[:, 4 + half, :], mean_w[:],
                                            xs[:, kc, 1 - kc + half * 512:1 - kc + half * 512 + 512],
                                            start=kc == 0, stop=kc == 1)
                        mmi.then_inc(fm_full, 1)
                    for half in range(2):
                        pe.wait_ge(fs_done, done(lb * 2 + half + 1))
                        for kc in range(2):
                            mmi = pe.matmul(ps[:, 6 + half, :], mean_w[:], sqf[:, kc, :], start=kc == 0, stop=kc == 1)
                        mmi.then_inc(fv_full, 1)
                    for half in range(2):
                        pe.wait_ge(hn_done, done(lb * 4 + 2 * half + 2))
                        for j in range(HB):
                            k = half * HB + j
                            for a, (full, free) in enumerate(((a_full, hh_done), (g_full, ge_done))):
                                if k >= 2:
                                    pe.wait_ge(free, done(lb * 12 + k - 1))
                                for kc in range(2):
                                    mmi = pe.matmul(ps[0:HP, 2 * a + k % 2, :], w1[:, kc, a, j, :],
                                                    cn[:, kc, half * 512:half * 512 + 512], start=kc == 0, stop=kc == 1)
                                mmi.then_inc(full, 1)
                    for half in range(2):
                        pe.wait_ge(hh_done, done(lb * 12 + (half + 1) * HB))
                        for oc in range(2):
                            for j in range(HB):
                                mmi = pe.matmul(ps[:, 4 + 2 * half + oc, :], w2[:, j, oc * P:(oc + 1) * P], hh[:, half, j, :],
                                                start=j == 0, stop=j == HB - 1)
                            mmi.then_inc(w2_full, 1)
                    pe.wait_ge(xo_done, done(lb * 4 + 4))

            with pe.Fori(0, nb) as b:
                feature_norm(b + nb, zc, lambda half: pe.wait_ge(zsum_done, done(b + 1)))

        @block.scalar
        def _(act):
            act.wait_ge(w_ready, sent(N_W))
            act.wait_ge(const_ready, done(8))
            act.wait_ge(lam_ready, done(1))
            act.activation(lam_t[:, :, :], lam_t[:, :, :], ACT.Exp, scale=-1.0).then_inc(lam_ready, 1)

            def feature_norm(k, src):
                for half in range(2):
                    act.wait_ge(cen_done, done(k * 2 + half + 1))
                    act.wait_ge(var_full, done(k * 2 + half))
                    act.activation(sq[:, :, :], src[:, :, half * 512:half * 512 + 512], ACT.Square).then_inc(sq_done, 1)
                    act.wait_ge(var_full, done(k * 2 + half + 1))
                    act.wait_ge(norm_done, done(k * 2 + half))
                    act.activation(rl[:, :], ps[:, 6 + half, :], ACT.Ln, bias=eps_c[:, 0:1]).then_inc(lv_done, 1)
                    act.wait_ge(lv_done, done(k * 2 + half + 1))
                    act.activation(rl[:, :], rl[:, :], ACT.Exp, scale=-0.5).then_inc(rs_done, 1)

            act.preload_act_table_set("natural_log_exp_and_others")
            with act.Fori(0, nb) as b:
                h0 = act.snap(b * HEADS)

                def middle(k):
                    act.wait_ge(rest_done, done(b * 16 + k + 1))
                    c, n, half = k // 8, k % 8 // 2, k % 2
                    act.activation(part[:, 1, n, c, half * 512:half * 512 + 512], rest[:, k % 2, :],
                                   ACT.Copy).then_inc(mid_done, 1)

                for s in range(QKV_SLOTS):
                    act.wait_ge(proj_full, done(b * QKV_SLOTS + s + 1))
                    if 8 <= s < 16:
                        if s == 8:
                            middle(7)
                        act.activation(va[:, s - 8, :], ps[:, s % 4, :], ACT.Copy).then_inc(v_done, 1)
                    else:
                        k = s if s < 8 else s - 8
                        c, n, half = k // 8, k % 8 // 2, k % 2
                        act.activation(part[:, 0, n, c, half * 512:half * 512 + 512], ps[:, s % 4, :],
                                       ACT.Copy).then_inc(high_done, 1)
                        if k % 8:
                            middle(k - 1)
                middle(15)

                def exps(g, kb):
                    for i in range(2):
                        act.wait_ge(st_full, done(g * 16 + 2 * kb + i + 1))
                        if i == 0:
                            act.wait_ge(pv_done, done(g * 8 + kb - 1))
                        act.activation(pt[:, kb % 2, i, kb * P:1024],
                                       ps[:, 2 * i:2 * i + 2, :].rearrange("p a q -> p (a q)")[:, kb * P:1024],
                                       ACT.Exp, scale=SCALE).then_inc(exp_done, 1)

                def copy_out(g):
                    act.wait_ge(pv_done, done(g * 8 + 8))
                    act.wait_ge(wy_done, done(g))
                    act.activation(ev[:, :], ps[:, 4:6, :].rearrange("p a q -> p (a q)"), ACT.Copy).then_inc(ev_done, 1)

                def invert(g):
                    act.wait_ge(ev_done, done(g + 1))
                    act.activation(rb[:, :], ev[64:128, :], ACT.Ln).then_inc(ln_done, 1)
                    act.wait_ge(ln_done, done(g + 1))
                    act.activation(rb[:, :], rb[:, :], ACT.Exp, scale=-1.0).then_inc(rb_done, 1)

                def group(g0, first, last):
                    for u in range(UNROLL):
                        g = g0 + u
                        for kb in range(8):
                            exps(g, kb)
                            if not (first and u == 0):
                                if kb == 0:
                                    copy_out(g - 1)
                                if kb == 1:
                                    invert(g - 1)

                group(h0, True, False)
                with act.Fori(1, HEADS // UNROLL) as j:
                    group(act.snap(b * HEADS + j * UNROLL), False, False)
                g = act.snap(b * HEADS + HEADS - 1)
                copy_out(g)
                invert(g)

                act.wait_ge(bnag_done, done(b * 4 + 4))
                act.activation(gl[:, :], mv[:, :, 1], ACT.Ln, bias=eps_c[:, 0:1]).then_inc(gl_done, 1)
                act.wait_ge(gl_done, done(b + 1))
                act.activation(gl[:, :], gl[:, :], ACT.Exp, scale=-0.5).then_inc(gr_done, 1)
                feature_norm(b, z)

            act.preload_act_table_set("natural_log_exp_and_others")
            with act.Fori(0, LAYERS) as l:
                act.wait_ge(wl_ready, sent((l + 1) * N_L))
                act.wait_ge(k2_ready, done(4))
                with act.Fori(0, nb) as b:
                    lb = act.snap(l * nb + b)

                    def squares(W):
                        act.wait_ge(qk_full, done(W + 1))
                        act.activation(sqw[:, :], ps[:, 0:2, :].rearrange("p a q -> p (a q)"), ACT.Square).then_inc(sqw_done, 1)

                    def inverse_norms(W):
                        act.wait_ge(ssc_done, done(W + 1))
                        act.activation(rn[:, :], rn[:, :], ACT.Ln, scale=float(2 ** (2 * NORM_SHIFT))).then_inc(lnq_done, 1)
                        act.wait_ge(lnq_done, done(W + 1))
                        act.activation(rn2[:, :], rn[:, :], ACT.Exp, scale=-0.5).then_inc(rn_done, 1)

                    def values(W, par):
                        act.wait_ge(v_full, done(W + 1))
                        act.wait_ge(o_full, done(W * 4))
                        act.activation(vt[:, par, :], ps[:, 2, :], ACT.Copy).then_inc(vt_done, 1)

                    def place_qk(W, par):
                        act.wait_ge(tq_full, done(W + 1))
                        for q in range(2):
                            rows = slice(64 * q, 64 * q + 64)
                            i = act.activation(qp[rows, q, :, :], ps[rows, 3, :].rearrange("p (a k) -> p a k", a=4), ACT.Copy)
                        i.then_inc(tq_read, 1)
                        act.wait_ge(t_full, done(W * 5 + 1))
                        act.activation(kp[:, :, par, :], ps[:, 6, :].rearrange("p (a k) -> p a k", a=4), ACT.Copy).then_inc(t_read, 1)

                    def exps(W, hp, first):
                        act.wait_ge(s_read, done(W * 4 + hp + 1))
                        n = P if first else 256
                        for q in range(2):
                            i = act.activation(sm[:, hp % 2, q, 0:n], sm[:, hp % 2, q, 0:n], ACT.Exp, scale=-1.0,
                                               bias=mxw[:, hp, q:q + 1], accum_out=sumw[:, hp, q:q + 1])
                        i.then_inc(e_done, 1)

                    def place_p(W, hp, first):
                        act.wait_ge(t_full, done(W * 5 + hp + 2))
                        act.wait_ge(o_full, done(W * 4 + hp - 1))
                        n = 1 if first else 2
                        act.activation(ptw[:, hp % 2, :, :].rearrange("p (q a) k -> p q a k", q=2)[:, :, 0:n, :],
                                       ps[:, 6, :].rearrange("p (q a k) -> p q a k", q=2, a=2)[:, :, 0:n, :],
                                       ACT.Copy).then_inc(t_read, 1)

                    def attend(W, par, first=False, last=False):
                        if not last:
                            squares(W + 1)
                        exps(W, 0, first)
                        if not last:
                            inverse_norms(W + 1)
                        exps(W, 1, first)
                        place_p(W, 0, first)
                        exps(W, 2, first)
                        place_p(W, 1, first)
                        exps(W, 3, first)
                        place_p(W, 2, first)
                        place_p(W, 3, first)
                        if not last:
                            values(W + 1, 1 - par)
                            place_qk(W + 1, 1 - par)

                    W0 = act.snap(lb * WIN)
                    squares(W0)
                    inverse_norms(W0)
                    values(W0, 0)
                    place_qk(W0, 0)
                    attend(W0, 0, first=True)
                    with act.Fori(0, WIN // 2 - 1) as j:
                        W1 = act.snap(W0 + j * 2 + 1)
                        attend(W1, 1)
                        attend(W1 + 1, 0)
                    attend(W0 + (WIN - 1), 1, last=True)

                    for half in range(2):
                        act.wait_ge(fc_done, done(lb * 4 + 2 * half + 2))
                        if half:
                            act.wait_ge(fv_full, done(lb * 2 + half))
                        act.activation(sqf[:, :, :], cn[:, :, half * 512:half * 512 + 512], ACT.Square).then_inc(fs_done, 1)
                        act.wait_ge(fv_full, done(lb * 2 + half + 1))
                        if half:
                            act.wait_ge(fn_done, done(lb * 2 + half))
                        act.activation(rlf[:, :], ps[:, 6 + half, :], ACT.Ln, bias=eps_c[:, 0:1]).then_inc(fl_done, 1)
                        act.wait_ge(fl_done, done(lb * 2 + half + 1))
                        act.activation(rlf[:, :], rlf[:, :], ACT.Exp, scale=-0.5).then_inc(fr_done, 1)
                        act.wait_ge(fn_done, done(lb * 2 + half + 1))
                        for kc in range(2):
                            act.activation(cn[:, kc, half * 512:half * 512 + 512], cn[:, kc, half * 512:half * 512 + 512],
                                           ACT.Identity, scale=lnp[:, 0, kc:kc + 1], bias=lnp[:, 1, kc:kc + 1]).then_inc(hn_done, 1)
                    for k in range(2 * HB):
                        act.wait_ge(g_full, done(lb * 12 + k + 1))
                        act.wait_ge(hh_done, done(lb * 12 + k - 1))
                        act.activation(ge[:, k % 2, :], ps[0:HP, 2 + k % 2, :], ACT.Gelu, bias=b1[:, 1, k % HB:k % HB + 1]).then_inc(ge_done, 1)

            with act.Fori(0, nb) as b:
                feature_norm(b + nb, zc)

        @block.vector
        def _(dve):
            dve.memset(mc[:, :, :, :], NEG).then_inc(const_ready, 1)
            dve.memset(kt[96:128, :, :, :], -1.0).then_inc(const_ready, 1)
            dve.wait_ge(w_ready, sent(N_W))
            dve.tensor_copy(ident_b[:], identf[:]).then_inc(ident_ready, 1)
            dve.tensor_tensor(lam_t[:, :, :], lam_in[:, 0:2, :], lam_in[:, 2:4, :], ALU.mult).then_inc(lam_ready, 1)
            dve.wait_ge(lam_ready, done(2))
            dve.tensor_scalar(lam_t[:, :, :], lam_t[:, :, :], 1.0, None, ALU.add).then_inc(lam_ready, 1)
            dve.wait_ge(lam_ready, done(3))
            dve.reciprocal(lam_t[:, :, :], lam_t[:, :, :]).then_inc(lam_ready, 1)
            dve.wait_ge(lam_ready, done(4))
            dve.tensor_tensor(lam_t[:, 0, :], lam_t[:, 1, :], lam_t[:, 0, :], ALU.subtract).then_inc(lam_ready, 1)
            dve.wait_ge(lam_ready, done(5))
            dve.tensor_scalar(nlam[:, :, :], lam_t[:, 0, :].unsqueeze(2).broadcast_to([P, HEADS, VC]),
                              -LAMBDA_INIT, None, ALU.add).then_inc(lam_ready, 1)
            dve.tensor_tensor(gsc[:, :], gnp[:, 0:2], gnp[:, 2:3].broadcast_to([P, 2]), ALU.mult).then_inc(lam_ready, 1)
            dve.wait_ge(lam_ready, done(7))
            dve.tensor_scalar(gsc[:, :], gsc[:, :], 1.0 - LAMBDA_INIT, None, ALU.mult).then_inc(lam_ready, 1)
            dve.wait_ge(lam_ready, done(8))
            dve.wait_ge(const_ready, done(8))

            def feature_norm(k, src):
                for half in range(2):
                    zh = src[:, :, half * 512:half * 512 + 512]
                    dve.wait_ge(mean_full, done(k * 2 + half + 1))
                    dve.tensor_tensor(zh, zh, ps[:, 4 + half, :].unsqueeze(1).broadcast_to([P, 2, 512]),
                                      ALU.subtract).then_inc(cen_done, 1)
                for half in range(2):
                    zh = src[:, :, half * 512:half * 512 + 512]
                    dve.wait_ge(rs_done, done(k * 2 + half + 1))
                    dve.tensor_tensor(zh, zh, rl[:, :].unsqueeze(1).broadcast_to([P, 2, 512]),
                                      ALU.mult).then_inc(norm_done, 1)

            with dve.Fori(0, nb) as b:
                h0 = dve.snap(b * HEADS)
                for k in range(16):
                    s = k if k < 8 else k + 8
                    c, n, half = k // 8, k % 8 // 2, k % 2
                    dve.wait_ge(high_done, done(b * 16 + k + 1))
                    dve.wait_ge(low_done, done(b * 16 + k - 1))
                    dve.tensor_tensor(rest[:, k % 2, :], ps[:, s % 4, :], part[:, 0, n, c, half * 512:half * 512 + 512],
                                      ALU.subtract).then_inc(rest_done, 1)

                def maxima(g, slot0, u):
                    for k in range(24):
                        r, c0, w, diag = PIECES[k % 12]
                        i, bank = k // 12, 6 + (u + k) % 2
                        dve.wait_ge(max_full, done(slot0 + k + 1))
                        if k == 0:
                            dve.wait_ge(mx_done, done(g))
                        into = mc[:, i, c0 // 512, r:r + 1]
                        if diag:
                            dve.wait_ge(max_free, done(slot0 + k - 1))
                            dve.sem_inc(dve_passed, 1)
                            ins = dve.tensor_tensor_reduce(out=junk[:, bank - 6, 0:w], in0=ps[:, bank, 0:w],
                                                           in1=causal[:, 512 - w:512], scale=1.0, scalar=NEG,
                                                           op0=ALU.add, op1=ALU.max, accum_out=into)
                        else:
                            ins = dve.reduce_max(into, ps[:, bank, 0:w], AX_X)
                        ins.then_inc(max_free, 1)
                    dve.wait_ge(max_free, done(slot0 + 24))
                    dve.tensor_tensor(mm[:, :, :], mc[:, :, 0, :], mc[:, :, 1, :], ALU.max).then_inc(mx_done, 1)
                    dve.wait_ge(mx_done, done(g + 1))
                    dve.tensor_copy(nm[:, 0, :, :], mm[:, :, :]).then_inc(mc_done, 1)
                    dve.wait_ge(mc_done, done(g + 1))
                    dve.tensor_tensor(nm[:, 1, :, :], mm[:, :, :], nm[:, 0, :, :], ALU.subtract).then_inc(nm_done, 1)
                    dve.wait_ge(max_full, done(slot0 + 25))
                    dve.wait_ge(mrow_ready, sent(2 * g))
                    dve.tensor_copy(mt[:, :], psb[0:32, 6 + u % 2, 0:P]).then_inc(max_free, 1)

                def normalise(g, u):
                    dve.wait_ge(rb_done, done(g + 1))
                    dve.wait_ge(y_ready[u % 2], sent(g - u % 2))
                    dve.tensor_tensor(wy[:, u % 2, :], ev[0:64, :], rb[:, :], ALU.mult).then_inc(wy_done, 1)

                maxima(h0, dve.snap(h0 * SLOTS), 0)

                def heads(g0, slots, first, last):
                    for u in range(UNROLL):
                        if not (last and u == UNROLL - 1):
                            maxima(g0 + u + 1, slots + (u + 1) * SLOTS, (u + 1) % UNROLL)
                        if not (first and u == 0):
                            normalise(g0 + (u - 1), (u + 1) % 2)

                heads(h0, dve.snap(h0 * SLOTS), True, False)
                with dve.Fori(1, HEADS // UNROLL - 1) as j:
                    g0 = dve.snap(b * HEADS + j * UNROLL)
                    heads(g0, dve.snap(g0 * SLOTS), False, False)
                g0 = dve.snap(b * HEADS + HEADS - UNROLL)
                heads(g0, dve.snap(g0 * SLOTS), False, True)
                normalise(g0 + UNROLL - 1, 1)

                for p in range(2):
                    dve.wait_ge(y_ready[p], sent((b + 1) * HEADS))
                for j in range(4):
                    dve.tensor_tensor(ya[:, j, :], ya[:, j, :], yb[:, j, :], ALU.add).then_inc(ysum_done, 1)
                    dve.wait_ge(ysum_done, done(b * 4 + j + 1))
                    for half in range(2):
                        dve.bn_stats(bs[:, j, half, :], ya[:, j, half * 512:half * 512 + 512]).then_inc(bn_done, 1)
                    dve.wait_ge(bn_done, done(b * 8 + 2 * j + 2))
                    dve.sem_inc(dve_passed, 1)
                    dve.bn_aggr(mv[:, j, :], bs[:, j, :, :].rearrange("p a s -> p (a s)")).then_inc(bnag_done, 1)
                dve.wait_ge(gr_done, done(b + 1))
                dve.tensor_scalar(ga[:, :], gl[:, :], gsc[:, 0:1], None, ALU.mult).then_inc(ga_done, 1)
                dve.wait_ge(ga_done, done(b + 1))
                dve.tensor_tensor(gb[:, :], mv[:, :, 0], ga[:, :], ALU.mult).then_inc(gt_done, 1)
                dve.wait_ge(gt_done, done(b + 1))
                dve.tensor_scalar(gb[:, :], gb[:, :], -1.0, gsc[:, 1:2], ALU.mult, ALU.add).then_inc(gb_done, 1)
                dve.wait_ge(gb_done, done(b + 1))
                for j in range(4):
                    dve.tensor_scalar(ya[:, j, :], ya[:, j, :], ga[:, j:j + 1], gb[:, j:j + 1],
                                      ALU.mult, ALU.add).then_inc(yn_done, 1)
                for n, (oc, half) in enumerate([(0, 0), (1, 0), (0, 1), (1, 1)]):
                    dve.wait_ge(out_full, done(b * 4 + n + 1))
                    dve.tensor_tensor(z[:, oc, half * 512:half * 512 + 512], ps[:, n, :],
                                      xt[:, oc, half * 512:half * 512 + 512], ALU.add).then_inc(z_done, 1)
                feature_norm(b, z)

            with dve.Fori(0, LAYERS) as l:
                dve.wait_ge(wl_ready, sent((l + 1) * N_L))
                dve.wait_ge(k2_ready, done(4))
                dve.tensor_tensor(tab[:, :, :, :].rearrange("p w a e -> p w (a e)"), tabc[:, :, :, :].rearrange("p w a e -> p w (a e)"),
                                  scl[:, :, :].rearrange("p a e -> p (a e)").unsqueeze(1).broadcast_to([P, WIN, 4 * LD]),
                                  ALU.mult).then_inc(tab_done, 1)
                dve.wait_ge(tab_done, done(l + 1))
                dve.sem_inc(dve_passed, 1)
                with dve.Fori(0, nb) as b:
                    lb = dve.snap(l * nb + b)
                    W0 = dve.snap(lb * WIN)
                    dve.wait_ge(xin_ready, sent(lb + 1))
                    dve.tensor_copy(xs[:, :, 1:1025], xin[:, :, :]).then_inc(xs_ready, 1)

                    def norms(W):
                        dve.wait_ge(sqw_done, done(W + 1))
                        dve.reduce_sum(rn[:, :], sqw[:, :].rearrange("p (h e) -> p h e", e=LD), AX_X).then_inc(ssq_done, 1)
                        dve.wait_ge(ssq_done, done(W + 1))
                        dve.tensor_scalar(rn[:, :], rn[:, :], 1e-24, None, ALU.max).then_inc(ssc_done, 1)

                    def rotate(w, W, k):
                        src = ps[:, 0:2, :].rearrange("p a (h e) -> p a h e", e=LD)
                        t = tab[:, bass.ds(w, 1), :, :].rearrange("p w (a s) e -> p (w a) s e", s=2)
                        if k == 0:
                            dve.wait_ge(rsum_done, done(W))
                            dve.wait_ge(sqw_done, done(W + 1))
                            dve.tensor_tensor(ra[:, :, :, :], src, t[:, :, 0:1, :].broadcast_to([P, 2, LHEADS, LD]),
                                              ALU.mult).then_inc(ra_done, 1)
                        else:
                            if k == 1:
                                dve.wait_ge(tq_full, done(W))
                                dve.wait_ge(t_full, done(W * 5 - 4))
                            lo, frm = (0, 32) if k == 1 else (32, 0)
                            dve.tensor_tensor(rr[:, :, :, lo:lo + 32], src[:, :, :, frm:frm + 32],
                                              t[:, :, 1:2, lo:lo + 32].broadcast_to([P, 2, LHEADS, 32]),
                                              ALU.mult).then_inc(ra_done, 1)

                    def largest(W, par, hp, first):
                        dve.wait_ge(s_full, done(W * 4 + hp + 1))
                        dve.wait_ge(t_full, done(W * 5 + hp))
                        dve.sem_inc(dve_passed, 1)
                        n = P if first else 256
                        for q in range(2):
                            i = dve.tensor_tensor_reduce(out=sm[:, hp % 2, q, 0:n], in0=ps[:, 4 + hp % 2, q * 256:q * 256 + n],
                                                         in1=window[:, par, 0:n], scale=-1.0, scalar=-NEG,
                                                         op0=ALU.add, op1=ALU.min, accum_out=mxw[:, hp, q:q + 1])
                        i.then_inc(s_read, 1)

                    def normalise(W, hp, first):
                        dve.wait_ge(e_done, done(W * 4 + hp + 1))
                        dve.reciprocal(sumw[:, hp, :], sumw[:, hp, :]).then_inc(rc_done, 1)
                        dve.wait_ge(rc_done, done(W * 4 + hp + 1))
                        n = P if first else 256
                        for q in range(2):
                            i = dve.tensor_scalar(sm[:, hp % 2, q, 0:n], sm[:, hp % 2, q, 0:n], sumw[:, hp, q:q + 1], None, ALU.mult)
                        i.then_inc(p_ready, 1)

                    def attend(w, W, par, first=False, last=False):
                        nx = not last
                        largest(W, par, 0, first)
                        if nx:
                            norms(W + 1)
                        largest(W, par, 1, first)
                        if nx:
                            rotate(w + 1, W + 1, 0)
                        normalise(W, 0, first)
                        largest(W, par, 2, first)
                        if nx:
                            rotate(w + 1, W + 1, 1)
                        normalise(W, 1, first)
                        largest(W, par, 3, first)
                        if nx:
                            rotate(w + 1, W + 1, 2)
                        normalise(W, 2, first)
                        normalise(W, 3, first)
                        dve.wait_ge(o_full, done(W * 4 + 4))
                        dve.tensor_copy(ot[:, :, bass.ds(w * P, P)], ps[:, 7, :].rearrange("p (a q) -> p a q", a=4)).then_inc(o_read, 1)

                    norms(W0)
                    for k in range(3):
                        rotate(0, W0, k)
                    attend(0, W0, 0, first=True)
                    with dve.Fori(0, WIN // 2 - 1) as j:
                        odd = dve.snap(j * 2 + 1)
                        W1 = dve.snap(W0 + odd)
                        attend(odd, W1, 1)
                        attend(odd + 1, W1 + 1, 0)
                    attend(WIN - 1, W0 + (WIN - 1), 1, last=True)

                    for n, (oc, half) in enumerate([(0, 0), (1, 0), (0, 1), (1, 1)]):
                        dve.wait_ge(wo_full, done(lb * 4 + n + 1))
                        xh = xs[:, oc, 1 + half * 512:1 + half * 512 + 512]
                        dve.tensor_tensor(xh, ps[:, n, :], xh, ALU.add).then_inc(xm_done, 1)
                    dve.wait_ge(xm_done, done(lb * 4 + 4))
                    for half in range(2):
                        dve.wait_ge(fm_full, done(lb * 2 + half + 1))
                        for kc in range(2):
                            dve.tensor_tensor(cn[:, kc, half * 512:half * 512 + 512],
                                              xs[:, kc, 1 - kc + half * 512:1 - kc + half * 512 + 512],
                                              ps[:, 4 + half, :], ALU.subtract).then_inc(fc_done, 1)
                    for half in range(2):
                        ch = cn[:, :, half * 512:half * 512 + 512]
                        dve.wait_ge(fr_done, done(lb * 2 + half + 1))
                        dve.tensor_tensor(ch, ch, rlf[:, :].unsqueeze(1).broadcast_to([P, 2, 512]), ALU.mult).then_inc(fn_done, 1)
                    for k in range(2 * HB):
                        dve.wait_ge(a_full, done(lb * 12 + k + 1))
                        dve.wait_ge(ge_done, done(lb * 12 + k + 1))
                        dve.scalar_tensor_tensor(hh[:, k // HB, k % HB, :], ps[0:HP, k % 2, :], b1[:, 0, k % HB:k % HB + 1],
                                                 ge[:, k % 2, :], ALU.add, ALU.mult).then_inc(hh_done, 1)
                    dve.wait_ge(storedb, sent(lb * 2))
                    for half in range(2):
                        for oc in range(2):
                            dve.wait_ge(w2_full, done(lb * 4 + half * 2 + oc + 1))
                            dve.scalar_tensor_tensor(xo[:, oc, half * 512:half * 512 + 512], ps[:, 4 + 2 * half + oc, :],
                                                     b2[:, oc:oc + 1], xs[:, oc, 1 + half * 512:1 + half * 512 + 512],
                                                     ALU.add, ALU.add).then_inc(xo_done, 1)
                    dve.wait_ge(xo_done, done(lb * 4 + 4))

            with dve.Fori(0, nb) as b:
                dve.wait_ge(z_ready, sent(b * 2 + 2))
                dve.tensor_tensor(zc[:], zc[:], xin[:], ALU.add).then_inc(zsum_done, 1)
                feature_norm(b + nb, zc)

        @block.gpsimd
        def _(pool):
            for s in counters:
                pool.sem_inc(s, START)
            pool.memset(ones[:], 1.0).then_inc(const_ready, 1)
            pool.memset(mean_w[:], 1.0 / 256).then_inc(const_ready, 1)
            pool.memset(eps_c[:], EPS).then_inc(const_ready, 1)
            pool.memset(causal[:], 0.0).then_inc(const_ready, 1)
            pool.memset(junk[:], 0.0).then_inc(const_ready, 1)
            pool.wait_ge(const_ready, done(7))
            pool.affine_select(out=causal[:], in_=causal[:], compare_op=ALU.is_ge, fill=NEG, base=512 - P,
                               pattern=[[-1, 512]], channel_multiplier=1).then_inc(const_ready, 1)
            pool.wait_ge(lam_ready, done(8))
            with pool.Fori(0, nb) as b:
                h0 = pool.snap(b * HEADS)
                for k in range(16):
                    c, n, half = k // 8, k % 8 // 2, k % 2
                    pool.wait_ge(mid_done, done(b * 16 + k + 1))
                    pool.tensor_tensor(part[:, 2, n, c, half * 512:half * 512 + 512], rest[:, k % 2, :],
                                       part[:, 1, n, c, half * 512:half * 512 + 512], ALU.subtract).then_inc(low_done, 1)

                def place_values(g, h, par):
                    pool.wait_ge(pv_done, done((g - 1) * 8))
                    pool.sem_inc(pool_passed, 1)
                    pool.tensor_copy(vs[:, par, :, 0, :], va[:, :, bass.ds(h * VC, VC)])
                    pool.tensor_tensor(vs[:, par, :, 1, :], va[:, :, bass.ds(h * VC, VC)],
                                       nlam[:, bass.ds(h, 1), :].broadcast_to([P, 8, VC]), ALU.mult).then_inc(vs_ready, 1)

                pool.wait_ge(v_done, done(b * 8 + 8))
                place_values(h0, 0, 0)
                def heads(g0, hh, last):
                    for u in range(UNROLL):
                        g = g0 + u
                        for kb in range(8):
                            pool.wait_ge(exp_done, done(g * 16 + 2 * kb + 2))
                            pool.sem_inc(pool_passed, 1)
                            diag = pt[:, kb % 2, :, kb * P:(kb + 1) * P]
                            pool.affine_select(out=diag, in_=diag, compare_op=ALU.is_ge, fill=0.0, base=0,
                                               pattern=[[0, 2], [1, P]], channel_multiplier=-1).then_inc(masked, 1)
                            if kb == 2 and not (last and u == UNROLL - 1):
                                place_values(g + 1, hh + u + 1, (u + 1) % 2)

                with pool.Fori(0, HEADS // UNROLL - 1) as j:
                    heads(pool.snap(b * HEADS + j * UNROLL), pool.snap(j * UNROLL), False)
                heads(pool.snap(b * HEADS + HEADS - UNROLL), HEADS - UNROLL, True)

            pool.wait_ge(stored, sent(nb * 2))
            pool.memset(window[:], 0.0).then_inc(k2_ready, 1)
            pool.memset(qp[:], 0.0).then_inc(k2_ready, 1)
            pool.memset(xs[:, :, 0:1], 0.0).then_inc(k2_ready, 1)
            pool.wait_ge(k2_ready, done(3))
            for par in range(2):
                own, prev = window[:, par, par * P:(par + 1) * P], window[:, par, (1 - par) * P:(2 - par) * P]
                pool.affine_select(out=own, in_=own, compare_op=ALU.is_ge, fill=NEG, base=0,
                                   pattern=[[-1, P]], channel_multiplier=1)
                i = pool.affine_select(out=prev, in_=prev, compare_op=ALU.is_ge, fill=NEG, base=0,
                                       pattern=[[1, P]], channel_multiplier=-1)
            i.then_inc(k2_ready, 1)
            with pool.Fori(0, LAYERS) as l:
                with pool.Fori(0, nb) as b:
                    W0 = pool.snap((l * nb + b) * WIN)

                    def combine(W):
                        pool.wait_ge(ra_done, done(W * 3 + 3))
                        flat = lambda t: t[:, :, :, :].rearrange("p a h e -> p (a h e)")
                        pool.tensor_tensor(flat(rr), flat(ra), flat(rr), ALU.add).then_inc(rsum_done, 1)
                        pool.wait_ge(rsum_done, done(W + 1))
                        pool.wait_ge(rn_done, done(W + 1))
                        r3 = rr[:, :, :, :].rearrange("p a h e -> p (a h) e")
                        pool.tensor_tensor(r3, r3, rn2[:, :].unsqueeze(2).broadcast_to([P, 2 * LHEADS, LD]),
                                           ALU.mult).then_inc(rot_done, 1)

                    def tokens(w, W, par):
                        pool.wait_ge(v_full, done(W - 1))
                        pool.sem_inc(pool_passed, 1)
                        for kc in range(2):
                            i = pool.tensor_copy(xw[:, par, kc, :], xs[:, kc, bass.ds(w * P + (1 - kc), P)])
                        i.then_inc(xw_ready, 1)

                    pool.wait_ge(xs_ready, done(l * nb + b + 1))
                    tokens(0, W0, 0)
                    tokens(1, W0 + 1, 1)
                    with pool.Fori(0, WIN // 2 - 1) as j:
                        w = pool.snap(j * 2)
                        W = pool.snap(W0 + w)
                        for par in range(2):
                            combine(W + par)
                            tokens(w + (par + 2), W + (par + 2), par)
                    combine(W0 + (WIN - 2))
                    combine(W0 + (WIN - 1))


def rotary_tables(np):
    f = np.float32
    n = WIN * P
    half = np.arange(0, LD, 2, dtype=f)
    inv = f(1.0) / f(10000.0) ** (half / f(LD))
    t = np.arange(n, dtype=f)
    ang = t[:, None] * inv[None, :]
    base = (half + f(0.4 * LD)) / f(1.4 * LD)
    decay = base[None, :].astype(f) ** ((t - n // 2) / f(64.0))[:, None]
    cos, sin = np.cos(ang), np.sin(ang)
    up = f(2.0 ** NORM_SHIFT)
    rows = [np.concatenate([cos, cos], 1) * np.concatenate([decay, decay], 1) * f(8.0) * up,
            np.concatenate([-sin, sin], 1) * np.concatenate([decay, decay], 1) * f(8.0) * up,
            np.concatenate([cos, cos], 1) / np.concatenate([decay, decay], 1) * up,
            np.concatenate([-sin, sin], 1) / np.concatenate([decay, decay], 1) * up]
    tab = np.stack(rows, 1).astype(f)
    return tab.reshape(WIN, P, 4, LD).transpose(1, 0, 2, 3)


def layouts(inp):
    import numpy as np

    f = {k.removeprefix("L0_"): np.asarray(v) for k, v in inp.items()}
    out = {}
    nb = f["attn_x"].shape[0]
    out["x"] = f["attn_x"].transpose(0, 2, 1).reshape(nb, 2, P, 1024)
    w = np.stack([f["attn_" + n].T for n in ("Wq1", "Wq2", "Wk1", "Wk2")])
    out["wqk"] = w.reshape(4, 2, P, 2, P).transpose(2, 1, 0, 3, 4)
    out["wv"] = f["attn_Wv"].T.reshape(2, P, 512).transpose(1, 0, 2)
    out["wc"] = f["attn_Wc"].T.reshape(4, P, 256).transpose(1, 0, 2)
    out["gnp"] = np.stack([np.tile(f["attn_" + n], 4) for n in ("gn_w", "gn_b", "gamma")], 1)
    lam = np.stack([f["attn_" + n].reshape(HEADS) for n in ("lq1", "lq2", "lk1", "lk2")])
    out["lam"] = np.broadcast_to(lam, (P, 4, HEADS))
    out["identf"] = np.eye(P, dtype=np.float32)

    flat = lambda a: a.reshape(LAYERS, a.shape[1], -1)
    out["wqkv"] = flat(f["ffn_wqkv"].reshape(LAYERS, 2, P, 1536).transpose(0, 2, 1, 3))
    out["wo"] = flat(f["ffn_wo"].reshape(LAYERS, 4, P, 256).transpose(0, 2, 1, 3))
    pad = HB * HP - HID
    w1 = f["ffn_w1"].reshape(LAYERS, 2, P, 2, HID)
    w1 = np.pad(w1, [(0, 0)] * 4 + [(0, pad)])
    out["w1"] = flat(w1.reshape(LAYERS, 2, P, 2, HB, HP).transpose(0, 2, 1, 3, 4, 5))
    w2 = np.pad(f["ffn_w2"], [(0, 0), (0, pad), (0, 0)])
    out["w2"] = flat(w2.reshape(LAYERS, HB, HP, 256).transpose(0, 2, 1, 3))
    b1 = np.pad(f["ffn_b1"].reshape(LAYERS, 2, HID), [(0, 0), (0, 0), (0, pad)])
    out["b1"] = flat(b1.reshape(LAYERS, 2, HB, HP).transpose(0, 3, 1, 2))
    out["b2"] = flat(f["ffn_b2"].reshape(LAYERS, 2, P).transpose(0, 2, 1))
    ln = np.stack([f["ffn_ln_g"], f["ffn_ln_b"]], 1).reshape(LAYERS, 2, 2, P)
    out["lnp"] = flat(ln.transpose(0, 3, 1, 2))
    qs, ks = f["ffn_q_scale"], f["ffn_k_scale"]
    scl = np.stack([qs, np.roll(qs, 32, 1), ks, np.roll(ks, 32, 1)], 1)
    out["scl"] = flat(np.broadcast_to(scl[:, None], (LAYERS, P, 4, LD)))
    out["tabc"] = rotary_tables(np)
    return {k: np.ascontiguousarray(v) for k, v in out.items()}

_INS = ["x", "wqk", "wv", "wc", "gnp", "lam", "identf", "wqkv", "wo", "w1", "w2", "b1", "b2", "lnp", "scl", "tabc"]


def kernel(**inputs):
    import numpy as _np
    import concourse.bacc as _bacc
    from concourse import mybir as _mybir
    from concourse.bass_utils import run_bass_kernel_spmd as _run

    nc = _bacc.Bacc("TRN2", target_bir_lowering=False, num_devices=1)
    laid = layouts(inputs)
    nb = laid["x"].shape[0]
    arrays, d = {}, {}
    for name in _INS:
        a = laid[name]
        arrays[f"in_{name}"] = a
        d[name] = nc.dram_tensor(f"in_{name}", a.shape, _mybir.dt.from_np(a.dtype), kind="ExternalInput").ap()
    d["sx"] = nc.dram_tensor("between_phases", (nb * (LAYERS + 1), 2, P, 1024), _mybir.dt.float32, kind="Internal").ap()
    d["out"] = nc.dram_tensor("out", (nb, 2, P, 1024), _mybir.dt.float32, kind="ExternalOutput").ap()
    program(nc, d, nb)
    r = _run(nc, [arrays], core_ids=[0])
    return r.results[0]["out"].reshape(nb, 256, 1024).transpose(0, 2, 1)
```

```python
import math
from contextlib import ExitStack

import concourse.bass as bass
from concourse import mybir

F32 = mybir.dt.float32
BF16 = mybir.dt.bfloat16
ALU = mybir.AluOpType
ACT = mybir.ActivationFunctionType
AX_X = mybir.AxisListType.X

P = 128
EPS = 1e-5
NEG = -3.0e38
START = 64

HEADS = 16
HS = 16
VC = 2 * HS
LAMBDA_INIT = 0.8 - 0.6 * math.exp(-0.3 * (12 - 1))
SCALE = 1.0 / math.sqrt(HS)
Q_PARTS = (0, 0, 0, 1, 1, 2)
K_PARTS = (0, 1, 2, 0, 1, 0)
KDIM = HS * len(Q_PARTS)
KALL = KDIM + 2
UNROLL = 4


LAYERS = 2
LHEADS = 8
LD = 64
WIN = 8
HID = 682
HB = 6
HP = -(-HID // HB)
NORM_SHIFT = 10


def done(n):
    return n + START


def sent(n):
    return 16 * n + START


def max_pieces():
    out = []
    for r in range(8):
        for c0 in range(0, (r + 1) * P, 512):
            c1 = min(c0 + 512, (r + 1) * P)
            out.append((r, c0, c1 - c0, c1 == (r + 1) * P))
    return out


def halves(kb):
    out = []
    for half in range(2):
        lo, hi = max(kb * P, half * 512), (half + 1) * 512
        if lo < hi:
            out.append((half, lo, hi))
    return out


PIECES = max_pieces()
SLOTS = 2 * len(PIECES) + 1
BESIDE = (4, 4, 3, 3, 3, 2, 2, 3)
T_AT = 6
AHEAD = 2 * SLOTS - 1


def slot_of(k):
    return k + (k >= T_AT)


def bank_of(slot):
    return 6 + slot % 2


QKV_SLOTS = 24


def keys_slot(W, w):
    return W * 5 if w == 0 else W * 5 - 1


def probs_slot(W, hp, last):
    return W * 5 + hp + (2 if hp == 3 and not last else 1)


def program(nc, d, nb):
    with ExitStack() as ctx:
        top = [nc.sbuf_base]

        def sb(name, shape, dt):
            n = 2 if dt == BF16 else 4
            for x in shape[1:]:
                n *= x
            at = (top[0] + 31) // 32 * 32
            top[0] = at + n
            return nc.alloc_sbuf_tensor_at(name, shape, dt, offset=at)

        def sem(name):
            s = ctx.enter_context(nc.semaphore(name))
            counters.append(s)
            return s

        counters = []
        ps = ctx.enter_context(nc.psum_tensor("ps", [P, 8, 512], F32))
        psb = ps[:, :, :].bitcast(BF16)

        ones = sb("ones", [P, VC], F32)
        mean_w = sb("mean_w", [P, P], F32)
        eps_c = sb("eps_c", [P, 1], F32)
        sq = sb("sq", [P, 2, 512], F32)
        rl = sb("rl", [P, 512], F32)
        identf = sb("identf", [P, P], F32)
        base_ab = top[0]
        ident_b = sb("ident_b", [P, P], BF16)
        causal = sb("causal", [P, 512], F32)
        wqk = sb("wqk", [P, 2, 4, 2, P], F32)
        wv = sb("wv", [P, 2, 512], F32)
        wc = sb("wc", [P, 4, 256], F32)
        gnp = sb("gnp", [P, 3], F32)
        gsc = sb("gsc", [P, 2], F32)
        lam_in = sb("lam_in", [P, 4, HEADS], F32)
        lam_t = sb("lam_t", [P, 2, HEADS], F32)
        nlam = sb("nlam", [P, HEADS, VC], F32)
        xt = sb("xt", [P, 2, 1024], F32)
        part = sb("part", [P, 3, 4, 2, 1024], BF16)
        rest = sb("rest", [P, 2, 512], F32)
        qt = sb("qt", [P, UNROLL, 2, 1024], BF16)
        kt = sb("kt", [P, UNROLL, 2, 1024], BF16)
        va = sb("va", [P, 8, 512], F32)
        vs = sb("vs", [P, 2, 8, 2, VC], F32)
        pt = sb("pt", [P, 2, 2, 1024], F32)
        junk = sb("junk", [P, 2, 512], BF16)
        mc = sb("mc", [P, 2, 2, 8], F32)
        mm = sb("mm", [P, 2, 8], F32)
        nm = sb("nm", [P, 2, 2, 8], BF16)
        mt = sb("mt", [32, P], BF16)
        ev = sb("ev", [P, 1024], F32)
        rb = sb("rb", [64, 1024], F32)
        wy = sb("wy", [64, 2, 1024], F32)
        ya = sb("ya", [P, 4, 1024], F32)
        yb = sb("yb", [P, 4, 1024], F32)
        bs = sb("bs", [P, 4, 2, 6], F32)
        mv = sb("mv", [P, 4, 2], F32)
        gl = sb("gl", [P, 4], F32)
        ga = sb("ga", [P, 4], F32)
        gb = sb("gb", [P, 4], F32)
        z = yb[:, 0:2, :]

        top[0] = base_ab
        window = sb("window", [P, 2, 256], F32)
        wqkv = sb("wqkv", [P, 2, 1536], F32)
        wo = sb("wo", [P, 4, 256], F32)
        w1 = sb("w1", [P, 2, 2, HB, HP], F32)
        w2 = sb("w2", [HP, HB, 256], F32)
        tabc = sb("tabc", [P, WIN, 4, LD], F32)
        tab = sb("tab", [P, WIN, 4, LD], F32)
        scl = sb("scl", [P, 4, LD], F32)
        lnp = sb("lnp", [P, 2, 2], F32)
        b1 = sb("b1", [HP, 2, HB], F32)
        b2 = sb("b2", [P, 2], F32)
        xin = sb("xin", [P, 2, 1024], F32)
        xs = sb("xs", [P, 2, 1025], F32)
        xm = sb("xm", [P, 2, 1025], F32)
        xw = sb("xw", [P, 2, 2, P], F32)
        sqw = sb("sqw", [P, 1024], F32)
        ra = sb("ra", [P, 2, LHEADS, LD], F32)
        rr = sb("rr", [P, 2, LHEADS, LD], F32)
        rn = sb("rn", [P, 2 * LHEADS], F32)
        lnn = sb("lnn", [P, 2 * LHEADS], F32)
        rn2 = sb("rn2", [P, 2 * LHEADS], F32)
        nt = sb("nt", [P, 2 * LHEADS], F32)
        qp = sb("qp", [P, 2, 4, P], F32)
        kp = sb("kp", [P, 4, 2, P], F32)
        vt = sb("vt", [P, 2, 512], F32)
        sm = sb("sm", [P, 2, 2, 256], F32)
        mxw = sb("mxw", [P, 4, 2], F32)
        sumw = sb("sumw", [P, 4, 2], F32)
        ptw = sb("ptw", [P, 2, 4, P], F32)
        ot = sb("ot", [P, 4, 1024], F32)
        cn = sb("cn", [P, 2, 1024], F32)
        sqf = sb("sqf", [P, 2, 512], F32)
        rlf = sb("rlf", [P, 512], F32)
        ge = sb("ge", [HP, 2, 512], F32)
        hh = sb("hh", [HP, 2, HB, 512], F32)
        xo = sb("xo", [P, 2, 1024], F32)
        zc = xo

        const_ready = sem("const_ready")
        w_ready = sem("w_ready")
        x_ready = sem("x_ready")
        ident_ready = sem("ident_ready")
        lam_ready = sem("lam_ready")
        proj_full = sem("proj_full")
        high_done = sem("high_done")
        rest_done = sem("rest_done")
        mid_done = sem("mid_done")
        low_done = sem("low_done")
        v_done = sem("v_done")
        op_ready = [sem(f"op_ready{u}") for u in range(UNROLL)]
        max_full = sem("max_full")
        max_free = sem("max_free")
        mc_done = sem("mc_done")
        mx_done = sem("mx_done")
        nm_done = sem("nm_done")
        mrow_ready = sem("mrow_ready")
        st_full = sem("st_full")
        exp_done = sem("exp_done")
        masked = sem("masked")
        vs_ready = sem("vs_ready")
        pv_done = sem("pv_done")
        ev_done = sem("ev_done")
        ln_done = sem("ln_done")
        rb_done = sem("rb_done")
        wy_done = sem("wy_done")
        y_ready = [sem(f"y_ready{p}") for p in range(2)]
        ysum_done = sem("ysum_done")
        bn_done = sem("bn_done")
        bnag_done = sem("bnag_done")
        gl_done = sem("gl_done")
        gr_done = sem("gr_done")
        ga_done = sem("ga_done")
        gt_done = sem("gt_done")
        gb_done = sem("gb_done")
        yn_done = sem("yn_done")
        yn2_done = sem("yn2_done")
        out_full = sem("out_full")
        z_done = sem("z_done")
        mean_full = sem("mean_full")
        cen_done = sem("cen_done")
        sq_done = sem("sq_done")
        var_full = sem("var_full")
        lv_done = sem("lv_done")
        rs_done = sem("rs_done")
        norm_done = sem("norm_done")
        stored = sem("stored")

        wl_ready = sem("wl_ready")
        k2_ready = sem("k2_ready")
        tab_done = sem("tab_done")
        xin_ready = sem("xin_ready")
        xs_ready = sem("xs_ready")
        xw_ready = sem("xw_ready")
        qk_full = sem("qk_full")
        v_full = sem("v_full")
        vt_done = sem("vt_done")
        sqw_done = sem("sqw_done")
        ssq_done = sem("ssq_done")
        ssc_done = sem("ssc_done")
        lnq_done = sem("lnq_done")
        rn_done = sem("rn_done")
        nt_done = sem("nt_done")
        ra_done = sem("ra_done")
        rr_done = sem("rr_done")
        rsum_done = sem("rsum_done")
        rot_done = sem("rot_done")
        tq_full = sem("tq_full")
        tq_read = sem("tq_read")
        s_full = sem("s_full")
        s_read = sem("s_read")
        e_done = sem("e_done")
        rc_done = sem("rc_done")
        p_ready = sem("p_ready")
        t_full = sem("t_full")
        t_read = sem("t_read")
        o_full = sem("o_full")
        o_read = sem("o_read")
        wo_full = sem("wo_full")
        xm_done = sem("xm_done")
        fm_full = sem("fm_full")
        fc_done = sem("fc_done")
        fs_done = sem("fs_done")
        fv_full = sem("fv_full")
        fl_done = sem("fl_done")
        fr_done = sem("fr_done")
        fn_done = sem("fn_done")
        hn_done = sem("hn_done")
        g_full = sem("g_full")
        a_full = sem("a_full")
        ge_done = sem("ge_done")
        hh_done = sem("hh_done")
        w2_full = sem("w2_full")
        xo_done = sem("xo_done")
        storedb = sem("storedb")
        z_ready = sem("z_ready")
        zsum_done = sem("zsum_done")
        storedc = sem("storedc")
        pe_passed = sem("pe_passed")
        dve_passed = sem("dve_passed")
        pool_passed = sem("pool_passed")

        N_W = 6
        N_L = 9
        block = ctx.enter_context(nc.Block())

        @block.sync
        def _(sp):
            sp.dma_start(wqk[:], d["wqk"]).then_inc(w_ready, 16)
            sp.dma_start(wv[:], d["wv"]).then_inc(w_ready, 16)
            sp.dma_start(lam_in[:], d["lam"]).then_inc(w_ready, 16)
            sp.dma_start(gnp[:], d["gnp"]).then_inc(w_ready, 16)
            sp.dma_start(identf[:], d["identf"]).then_inc(w_ready, 16)
            sp.dma_start(wc[:], d["wc"]).then_inc(w_ready, 16)
            with sp.Fori(0, nb) as b:
                sp.wait_ge(z_done, done(b * 4))
                sp.dma_start(xt[:], d["x"][bass.ds(b, 1)].rearrange("a c p t -> p (a c) t")).then_inc(x_ready, 16)

                def operands(h):
                    u, c, p0 = h % UNROLL, h // 8, HS * (h % 8)
                    sp.wait_ge(low_done, done(b * 16 + 8 * c + 8))
                    sp.wait_ge(st_full, done((b * 16 + h - 3) * 16))
                    for s in range(6):
                        for t, parts, n in ((qt, Q_PARTS, 0), (kt, K_PARTS, 2)):
                            sp.dma_start(t[HS * s:HS * (s + 1), u, :, :],
                                         part[p0:p0 + HS, parts[s], n:n + 2, c, :]).then_inc(op_ready[u], 16)

                def max_rows(h):
                    slot = SLOTS - 1 if h == 0 else AHEAD + (h - 1) * SLOTS + (T_AT if h < HEADS - 1 else 0)
                    sp.wait_ge(max_free, done(b * HEADS * SLOTS + slot + 1))
                    for a in range(2):
                        sp.dma_start(qt[KDIM + a:KDIM + a + 1, h % UNROLL, :, :].rearrange("p i (k q) -> p (i k) q", q=P),
                                     mt[16 * a:16 * a + 16, :]).then_inc(mrow_ready, 16)

                def values_out(h):
                    sp.wait_ge(wy_done, done(b * 16 + h + 1))
                    if h == 0:
                        sp.wait_ge(norm_done, done(b * 2))
                        sp.wait_ge(stored, sent(b * 2))
                    for a, t in ((0, ya), (1, yb)):
                        sp.dma_start(t[VC * (h % 4):VC * (h % 4 + 1), h // 4, :],
                                     wy[32 * a:32 * a + 32, h % 2, :]).then_inc(y_ready[h % 2], 16)

                for h in range(3):
                    operands(h)
                max_rows(0)
                for h in range(HEADS):
                    if h + 3 < HEADS:
                        operands(h + 3)
                    if h + 1 < HEADS:
                        max_rows(h + 1)
                    if h:
                        values_out(h - 1)
                values_out(HEADS - 1)
                for half in range(2):
                    sp.wait_ge(norm_done, done(b * 2 + half + 1))
                    sp.dma_start(d["sx"][bass.ds(b, 1), :, :, half * 512:half * 512 + 512].rearrange("a c p t -> p (a c) t"),
                                 z[:, :, half * 512:half * 512 + 512]).then_inc(stored, 16)
            sp.wait_ge(stored, sent(nb * 2))

            with sp.Fori(0, LAYERS) as l:
                sp.wait_ge(storedb, sent(l * (nb * 2)))
                for t, name in ((wqkv, "wqkv"), (tabc, "tabc"), (scl, "scl"), (wo, "wo"), (w1, "w1"), (w2, "w2"),
                                (lnp, "lnp"), (b1, "b1"), (b2, "b2")):
                    src = d[name] if name == "tabc" else d[name][bass.ds(l, 1)].rearrange("a p n -> p (a n)")
                    if name != "tabc" and len(t.shape) > 2:
                        axes = "ijkm"[:len(t.shape) - 1]
                        src = src.rearrange(f"p ({' '.join(axes)}) -> p {' '.join(axes)}", **dict(zip(axes[1:], t.shape[2:])))
                    sp.dma_start(t[:], src).then_inc(wl_ready, 16)

                def load(b):
                    lb = l * nb + b
                    sp.wait_ge(xs_ready, done(lb))
                    sp.dma_start(xin[:], d["sx"][bass.ds(lb, 1)].rearrange("a c p t -> p (a c) t")).then_inc(xin_ready, 16)

                def store(b):
                    lb = l * nb + b
                    for half in range(2):
                        sp.wait_ge(xo_done, done(lb * 4 + 2 * half + 2))
                        sp.dma_start(d["sx"][bass.ds(lb + nb, 1), :, :, half * 512:half * 512 + 512].rearrange("a c p t -> p (a c) t"),
                                     xo[:, :, half * 512:half * 512 + 512]).then_inc(storedb, 16)

                load(0)
                with sp.Fori(0, nb - 1) as b:
                    load(b + 1)
                    store(b)
                store(nb - 1)
            sp.wait_ge(storedb, sent(LAYERS * nb * 2))

            with sp.Fori(0, nb) as b:
                sp.wait_ge(storedc, sent(b * 2))
                sp.dma_start(zc[:], d["sx"][bass.ds(b + LAYERS * nb, 1)].rearrange("a c p t -> p (a c) t")).then_inc(z_ready, 16)
                sp.dma_start(xin[:], d["sx"][bass.ds(b, 1)].rearrange("a c p t -> p (a c) t")).then_inc(z_ready, 16)
                for half in range(2):
                    sp.wait_ge(norm_done, done(nb * 2 + b * 2 + half + 1))
                    sp.dma_start(d["out"][bass.ds(b, 1), :, :, half * 512:half * 512 + 512].rearrange("a c p t -> p (a c) t"),
                                 zc[:, :, half * 512:half * 512 + 512]).then_inc(storedc, 16)
            sp.wait_ge(storedc, sent(nb * 2))

        @block.tensor
        def _(pe):
            pe.wait_ge(w_ready, sent(N_W))
            pe.wait_ge(const_ready, done(8))
            pe.wait_ge(ident_ready, done(1))

            def feature_norm(k, src, ready):
                for half in range(2):
                    ready(half)
                    for c in range(2):
                        mmi = pe.matmul(ps[:, 4 + half, :], mean_w[:], src[:, c, half * 512:half * 512 + 512],
                                        start=c == 0, stop=c == 1)
                    mmi.then_inc(mean_full, 1)
                for half in range(2):
                    pe.wait_ge(sq_done, done(k * 2 + half + 1))
                    for c in range(2):
                        mmi = pe.matmul(ps[:, 6 + half, :], mean_w[:], sq[:, c, :], start=c == 0, stop=c == 1)
                    mmi.then_inc(var_full, 1)

            with pe.Fori(0, nb) as b:
                h0 = pe.snap(b * HEADS)

                pe.wait_ge(x_ready, sent(b + 1))
                pe.wait_ge(norm_done, done(b * 2))
                for s in range(QKV_SLOTS):
                    k = s if s < 8 else s - 8
                    if s >= 4:
                        o = s - 4
                        if 8 <= o < 16:
                            pe.wait_ge(v_done, done(b * 8 + o - 8 + 1))
                        else:
                            pe.wait_ge(rest_done, done(b * 16 + (o if o < 8 else o - 8) + 1))
                    for kc in range(2):
                        if 8 <= s < 16:
                            blk = s - 8
                            mmi = pe.matmul(ps[:, s % 4, :], xt[:, kc, blk * P:(blk + 1) * P], wv[:, kc, :],
                                            start=kc == 0, stop=kc == 1)
                        else:
                            c, n, half = k // 8, k % 8 // 2, k % 2
                            mmi = pe.matmul(ps[:, s % 4, :], wqk[:, kc, n, c, :], xt[:, kc, half * 512:half * 512 + 512],
                                            start=kc == 0, stop=kc == 1)
                    mmi.then_inc(proj_full, 1)

                def piece(g, u, k, slot, parity):
                    r, c0, w, _ = PIECES[k % 12]
                    i = k // 12
                    if k == 0:
                        pe.wait_ge(op_ready[u], sent((g - u) * 3 + 12))
                    pe.wait_ge(max_free, done(slot - 1))
                    pe.matmul(ps[:, bank_of(parity), 0:w], qt[0:KDIM, u, i, r * P:(r + 1) * P],
                              kt[0:KDIM, u, i, c0:c0 + w], start=True, stop=True).then_inc(max_full, 1)

                def max_transpose(g, slot, parity):
                    pe.wait_ge(nm_done, done(g + 1))
                    pe.wait_ge(max_free, done(slot - 1))
                    pe.transpose(psb[0:32, bank_of(parity), 0:P], nm[:, :, :, :].rearrange("p a i k -> p (a i k)"),
                                 ident_b[:]).then_inc(max_full, 1)

                def scores(g, u, kb, i):
                    if kb == 0 and i == 0:
                        pe.wait_ge(mrow_ready, sent(2 * g + 2))
                    pe.wait_ge(exp_done, done(g * 16 + 2 * kb + i - 1))
                    for half, lo, hi in halves(kb):
                        mmi = pe.matmul(ps[:, 2 * i + half, lo - half * 512:hi - half * 512],
                                        kt[0:KALL, u, i, kb * P:(kb + 1) * P], qt[0:KALL, u, i, lo:hi],
                                        start=True, stop=True)
                    mmi.then_inc(st_full, 1)

                def values(g, u, kb, n):
                    half, lo, hi = halves(kb)[n]
                    if kb == 0:
                        pe.wait_ge(ev_done, done(g * 2 + (half - 1)))
                    if n == 0:
                        if kb == 0:
                            pe.wait_ge(vs_ready, done(g + 1))
                        pe.wait_ge(masked, done(g * 8 + kb + 1))
                    for q in range(4):
                        i = q % 2
                        w = vs[:, u % 2, kb, i, :] if q < 2 else ones[:]
                        mmi = pe.matmul(ps[32 * q:32 * q + 32, 4 + half, lo - half * 512:hi - half * 512], w,
                                        pt[:, kb % 2, i, lo:hi], start=kb == 0, stop=kb == 4 * half + 3)
                    if n == len(halves(kb)) - 1:
                        mmi.then_inc(pv_done, 1)

                def group(g0, slots, last):
                    for u in range(UNROLL):
                        g = g0 + u
                        nxt, un = g + 1, (u + 1) % UNROLL
                        one = not (last and u == UNROLL - 1)
                        two = not (last and u >= UNROLL - 2)
                        slot, parity, k = slots + u * SLOTS, 1 + u, 0
                        for kb in range(8):
                            steps = [(values, (g, u, kb, n)) for n in range(len(halves(kb)))]
                            if kb < 7:
                                steps = [(scores, (g, u, kb + 1, 0)), (scores, (g, u, kb + 1, 1))] + steps
                            elif one:
                                steps = [(scores, (nxt, un, 0, 0)), (scores, (nxt, un, 0, 1))] + steps
                            if one and not two and kb == 1:
                                max_transpose(nxt, slot, parity)
                            for n, (step, args) in enumerate(steps):
                                step(*args)
                                while two and k < sum(BESIDE[:kb]) + BESIDE[kb] * (n + 1) // len(steps):
                                    if k == T_AT:
                                        max_transpose(nxt, slot + k, parity + k)
                                    piece(g + 2, (u + 2) % UNROLL, k, slot + slot_of(k), parity + slot_of(k))
                                    k += 1

                first = pe.snap(h0 * SLOTS)
                for k in range(24):
                    piece(h0, 0, k, first + k, k)
                max_transpose(h0, first + 24, 24)
                for k in range(24):
                    piece(h0 + 1, 1, k, first + (SLOTS + k), SLOTS + k)
                scores(h0, 0, 0, 0)
                scores(h0, 0, 0, 1)
                with pe.Fori(0, HEADS // UNROLL - 1) as j:
                    g0 = pe.snap(b * HEADS + j * UNROLL)
                    group(g0, pe.snap(g0 * SLOTS + AHEAD), False)
                g0 = pe.snap(b * HEADS + HEADS - UNROLL)
                group(g0, pe.snap(g0 * SLOTS + AHEAD), True)

                for n, (oc, half) in enumerate([(0, 0), (1, 0), (0, 1), (1, 1)]):
                    if n == 0:
                        pe.wait_ge(yn_done, done(b * 4 + 4))
                    for f in range(4):
                        mmi = pe.matmul(ps[:, n, :], wc[:, f, oc * P:(oc + 1) * P], ya[:, f, half * 512:half * 512 + 512],
                                        start=f == 0, stop=f == 3)
                    mmi.then_inc(out_full, 1)
                feature_norm(b, z, lambda half: pe.wait_ge(z_done, done(b * 4 + 2 * half + 2)))

            with pe.Fori(0, LAYERS) as l:
                pe.wait_ge(k2_ready, done(5))
                pe.wait_ge(wl_ready, sent((l + 1) * N_L))
                pe.sem_inc(pe_passed, 1)
                with pe.Fori(0, nb) as b:
                    lb = pe.snap(l * nb + b)

                    def project(par, n):
                        for kc in range(2):
                            mmi = pe.matmul(ps[:, n, :], xw[:, par, kc, :], wqkv[:, kc, n * 512:n * 512 + 512],
                                            start=kc == 0, stop=kc == 1)
                        return mmi

                    def queries_keys(W, par):
                        pe.wait_ge(xw_ready, done(W + 1))
                        pe.wait_ge(ra_done, done(W * 3))
                        pe.wait_ge(sqw_done, done(W))
                        project(par, 0)
                        project(par, 1).then_inc(qk_full, 1)

                    def values(W, par):
                        pe.wait_ge(vt_done, done(W))
                        project(par, 2).then_inc(v_full, 1)

                    def transpose_qk(W, w):
                        pe.wait_ge(rot_done, done(W + 1))
                        pe.wait_ge(t_read, done(keys_slot(W, w)))
                        for hp in range(4):
                            mmi = pe.transpose(ps[:, 6, hp * P:(hp + 1) * P],
                                               rr[:, 1, 2 * hp:2 * hp + 2, :].rearrange("p h e -> p (h e)"), identf[:])
                        mmi.then_inc(t_full, 1)
                        pe.wait_ge(tq_read, done(W))
                        for hp in range(4):
                            mmi = pe.transpose(ps[:, 3, hp * P:(hp + 1) * P],
                                               rr[:, 0, 2 * hp:2 * hp + 2, :].rearrange("p h e -> p (h e)"), identf[:])
                        mmi.then_inc(tq_full, 1)

                    def scores(W, w, hp):
                        first = w == 0
                        if hp == 0:
                            pe.wait_ge(t_read, done(keys_slot(W, w) + 1))
                            pe.wait_ge(tq_read, done(W + 1))
                        pe.wait_ge(s_read, done(W * 4 + hp - 1))
                        n = P if first else 256
                        for q in range(2):
                            mmi = pe.matmul(ps[:, 4 + hp % 2, q * 256:q * 256 + n], qp[:, q, hp, :],
                                            kp[:, hp, :, :].rearrange("p a k -> p (a k)")[:, 0:n], start=True, stop=True)
                        mmi.then_inc(s_full, 1)

                    def transpose_p(W, w, hp):
                        slot = probs_slot(W, hp, w == WIN - 1)
                        pe.wait_ge(p_ready, done(W * 4 + hp + 1))
                        pe.wait_ge(t_read, done(slot))
                        for q in range(2):
                            for a in range(1 if w == 0 else 2):
                                mmi = pe.transpose(ps[:, 6, (2 * q + a) * P:(2 * q + a + 1) * P],
                                                   sm[:, hp % 2, q, a * P:(a + 1) * P], identf[:])
                        mmi.then_inc(t_full, 1)

                    def weigh(W, w, hp):
                        n = 1 if w == 0 else 2
                        if hp == 0:
                            pe.wait_ge(vt_done, done(W + 1))
                            pe.wait_ge(o_read, done(W))
                        pe.wait_ge(t_read, done(probs_slot(W, hp, w == WIN - 1) + 1))
                        for a in range(n):
                            for q in range(2):
                                mmi = pe.matmul(ps[64 * q:64 * q + 64, 7, hp * P:(hp + 1) * P],
                                                vt[:, a, (2 * hp + q) * LD:(2 * hp + q + 1) * LD],
                                                ptw[:, hp % 2, 2 * q + a, :], start=a == 0, stop=a == n - 1)
                        mmi.then_inc(o_full, 1)

                    def attend(W, w):
                        par, more = w % 2, w < WIN - 1
                        values(W, par)
                        transpose_p(W, w, 0)
                        scores(W, w, 2)
                        weigh(W, w, 0)
                        transpose_p(W, w, 1)
                        if w < WIN - 2:
                            queries_keys(W + 2, par)
                        scores(W, w, 3)
                        weigh(W, w, 1)
                        transpose_p(W, w, 2)
                        if more:
                            transpose_qk(W + 1, w + 1)
                        weigh(W, w, 2)
                        transpose_p(W, w, 3)
                        if more:
                            scores(W + 1, w + 1, 0)
                        weigh(W, w, 3)
                        if more:
                            scores(W + 1, w + 1, 1)

                    W0 = pe.snap(lb * WIN)
                    queries_keys(W0, 0)
                    queries_keys(W0 + 1, 1)
                    transpose_qk(W0, 0)
                    scores(W0, 0, 0)
                    scores(W0, 0, 1)
                    attend(W0, 0)
                    with pe.Fori(0, 2) as j:
                        W1 = pe.snap(W0 + j * 2 + 1)
                        attend(W1, 1)
                        attend(W1 + 1, 2)
                    for w in (5, 6, 7):
                        attend(W0 + w, w)

                    for n, (oc, half) in enumerate([(0, 0), (1, 0), (0, 1), (1, 1)]):
                        if n == 0:
                            pe.wait_ge(o_read, done(W0 + WIN))
                            pe.wait_ge(tq_read, done(W0 + WIN))
                        for f in range(4):
                            mmi = pe.matmul(ps[:, n, :], wo[:, f, oc * P:(oc + 1) * P], ot[:, f, half * 512:half * 512 + 512],
                                            start=f == 0, stop=f == 3)
                        mmi.then_inc(wo_full, 1)
                    for half in range(2):
                        pe.wait_ge(xm_done, done(lb * 4 + 2 * half + 2))
                        for kc in range(2):
                            mmi = pe.matmul(ps[:, 4 + half, :], mean_w[:],
                                            xm[:, kc, 1 - kc + half * 512:1 - kc + half * 512 + 512],
                                            start=kc == 0, stop=kc == 1)
                        mmi.then_inc(fm_full, 1)
                    for half in range(2):
                        pe.wait_ge(fs_done, done(lb * 2 + half + 1))
                        for kc in range(2):
                            mmi = pe.matmul(ps[:, 6 + half, :], mean_w[:], sqf[:, kc, :], start=kc == 0, stop=kc == 1)
                        mmi.then_inc(fv_full, 1)
                    for half in range(2):
                        pe.wait_ge(hn_done, done(lb * 4 + 2 * half + 2))
                        for j in range(HB):
                            k = half * HB + j
                            for a, (full, free) in enumerate(((a_full, hh_done), (g_full, ge_done))):
                                if k >= 2:
                                    pe.wait_ge(free, done(lb * 12 + k - 1))
                                for kc in range(2):
                                    mmi = pe.matmul(ps[0:HP, 2 * a + k % 2, :], w1[:, kc, a, j, :],
                                                    cn[:, kc, half * 512:half * 512 + 512], start=kc == 0, stop=kc == 1)
                                mmi.then_inc(full, 1)
                    for half in range(2):
                        pe.wait_ge(hh_done, done(lb * 12 + (half + 1) * HB))
                        for oc in range(2):
                            for j in range(HB):
                                mmi = pe.matmul(ps[:, 4 + 2 * half + oc, :], w2[:, j, oc * P:(oc + 1) * P], hh[:, half, j, :],
                                                start=j == 0, stop=j == HB - 1)
                            mmi.then_inc(w2_full, 1)
                    pe.wait_ge(xo_done, done(lb * 4 + 4))

            with pe.Fori(0, nb) as b:
                feature_norm(b + nb, zc, lambda half: pe.wait_ge(zsum_done, done(b + 1)))

        @block.scalar
        def _(act):
            act.wait_ge(w_ready, sent(N_W))
            act.wait_ge(const_ready, done(8))
            act.wait_ge(lam_ready, done(1))
            act.activation(lam_t[:, :, :], lam_t[:, :, :], ACT.Exp, scale=-1.0).then_inc(lam_ready, 1)

            def feature_norm(k, src):
                for half in range(2):
                    act.wait_ge(cen_done, done(k * 2 + half + 1))
                    act.wait_ge(var_full, done(k * 2 + half))
                    act.activation(sq[:, :, :], src[:, :, half * 512:half * 512 + 512], ACT.Square).then_inc(sq_done, 1)
                    act.wait_ge(var_full, done(k * 2 + half + 1))
                    act.wait_ge(norm_done, done(k * 2 + half))
                    act.activation(rl[:, :], ps[:, 6 + half, :], ACT.Ln, bias=eps_c[:, 0:1]).then_inc(lv_done, 1)
                    act.wait_ge(lv_done, done(k * 2 + half + 1))
                    act.activation(rl[:, :], rl[:, :], ACT.Exp, scale=-0.5).then_inc(rs_done, 1)

            act.preload_act_table_set("natural_log_exp_and_others")
            with act.Fori(0, nb) as b:
                h0 = act.snap(b * HEADS)

                def middle(k):
                    act.wait_ge(rest_done, done(b * 16 + k + 1))
                    c, n, half = k // 8, k % 8 // 2, k % 2
                    act.activation(part[:, 1, n, c, half * 512:half * 512 + 512], rest[:, k % 2, :],
                                   ACT.Copy).then_inc(mid_done, 1)

                for s in range(QKV_SLOTS):
                    act.wait_ge(proj_full, done(b * QKV_SLOTS + s + 1))
                    if 8 <= s < 16:
                        if s == 8:
                            middle(7)
                        act.activation(va[:, s - 8, :], ps[:, s % 4, :], ACT.Copy).then_inc(v_done, 1)
                    else:
                        k = s if s < 8 else s - 8
                        c, n, half = k // 8, k % 8 // 2, k % 2
                        act.activation(part[:, 0, n, c, half * 512:half * 512 + 512], ps[:, s % 4, :],
                                       ACT.Copy).then_inc(high_done, 1)
                        if k % 8:
                            middle(k - 1)
                middle(15)

                def exps(g, kb):
                    for i in range(2):
                        act.wait_ge(st_full, done(g * 16 + 2 * kb + i + 1))
                        if i == 0:
                            act.wait_ge(pv_done, done(g * 8 + kb - 1))
                        act.activation(pt[:, kb % 2, i, kb * P:1024],
                                       ps[:, 2 * i:2 * i + 2, :].rearrange("p a q -> p (a q)")[:, kb * P:1024],
                                       ACT.Exp, scale=SCALE).then_inc(exp_done, 1)

                def copy_out(g, half):
                    act.wait_ge(pv_done, done(g * 8 + 4 * half + 4))
                    if half == 0:
                        act.wait_ge(wy_done, done(g))
                    act.activation(ev[:, half * 512:half * 512 + 512], ps[:, 4 + half, :], ACT.Copy).then_inc(ev_done, 1)

                def invert(g):
                    act.wait_ge(ev_done, done(g * 2 + 2))
                    act.activation(rb[:, :], ev[64:128, :], ACT.Ln).then_inc(ln_done, 1)
                    act.wait_ge(ln_done, done(g + 1))
                    act.activation(rb[:, :], rb[:, :], ACT.Exp, scale=-1.0).then_inc(rb_done, 1)

                def group(g0, first, last):
                    for u in range(UNROLL):
                        g = g0 + u
                        for kb in range(8):
                            exps(g, kb)
                            if kb == 5:
                                copy_out(g, 0)
                            if kb == 0 and not (first and u == 0):
                                copy_out(g - 1, 1)
                            if kb == 1 and not (first and u == 0):
                                invert(g - 1)

                group(h0, True, False)
                with act.Fori(1, HEADS // UNROLL) as j:
                    group(act.snap(b * HEADS + j * UNROLL), False, False)
                g = act.snap(b * HEADS + HEADS - 1)
                copy_out(g, 1)
                invert(g)

                act.wait_ge(bnag_done, done(b * 4 + 4))
                act.activation(gl[:, :], mv[:, :, 1], ACT.Ln, bias=eps_c[:, 0:1]).then_inc(gl_done, 1)
                act.wait_ge(gl_done, done(b + 1))
                act.activation(gl[:, :], gl[:, :], ACT.Exp, scale=-0.5).then_inc(gr_done, 1)
                feature_norm(b, z)

            with act.Fori(0, LAYERS) as l:
                act.wait_ge(wl_ready, sent((l + 1) * N_L))
                act.wait_ge(k2_ready, done(5))
                with act.Fori(0, nb) as b:
                    act.preload_act_table_set("natural_log_exp_and_others")
                    lb = act.snap(l * nb + b)

                    def squares(W):
                        act.wait_ge(qk_full, done(W + 1))
                        act.activation(sqw[:, :], ps[:, 0:2, :].rearrange("p a q -> p (a q)"), ACT.Square).then_inc(sqw_done, 1)

                    def inverse_norms(W):
                        act.wait_ge(ssc_done, done(W + 1))
                        act.activation(lnn[:, :], rn[:, :], ACT.Ln).then_inc(lnq_done, 1)
                        act.wait_ge(lnq_done, done(W + 1))
                        act.wait_ge(rot_done, done(W))
                        act.activation(rn2[:, :], lnn[:, :], ACT.Exp, scale=-0.5).then_inc(rn_done, 1)

                    def values(W, par):
                        act.wait_ge(v_full, done(W + 1))
                        act.wait_ge(o_full, done(W * 4))
                        act.activation(vt[:, par, :], ps[:, 2, :], ACT.Copy).then_inc(vt_done, 1)

                    def place_qk(W, w):
                        act.wait_ge(t_full, done(keys_slot(W, w) + 1))
                        act.activation(kp[:, :, w % 2, :], ps[:, 6, :].rearrange("p (a k) -> p a k", a=4), ACT.Copy).then_inc(t_read, 1)
                        act.wait_ge(tq_full, done(W + 1))
                        for q in range(2):
                            rows = slice(64 * q, 64 * q + 64)
                            i = act.activation(qp[rows, q, :, :], ps[rows, 3, :].rearrange("p (a k) -> p a k", a=4), ACT.Copy)
                        i.then_inc(tq_read, 1)

                    def exps(W, w, hp):
                        act.wait_ge(s_read, done(W * 4 + hp + 1))
                        n = P if w == 0 else 256
                        for q in range(2):
                            i = act.activation(sm[:, hp % 2, q, 0:n], sm[:, hp % 2, q, 0:n], ACT.Exp, scale=-1.0,
                                               bias=mxw[:, hp, q:q + 1], accum_out=sumw[:, hp, q:q + 1])
                        i.then_inc(e_done, 1)

                    def place_p(W, w, hp):
                        act.wait_ge(t_full, done(probs_slot(W, hp, w == WIN - 1) + 1))
                        act.wait_ge(o_full, done(W * 4 + hp - 1))
                        n = 1 if w == 0 else 2
                        act.activation(ptw[:, hp % 2, :, :].rearrange("p (q a) k -> p q a k", q=2)[:, :, 0:n, :],
                                       ps[:, 6, :].rearrange("p (q a k) -> p q a k", q=2, a=2)[:, :, 0:n, :],
                                       ACT.Copy).then_inc(t_read, 1)

                    def attend(W, w):
                        more = w < WIN - 1
                        exps(W, w, 0)
                        exps(W, w, 1)
                        values(W, w % 2)
                        place_p(W, w, 0)
                        exps(W, w, 2)
                        place_p(W, w, 1)
                        if w < WIN - 2:
                            squares(W + 2)
                        place_p(W, w, 2)
                        exps(W, w, 3)
                        if more:
                            place_qk(W + 1, w + 1)
                        place_p(W, w, 3)
                        if w < WIN - 2:
                            inverse_norms(W + 2)

                    W0 = act.snap(lb * WIN)
                    squares(W0)
                    inverse_norms(W0)
                    squares(W0 + 1)
                    place_qk(W0, 0)
                    inverse_norms(W0 + 1)
                    attend(W0, 0)
                    with act.Fori(0, 2) as j:
                        W1 = act.snap(W0 + j * 2 + 1)
                        attend(W1, 1)
                        attend(W1 + 1, 2)
                    for w in (5, 6, 7):
                        attend(W0 + w, w)

                    for half in range(2):
                        act.wait_ge(fc_done, done(lb * 4 + 2 * half + 2))
                        if half:
                            act.wait_ge(fv_full, done(lb * 2 + half))
                        act.activation(sqf[:, :, :], cn[:, :, half * 512:half * 512 + 512], ACT.Square).then_inc(fs_done, 1)
                        act.wait_ge(fv_full, done(lb * 2 + half + 1))
                        if half:
                            act.wait_ge(fn_done, done(lb * 2 + half))
                        act.activation(rlf[:, :], ps[:, 6 + half, :], ACT.Ln, bias=eps_c[:, 0:1]).then_inc(fl_done, 1)
                        act.wait_ge(fl_done, done(lb * 2 + half + 1))
                        act.activation(rlf[:, :], rlf[:, :], ACT.Exp, scale=-0.5).then_inc(fr_done, 1)
                        act.wait_ge(fn_done, done(lb * 2 + half + 1))
                        for kc in range(2):
                            act.activation(cn[:, kc, half * 512:half * 512 + 512], cn[:, kc, half * 512:half * 512 + 512],
                                           ACT.Identity, scale=lnp[:, 0, kc:kc + 1], bias=lnp[:, 1, kc:kc + 1]).then_inc(hn_done, 1)
                    for k in range(2 * HB):
                        act.wait_ge(g_full, done(lb * 12 + k + 1))
                        act.wait_ge(hh_done, done(lb * 12 + k - 1))
                        act.activation(ge[:, k % 2, :], ps[0:HP, 2 + k % 2, :], ACT.Gelu, bias=b1[:, 1, k % HB:k % HB + 1]).then_inc(ge_done, 1)

            act.preload_act_table_set("natural_log_exp_and_others")
            with act.Fori(0, nb) as b:
                feature_norm(b + nb, zc)

        @block.vector
        def _(dve):
            dve.memset(mc[:, :, :, :], NEG).then_inc(const_ready, 1)
            dve.memset(kt[96:128, :, :, :], -1.0).then_inc(const_ready, 1)
            dve.wait_ge(w_ready, sent(N_W))
            dve.tensor_copy(ident_b[:], identf[:]).then_inc(ident_ready, 1)
            dve.tensor_tensor(lam_t[:, :, :], lam_in[:, 0:2, :], lam_in[:, 2:4, :], ALU.mult).then_inc(lam_ready, 1)
            dve.wait_ge(lam_ready, done(2))
            dve.tensor_scalar(lam_t[:, :, :], lam_t[:, :, :], 1.0, None, ALU.add).then_inc(lam_ready, 1)
            dve.wait_ge(lam_ready, done(3))
            dve.reciprocal(lam_t[:, :, :], lam_t[:, :, :]).then_inc(lam_ready, 1)
            dve.wait_ge(lam_ready, done(4))
            dve.tensor_tensor(lam_t[:, 0, :], lam_t[:, 1, :], lam_t[:, 0, :], ALU.subtract).then_inc(lam_ready, 1)
            dve.wait_ge(lam_ready, done(5))
            dve.tensor_scalar(nlam[:, :, :], lam_t[:, 0, :].unsqueeze(2).broadcast_to([P, HEADS, VC]),
                              -LAMBDA_INIT, None, ALU.add).then_inc(lam_ready, 1)
            dve.tensor_tensor(gsc[:, :], gnp[:, 0:2], gnp[:, 2:3].broadcast_to([P, 2]), ALU.mult).then_inc(lam_ready, 1)
            dve.wait_ge(lam_ready, done(7))
            dve.tensor_scalar(gsc[:, :], gsc[:, :], 1.0 - LAMBDA_INIT, None, ALU.mult).then_inc(lam_ready, 1)
            dve.wait_ge(lam_ready, done(8))
            dve.wait_ge(const_ready, done(8))

            def feature_norm(k, src):
                for half in range(2):
                    zh = src[:, :, half * 512:half * 512 + 512]
                    dve.wait_ge(mean_full, done(k * 2 + half + 1))
                    dve.tensor_tensor(zh, zh, ps[:, 4 + half, :].unsqueeze(1).broadcast_to([P, 2, 512]),
                                      ALU.subtract).then_inc(cen_done, 1)
                for half in range(2):
                    zh = src[:, :, half * 512:half * 512 + 512]
                    dve.wait_ge(rs_done, done(k * 2 + half + 1))
                    dve.tensor_tensor(zh, zh, rl[:, :].unsqueeze(1).broadcast_to([P, 2, 512]),
                                      ALU.mult).then_inc(norm_done, 1)

            with dve.Fori(0, nb) as b:
                h0 = dve.snap(b * HEADS)
                for k in range(16):
                    s = k if k < 8 else k + 8
                    c, n, half = k // 8, k % 8 // 2, k % 2
                    dve.wait_ge(high_done, done(b * 16 + k + 1))
                    dve.wait_ge(low_done, done(b * 16 + k - 1))
                    dve.tensor_tensor(rest[:, k % 2, :], ps[:, s % 4, :], part[:, 0, n, c, half * 512:half * 512 + 512],
                                      ALU.subtract).then_inc(rest_done, 1)

                def piece(g, k, slot, parity):
                    r, c0, w, diag = PIECES[k % 12]
                    i, bank = k // 12, bank_of(parity)
                    dve.wait_ge(max_full, done(slot + 1))
                    if k == 0:
                        dve.wait_ge(mx_done, done(g))
                    into = mc[:, i, c0 // 512, r:r + 1]
                    if diag:
                        dve.wait_ge(max_free, done(slot - 1))
                        dve.sem_inc(dve_passed, 1)
                        ins = dve.tensor_tensor_reduce(out=junk[:, bank - 6, 0:w], in0=ps[:, bank, 0:w],
                                                       in1=causal[:, 512 - w:512], scale=1.0, scalar=NEG,
                                                       op0=ALU.add, op1=ALU.max, accum_out=into)
                    else:
                        ins = dve.reduce_max(into, ps[:, bank, 0:w], AX_X)
                    ins.then_inc(max_free, 1)

                def two_parts(g, slot):
                    dve.wait_ge(max_free, done(slot + 1))
                    dve.tensor_tensor(mm[:, :, :], mc[:, :, 0, :], mc[:, :, 1, :], ALU.max).then_inc(mx_done, 1)
                    dve.wait_ge(mx_done, done(g + 1))
                    dve.tensor_copy(nm[:, 0, :, :], mm[:, :, :]).then_inc(mc_done, 1)
                    dve.wait_ge(mc_done, done(g + 1))
                    dve.tensor_tensor(nm[:, 1, :, :], mm[:, :, :], nm[:, 0, :, :], ALU.subtract).then_inc(nm_done, 1)

                def copy_maxima(g, slot, parity):
                    dve.wait_ge(max_full, done(slot + 1))
                    dve.wait_ge(mrow_ready, sent(2 * g))
                    dve.tensor_copy(mt[:, :], psb[0:32, bank_of(parity), 0:P]).then_inc(max_free, 1)

                def normalise(g, u):
                    dve.wait_ge(rb_done, done(g + 1))
                    dve.wait_ge(y_ready[u % 2], sent(g - u % 2))
                    dve.tensor_tensor(wy[:, u % 2, :], ev[0:64, :], rb[:, :], ALU.mult).then_inc(wy_done, 1)

                first = dve.snap(h0 * SLOTS)
                for k in range(24):
                    piece(h0, k, first + k, k)
                two_parts(h0, first + 23)
                copy_maxima(h0, first + 24, 24)
                for k in range(24):
                    piece(h0 + 1, k, first + (SLOTS + k), SLOTS + k)
                two_parts(h0 + 1, first + (SLOTS + 23))

                def heads(g0, slots, first, last):
                    for u in range(UNROLL):
                        g = g0 + u
                        slot, parity = slots + u * SLOTS, 1 + u
                        if not (last and u >= UNROLL - 2):
                            for k in range(24):
                                if k == T_AT:
                                    copy_maxima(g + 1, slot + k, parity + k)
                                if k == T_AT + 4 and not (first and u == 0):
                                    normalise(g - 1, (u + 1) % 2)
                                piece(g + 2, k, slot + slot_of(k), parity + slot_of(k))
                            two_parts(g + 2, slot + 24)
                        else:
                            if u == UNROLL - 2:
                                copy_maxima(g + 1, slot, parity)
                            normalise(g - 1, (u + 1) % 2)

                heads(h0, dve.snap(h0 * SLOTS + AHEAD), True, False)
                with dve.Fori(1, HEADS // UNROLL - 1) as j:
                    g0 = dve.snap(b * HEADS + j * UNROLL)
                    heads(g0, dve.snap(g0 * SLOTS + AHEAD), False, False)
                g0 = dve.snap(b * HEADS + HEADS - UNROLL)
                heads(g0, dve.snap(g0 * SLOTS + AHEAD), False, True)
                normalise(g0 + UNROLL - 1, 1)

                for p in range(2):
                    dve.wait_ge(y_ready[p], sent((b + 1) * HEADS))
                for j in range(4):
                    dve.tensor_tensor(ya[:, j, :], ya[:, j, :], yb[:, j, :], ALU.add).then_inc(ysum_done, 1)
                    dve.wait_ge(ysum_done, done(b * 4 + j + 1))
                    for half in range(2):
                        dve.bn_stats(bs[:, j, half, :], ya[:, j, half * 512:half * 512 + 512]).then_inc(bn_done, 1)
                    dve.wait_ge(bn_done, done(b * 8 + 2 * j + 2))
                    dve.sem_inc(dve_passed, 1)
                    dve.bn_aggr(mv[:, j, :], bs[:, j, :, :].rearrange("p a s -> p (a s)")).then_inc(bnag_done, 1)
                dve.wait_ge(gr_done, done(b + 1))
                dve.tensor_scalar(ga[:, :], gl[:, :], gsc[:, 0:1], None, ALU.mult).then_inc(ga_done, 1)
                dve.wait_ge(ga_done, done(b + 1))
                dve.tensor_tensor(gb[:, :], mv[:, :, 0], ga[:, :], ALU.mult).then_inc(gt_done, 1)
                dve.wait_ge(gt_done, done(b + 1))
                dve.tensor_scalar(gb[:, :], gb[:, :], -1.0, gsc[:, 1:2], ALU.mult, ALU.add).then_inc(gb_done, 1)
                dve.wait_ge(gb_done, done(b + 1))
                for j in range(4):
                    dve.tensor_scalar(ya[:, j, :], ya[:, j, :], ga[:, j:j + 1], gb[:, j:j + 1],
                                      ALU.mult, ALU.add).then_inc(yn_done, 1)
                for n, (oc, half) in enumerate([(0, 0), (1, 0), (0, 1), (1, 1)]):
                    dve.wait_ge(out_full, done(b * 4 + n + 1))
                    dve.tensor_tensor(z[:, oc, half * 512:half * 512 + 512], ps[:, n, :],
                                      xt[:, oc, half * 512:half * 512 + 512], ALU.add).then_inc(z_done, 1)
                feature_norm(b, z)

            with dve.Fori(0, LAYERS) as l:
                dve.wait_ge(wl_ready, sent((l + 1) * N_L))
                dve.wait_ge(k2_ready, done(5))
                dve.tensor_tensor(tab[:, :, :, :].rearrange("p w a e -> p w (a e)"), tabc[:, :, :, :].rearrange("p w a e -> p w (a e)"),
                                  scl[:, :, :].rearrange("p a e -> p (a e)").unsqueeze(1).broadcast_to([P, WIN, 4 * LD]),
                                  ALU.mult).then_inc(tab_done, 1)
                dve.wait_ge(tab_done, done(l + 1))
                dve.sem_inc(dve_passed, 1)
                with dve.Fori(0, nb) as b:
                    lb = dve.snap(l * nb + b)
                    W0 = dve.snap(lb * WIN)

                    def norms(W):
                        dve.wait_ge(sqw_done, done(W + 1))
                        dve.wait_ge(rot_done, done(W))
                        dve.reduce_sum(rn[:, :], sqw[:, :].rearrange("p (h e) -> p h e", e=LD), AX_X).then_inc(ssq_done, 1)
                        dve.wait_ge(ssq_done, done(W + 1))
                        dve.tensor_scalar(rn[:, :], rn[:, :], 1e-24, float(2 ** (2 * NORM_SHIFT)),
                                          ALU.max, ALU.mult).then_inc(ssc_done, 1)

                    def rotate(w, W, k):
                        src = ps[:, 0:2, :].rearrange("p a (h e) -> p a h e", e=LD)
                        t = tab[:, bass.ds(w, 1), :, :].rearrange("p w (a s) e -> p (w a) s e", s=2)
                        if k == 0:
                            dve.wait_ge(rsum_done, done(W))
                            dve.wait_ge(sqw_done, done(W + 1))
                            dve.tensor_tensor(ra[:, :, :, :], src, t[:, :, 0:1, :].broadcast_to([P, 2, LHEADS, LD]),
                                              ALU.mult).then_inc(ra_done, 1)
                        else:
                            if k == 1:
                                dve.wait_ge(tq_full, done(W))
                            lo, frm = (0, 32) if k == 1 else (32, 0)
                            dve.tensor_tensor(rr[:, :, :, lo:lo + 32], src[:, :, :, frm:frm + 32],
                                              t[:, :, 1:2, lo:lo + 32].broadcast_to([P, 2, LHEADS, 32]),
                                              ALU.mult).then_inc(ra_done, 1)

                    def largest(W, w, hp):
                        dve.wait_ge(s_full, done(W * 4 + hp + 1))
                        dve.wait_ge(t_full, done(W * 5 + (-1, 1, 2, 3)[hp]))
                        dve.sem_inc(dve_passed, 1)
                        n = P if w == 0 else 256
                        for q in range(2):
                            i = dve.tensor_tensor_reduce(out=sm[:, hp % 2, q, 0:n], in0=ps[:, 4 + hp % 2, q * 256:q * 256 + n],
                                                         in1=window[:, w % 2, 0:n], scale=-1.0, scalar=-NEG,
                                                         op0=ALU.add, op1=ALU.min, accum_out=mxw[:, hp, q:q + 1])
                        i.then_inc(s_read, 1)

                    def normalise(W, w, hp):
                        dve.wait_ge(e_done, done(W * 4 + hp + 1))
                        dve.reciprocal(sumw[:, hp, :], sumw[:, hp, :]).then_inc(rc_done, 1)
                        dve.wait_ge(rc_done, done(W * 4 + hp + 1))
                        n = P if w == 0 else 256
                        for q in range(2):
                            i = dve.tensor_scalar(sm[:, hp % 2, q, 0:n], sm[:, hp % 2, q, 0:n], sumw[:, hp, q:q + 1], None, ALU.mult)
                        i.then_inc(p_ready, 1)

                    def attend(W, w, at):
                        largest(W, w, 1)
                        normalise(W, w, 0)
                        normalise(W, w, 1)
                        largest(W, w, 2)
                        normalise(W, w, 2)
                        largest(W, w, 3)
                        if w < WIN - 2:
                            norms(W + 2)
                        normalise(W, w, 3)
                        if w < WIN - 2:
                            for k in range(3):
                                rotate(at + 2, W + 2, k)
                        if w < WIN - 1:
                            largest(W + 1, w + 1, 0)
                        dve.wait_ge(o_full, done(W * 4 + 4))
                        dve.tensor_copy(ot[:, :, bass.ds(at * P, P)], ps[:, 7, :].rearrange("p (a q) -> p a q", a=4)).then_inc(o_read, 1)

                    for k in range(3):
                        rotate(0, W0, k)
                    norms(W0)
                    rotate(1, W0 + 1, 0)
                    norms(W0 + 1)
                    rotate(1, W0 + 1, 1)
                    rotate(1, W0 + 1, 2)
                    largest(W0, 0, 0)
                    attend(W0, 0, 0)
                    with dve.Fori(0, 2) as j:
                        odd = dve.snap(j * 2 + 1)
                        W1 = dve.snap(W0 + odd)
                        attend(W1, 1, odd)
                        attend(W1 + 1, 2, odd + 1)
                    for w in (5, 6, 7):
                        attend(W0 + w, w, w)

                    for n, (oc, half) in enumerate([(0, 0), (1, 0), (0, 1), (1, 1)]):
                        dve.wait_ge(wo_full, done(lb * 4 + n + 1))
                        xh = xs[:, oc, 1 + half * 512:1 + half * 512 + 512]
                        dve.tensor_tensor(xm[:, oc, 1 + half * 512:1 + half * 512 + 512], ps[:, n, :], xh, ALU.add).then_inc(xm_done, 1)
                    dve.wait_ge(xm_done, done(lb * 4 + 4))
                    for half in range(2):
                        dve.wait_ge(fm_full, done(lb * 2 + half + 1))
                        for kc in range(2):
                            dve.tensor_tensor(cn[:, kc, half * 512:half * 512 + 512],
                                              xm[:, kc, 1 - kc + half * 512:1 - kc + half * 512 + 512],
                                              ps[:, 4 + half, :], ALU.subtract).then_inc(fc_done, 1)
                    for half in range(2):
                        ch = cn[:, :, half * 512:half * 512 + 512]
                        dve.wait_ge(fr_done, done(lb * 2 + half + 1))
                        dve.tensor_tensor(ch, ch, rlf[:, :].unsqueeze(1).broadcast_to([P, 2, 512]), ALU.mult).then_inc(fn_done, 1)
                    for k in range(2 * HB):
                        dve.wait_ge(a_full, done(lb * 12 + k + 1))
                        dve.wait_ge(ge_done, done(lb * 12 + k + 1))
                        dve.scalar_tensor_tensor(hh[:, k // HB, k % HB, :], ps[0:HP, k % 2, :], b1[:, 0, k % HB:k % HB + 1],
                                                 ge[:, k % 2, :], ALU.add, ALU.mult).then_inc(hh_done, 1)
                    dve.wait_ge(storedb, sent(lb * 2))
                    for half in range(2):
                        for oc in range(2):
                            dve.wait_ge(w2_full, done(lb * 4 + half * 2 + oc + 1))
                            dve.scalar_tensor_tensor(xo[:, oc, half * 512:half * 512 + 512], ps[:, 4 + 2 * half + oc, :],
                                                     b2[:, oc:oc + 1], xm[:, oc, 1 + half * 512:1 + half * 512 + 512],
                                                     ALU.add, ALU.add).then_inc(xo_done, 1)
                    dve.wait_ge(xo_done, done(lb * 4 + 4))

            with dve.Fori(0, nb) as b:
                dve.wait_ge(z_ready, sent(b * 2 + 2))
                dve.tensor_tensor(zc[:], zc[:], xin[:], ALU.add).then_inc(zsum_done, 1)
                feature_norm(b + nb, zc)

        @block.gpsimd
        def _(pool):
            for s in counters:
                pool.sem_inc(s, START)
            pool.memset(ones[:], 1.0).then_inc(const_ready, 1)
            pool.memset(mean_w[:], 1.0 / 256).then_inc(const_ready, 1)
            pool.memset(eps_c[:], EPS).then_inc(const_ready, 1)
            pool.memset(causal[:], 0.0).then_inc(const_ready, 1)
            pool.memset(junk[:], 0.0).then_inc(const_ready, 1)
            pool.wait_ge(const_ready, done(7))
            pool.affine_select(out=causal[:], in_=causal[:], compare_op=ALU.is_ge, fill=NEG, base=512 - P,
                               pattern=[[-1, 512]], channel_multiplier=1).then_inc(const_ready, 1)
            pool.wait_ge(lam_ready, done(8))
            with pool.Fori(0, nb) as b:
                h0 = pool.snap(b * HEADS)
                for k in range(16):
                    c, n, half = k // 8, k % 8 // 2, k % 2
                    pool.wait_ge(mid_done, done(b * 16 + k + 1))
                    pool.tensor_tensor(part[:, 2, n, c, half * 512:half * 512 + 512], rest[:, k % 2, :],
                                       part[:, 1, n, c, half * 512:half * 512 + 512], ALU.subtract).then_inc(low_done, 1)

                def place_values(g, h, par, i):
                    v = va[:, :, bass.ds(h * VC, VC)]
                    if i == 0:
                        pool.wait_ge(pv_done, done((g - 1) * 8))
                        pool.sem_inc(pool_passed, 1)
                        pool.tensor_copy(vs[:, par, :, 0, :], v)
                    else:
                        pool.tensor_tensor(vs[:, par, :, 1, :], v, nlam[:, bass.ds(h, 1), :].broadcast_to([P, 8, VC]),
                                           ALU.mult).then_inc(vs_ready, 1)

                pool.wait_ge(v_done, done(b * 8 + 8))
                place_values(h0, 0, 0, 0)
                place_values(h0, 0, 0, 1)

                def heads(g0, hh, last):
                    for u in range(UNROLL):
                        g = g0 + u
                        for kb in range(8):
                            pool.wait_ge(exp_done, done(g * 16 + 2 * kb + 2))
                            pool.sem_inc(pool_passed, 1)
                            diag = pt[:, kb % 2, :, kb * P:(kb + 1) * P]
                            pool.affine_select(out=diag, in_=diag, compare_op=ALU.is_ge, fill=0.0, base=0,
                                               pattern=[[0, 2], [1, P]], channel_multiplier=-1).then_inc(masked, 1)
                            if kb < 2 and not (last and u == UNROLL - 1):
                                place_values(g + 1, hh + u + 1, (u + 1) % 2, kb)

                with pool.Fori(0, HEADS // UNROLL - 1) as j:
                    heads(pool.snap(b * HEADS + j * UNROLL), pool.snap(j * UNROLL), False)
                heads(pool.snap(b * HEADS + HEADS - UNROLL), HEADS - UNROLL, True)

            pool.wait_ge(stored, sent(nb * 2))
            pool.memset(window[:], 0.0).then_inc(k2_ready, 1)
            pool.memset(qp[:], 0.0).then_inc(k2_ready, 1)
            pool.memset(xs[:, :, 0:1], 0.0).then_inc(k2_ready, 1)
            pool.memset(xm[:, :, 0:1], 0.0).then_inc(k2_ready, 1)
            pool.wait_ge(k2_ready, done(4))
            for par in range(2):
                own, prev = window[:, par, par * P:(par + 1) * P], window[:, par, (1 - par) * P:(2 - par) * P]
                pool.affine_select(out=own, in_=own, compare_op=ALU.is_ge, fill=NEG, base=0,
                                   pattern=[[-1, P]], channel_multiplier=1)
                i = pool.affine_select(out=prev, in_=prev, compare_op=ALU.is_ge, fill=NEG, base=0,
                                       pattern=[[1, P]], channel_multiplier=-1)
            i.then_inc(k2_ready, 1)
            with pool.Fori(0, LAYERS) as l:
                with pool.Fori(0, nb) as b:
                    W0 = pool.snap((l * nb + b) * WIN)

                    def combine(W):
                        pool.wait_ge(ra_done, done(W * 3 + 3))
                        flat = lambda t: t[:, :, :, :].rearrange("p a h e -> p (a h e)")
                        pool.tensor_tensor(flat(rr), flat(ra), flat(rr), ALU.add).then_inc(rsum_done, 1)
                        pool.wait_ge(rn_done, done(W + 1))
                        pool.tensor_tensor(nt[:, :], rn2[:, :], rn2[:, :], ALU.mult).then_inc(nt_done, 1)
                        pool.wait_ge(nt_done, done(W * 4 + 1))
                        pool.tensor_tensor(nt[:, :], nt[:, :], rn[:, :], ALU.mult).then_inc(nt_done, 1)
                        pool.wait_ge(nt_done, done(W * 4 + 2))
                        pool.sem_inc(pool_passed, 1)
                        pool.tensor_scalar(nt[:, :], nt[:, :], -0.5, 1.5, ALU.mult, ALU.add).then_inc(nt_done, 1)
                        pool.wait_ge(nt_done, done(W * 4 + 3))
                        pool.tensor_tensor(nt[:, :], nt[:, :], rn2[:, :], ALU.mult).then_inc(nt_done, 1)
                        pool.wait_ge(nt_done, done(W * 4 + 4))
                        pool.wait_ge(rsum_done, done(W + 1))
                        r3 = rr[:, :, :, :].rearrange("p a h e -> p (a h) e")
                        pool.tensor_tensor(r3, r3, nt[:, :].unsqueeze(2).broadcast_to([P, 2 * LHEADS, LD]),
                                           ALU.mult).then_inc(rot_done, 1)

                    def tokens(w, W, par):
                        pool.wait_ge(v_full, done(W - 1))
                        pool.sem_inc(pool_passed, 1)
                        for kc in range(2):
                            i = pool.tensor_copy(xw[:, par, kc, :], xs[:, kc, bass.ds(w * P + (1 - kc), P)])
                        i.then_inc(xw_ready, 1)

                    pool.wait_ge(xin_ready, sent(l * nb + b + 1))
                    pool.wait_ge(xm_done, done((l * nb + b) * 4))
                    pool.sem_inc(pool_passed, 1)
                    pool.tensor_copy(xs[:, :, 1:1025], xin[:, :, :]).then_inc(xs_ready, 1)
                    pool.wait_ge(xs_ready, done(l * nb + b + 1))
                    tokens(0, W0, 0)
                    tokens(1, W0 + 1, 1)
                    combine(W0)
                    with pool.Fori(0, WIN // 2 - 1) as j:
                        w = pool.snap(j * 2)
                        W = pool.snap(W0 + w)
                        for par in range(2):
                            combine(W + (par + 1))
                            tokens(w + (par + 2), W + (par + 2), par)
                    combine(W0 + (WIN - 1))


def rotary_tables(np):
    f = np.float32
    n = WIN * P
    half = np.arange(0, LD, 2, dtype=f)
    inv = f(1.0) / f(10000.0) ** (half / f(LD))
    t = np.arange(n, dtype=f)
    ang = t[:, None] * inv[None, :]
    base = (half + f(0.4 * LD)) / f(1.4 * LD)
    decay = base[None, :].astype(f) ** ((t - n // 2) / f(64.0))[:, None]
    cos, sin = np.cos(ang), np.sin(ang)
    up = f(2.0 ** NORM_SHIFT)
    rows = [np.concatenate([cos, cos], 1) * np.concatenate([decay, decay], 1) * f(8.0) * up,
            np.concatenate([-sin, sin], 1) * np.concatenate([decay, decay], 1) * f(8.0) * up,
            np.concatenate([cos, cos], 1) / np.concatenate([decay, decay], 1) * up,
            np.concatenate([-sin, sin], 1) / np.concatenate([decay, decay], 1) * up]
    tab = np.stack(rows, 1).astype(f)
    return tab.reshape(WIN, P, 4, LD).transpose(1, 0, 2, 3)


def layouts(inp):
    import numpy as np

    f = {k.removeprefix("L0_"): np.asarray(v) for k, v in inp.items()}
    out = {}
    nb = f["attn_x"].shape[0]
    out["x"] = f["attn_x"].transpose(0, 2, 1).reshape(nb, 2, P, 1024)
    w = np.stack([f["attn_" + n].T for n in ("Wq1", "Wq2", "Wk1", "Wk2")])
    out["wqk"] = w.reshape(4, 2, P, 2, P).transpose(2, 1, 0, 3, 4)
    out["wv"] = f["attn_Wv"].T.reshape(2, P, 512).transpose(1, 0, 2)
    out["wc"] = f["attn_Wc"].T.reshape(4, P, 256).transpose(1, 0, 2)
    out["gnp"] = np.stack([np.tile(f["attn_" + n], 4) for n in ("gn_w", "gn_b", "gamma")], 1)
    lam = np.stack([f["attn_" + n].reshape(HEADS) for n in ("lq1", "lq2", "lk1", "lk2")])
    out["lam"] = np.broadcast_to(lam, (P, 4, HEADS))
    out["identf"] = np.eye(P, dtype=np.float32)

    flat = lambda a: a.reshape(LAYERS, a.shape[1], -1)
    out["wqkv"] = flat(f["ffn_wqkv"].reshape(LAYERS, 2, P, 1536).transpose(0, 2, 1, 3))
    out["wo"] = flat(f["ffn_wo"].reshape(LAYERS, 4, P, 256).transpose(0, 2, 1, 3))
    pad = HB * HP - HID
    w1 = f["ffn_w1"].reshape(LAYERS, 2, P, 2, HID)
    w1 = np.pad(w1, [(0, 0)] * 4 + [(0, pad)])
    out["w1"] = flat(w1.reshape(LAYERS, 2, P, 2, HB, HP).transpose(0, 2, 1, 3, 4, 5))
    w2 = np.pad(f["ffn_w2"], [(0, 0), (0, pad), (0, 0)])
    out["w2"] = flat(w2.reshape(LAYERS, HB, HP, 256).transpose(0, 2, 1, 3))
    b1 = np.pad(f["ffn_b1"].reshape(LAYERS, 2, HID), [(0, 0), (0, 0), (0, pad)])
    out["b1"] = flat(b1.reshape(LAYERS, 2, HB, HP).transpose(0, 3, 1, 2))
    out["b2"] = flat(f["ffn_b2"].reshape(LAYERS, 2, P).transpose(0, 2, 1))
    ln = np.stack([f["ffn_ln_g"], f["ffn_ln_b"]], 1).reshape(LAYERS, 2, 2, P)
    out["lnp"] = flat(ln.transpose(0, 3, 1, 2))
    qs, ks = f["ffn_q_scale"], f["ffn_k_scale"]
    scl = np.stack([qs, np.roll(qs, 32, 1), ks, np.roll(ks, 32, 1)], 1)
    out["scl"] = flat(np.broadcast_to(scl[:, None], (LAYERS, P, 4, LD)))
    out["tabc"] = rotary_tables(np)
    return {k: np.ascontiguousarray(v) for k, v in out.items()}

_INS = ["x", "wqk", "wv", "wc", "gnp", "lam", "identf", "wqkv", "wo", "w1", "w2", "b1", "b2", "lnp", "scl", "tabc"]


def kernel(**inputs):
    import numpy as _np
    import concourse.bacc as _bacc
    from concourse import mybir as _mybir
    from concourse.bass_utils import run_bass_kernel_spmd as _run

    nc = _bacc.Bacc("TRN2", target_bir_lowering=False, num_devices=1)
    laid = layouts(inputs)
    nb = laid["x"].shape[0]
    arrays, d = {}, {}
    for name in _INS:
        a = laid[name]
        arrays[f"in_{name}"] = a
        d[name] = nc.dram_tensor(f"in_{name}", a.shape, _mybir.dt.from_np(a.dtype), kind="ExternalInput").ap()
    d["sx"] = nc.dram_tensor("between_phases", (nb * (LAYERS + 1), 2, P, 1024), _mybir.dt.float32, kind="Internal").ap()
    d["out"] = nc.dram_tensor("out", (nb, 2, P, 1024), _mybir.dt.float32, kind="ExternalOutput").ap()
    program(nc, d, nb)
    r = _run(nc, [arrays], core_ids=[0])
    return r.results[0]["out"].reshape(nb, 256, 1024).transpose(0, 2, 1)
```

```python
import math
from contextlib import ExitStack

import concourse.bass as bass
from concourse import mybir

F32 = mybir.dt.float32
BF16 = mybir.dt.bfloat16
ALU = mybir.AluOpType
ACT = mybir.ActivationFunctionType
AX_X = mybir.AxisListType.X

P = 128
EPS = 1e-5
NEG = -3.0e38
START = 64

HEADS = 16
HS = 16
VC = 2 * HS
LAMBDA_INIT = 0.8 - 0.6 * math.exp(-0.3 * (12 - 1))
SCALE = 1.0 / math.sqrt(HS)
Q_PARTS = (0, 0, 0, 1, 1, 2)
K_PARTS = (0, 1, 2, 0, 1, 0)
KDIM = HS * len(Q_PARTS)
KALL = KDIM + 2
UNROLL = 4


LAYERS = 2
LHEADS = 8
LD = 64
WIN = 8
HID = 682
HB = 6
HP = -(-HID // HB)
NORM_SHIFT = 10


def done(n):
    return n + START


def sent(n):
    return 16 * n + START


def max_pieces():
    out = []
    for r in range(8):
        for c0 in range(0, (r + 1) * P, 512):
            c1 = min(c0 + 512, (r + 1) * P)
            out.append((r, c0, c1 - c0, c1 == (r + 1) * P))
    return out


def halves(kb):
    out = []
    for half in range(2):
        lo, hi = max(kb * P, half * 512), (half + 1) * 512
        if lo < hi:
            out.append((half, lo, hi))
    return out


PIECES = max_pieces()
SLOTS = 2 * len(PIECES) + 1
BESIDE = (4, 4, 3, 3, 3, 2, 2, 3)
T_AT = 6
AHEAD = 2 * SLOTS - 1


def slot_of(k):
    return k + (k >= T_AT)


def bank_of(slot):
    return 6 + slot % 2


QKV_SLOTS = 24


def keys_slot(W, w):
    return W * 5 if w == 0 else W * 5 - 1


def probs_slot(W, hp, last):
    return W * 5 + hp + (2 if hp == 3 and not last else 1)


def program(nc, d, nb):
    assert nb % 2 == 0
    with ExitStack() as ctx:
        top = [nc.sbuf_base]

        def sb(name, shape, dt):
            n = 2 if dt == BF16 else 4
            for x in shape[1:]:
                n *= x
            at = (top[0] + 31) // 32 * 32
            top[0] = at + n
            return nc.alloc_sbuf_tensor_at(name, shape, dt, offset=at)

        def sem(name):
            s = ctx.enter_context(nc.semaphore(name))
            counters.append(s)
            return s

        counters = []
        ps = ctx.enter_context(nc.psum_tensor("ps", [P, 8, 512], F32))
        psb = ps[:, :, :].bitcast(BF16)

        ones = sb("ones", [P, VC], F32)
        mean_w = sb("mean_w", [P, P], F32)
        eps_c = sb("eps_c", [P, 1], F32)
        sq = sb("sq", [P, 2, 512], F32)
        rl = sb("rl", [P, 512], F32)
        identf = sb("identf", [P, P], F32)
        base_ab = top[0]
        ident_b = sb("ident_b", [P, P], BF16)
        causal = sb("causal", [P, 512], F32)
        wqk = sb("wqk", [P, 2, 4, 2, P], F32)
        wv = sb("wv", [P, 2, 512], F32)
        wc = sb("wc", [P, 4, 256], F32)
        gnp = sb("gnp", [P, 3], F32)
        gsc = sb("gsc", [P, 2], F32)
        lam_in = sb("lam_in", [P, 4, HEADS], F32)
        lam_t = sb("lam_t", [P, 2, HEADS], F32)
        nlam = sb("nlam", [P, HEADS, VC], F32)
        xt = sb("xt", [P, 2, 1024], F32)
        part = sb("part", [P, 3, 4, 2, 1024], BF16)
        rest = sb("rest", [P, 2, 512], F32)
        qt = sb("qt", [P, UNROLL, 2, 1024], BF16)
        kt = sb("kt", [P, UNROLL, 2, 1024], BF16)
        va = sb("va", [P, 8, 512], F32)
        vs = sb("vs", [P, 2, 8, 2, VC], F32)
        pt = sb("pt", [P, 2, 2, 1024], F32)
        junk = sb("junk", [P, 2, 512], BF16)
        mc = sb("mc", [P, 2, 2, 8], F32)
        mm = sb("mm", [P, 2, 8], F32)
        nm = sb("nm", [P, 2, 2, 8], BF16)
        mt = sb("mt", [32, P], BF16)
        ev = sb("ev", [P, 1024], F32)
        rb = sb("rb", [64, 1024], F32)
        wy = sb("wy", [64, 2, 1024], F32)
        ya = sb("ya", [P, 4, 1024], F32)
        yb = sb("yb", [P, 4, 1024], F32)
        bs = sb("bs", [P, 4, 2, 6], F32)
        mv = sb("mv", [P, 4, 2], F32)
        gl = sb("gl", [P, 4], F32)
        ga = sb("ga", [P, 4], F32)
        gb = sb("gb", [P, 4], F32)
        z = yb[:, 0:2, :]

        top[0] = base_ab
        window = sb("window", [P, 2, 256], F32)
        wqkv = sb("wqkv", [P, 2, 1536], F32)
        wo = sb("wo", [P, 4, 256], F32)
        w1 = sb("w1", [P, 2, 2, HB, HP], F32)
        w2 = sb("w2", [HP, HB, 256], F32)
        tabc = sb("tabc", [P, WIN, 4, LD], F32)
        tab = sb("tab", [P, WIN, 4, LD], F32)
        scl = sb("scl", [P, 4, LD], F32)
        lnp = sb("lnp", [P, 2, 2], F32)
        b1 = sb("b1", [HP, 2, HB], F32)
        b2 = sb("b2", [P, 2], F32)
        xin = sb("xin", [P, 2, 1024], F32)
        xs = sb("xs", [P, 2, 1025], F32)
        xm = sb("xm", [P, 2, 1025], F32)
        xw = sb("xw", [P, 2, 2, P], F32)
        sqw = sb("sqw", [P, 1024], F32)
        ra = sb("ra", [P, 2, LHEADS, LD], F32)
        rr = sb("rr", [P, 2, LHEADS, LD], F32)
        rn = sb("rn", [P, 2 * LHEADS], F32)
        lnn = sb("lnn", [P, 2 * LHEADS], F32)
        rn2 = sb("rn2", [P, 2 * LHEADS], F32)
        nt = sb("nt", [P, 2 * LHEADS], F32)
        qp = sb("qp", [P, 2, 4, P], F32)
        kp = sb("kp", [P, 4, 2, P], F32)
        vt = sb("vt", [P, 2, 512], F32)
        sm = sb("sm", [P, 2, 2, 256], F32)
        mxw = sb("mxw", [P, 4, 2], F32)
        sumw = sb("sumw", [P, 4, 2], F32)
        ptw = sb("ptw", [P, 2, 4, P], F32)
        ot = sb("ot", [P, 4, 1024], F32)
        cn = sb("cn", [P, 2, 1024], F32)
        sqf = sb("sqf", [P, 2, 512], F32)
        rlf = sb("rlf", [P, 512], F32)
        ge = sb("ge", [HP, 2, 512], F32)
        hh = sb("hh", [HP, 2, HB, 512], F32)
        xo = sb("xo", [P, 2, 1024], F32)
        zc = sb("zc", [P, 2, 1024], F32)
        xc = sb("xc", [P, 2, 1024], F32)
        units = ((xo, xin, 0), (xo, xin, 1), (zc, xc, 0), (zc, xc, 1))

        const_ready = sem("const_ready")
        w_ready = sem("w_ready")
        x_ready = sem("x_ready")
        ident_ready = sem("ident_ready")
        lam_ready = sem("lam_ready")
        proj_full = sem("proj_full")
        high_done = sem("high_done")
        rest_done = sem("rest_done")
        mid_done = sem("mid_done")
        low_done = sem("low_done")
        v_done = sem("v_done")
        op_ready = [sem(f"op_ready{u}") for u in range(UNROLL)]
        max_full = sem("max_full")
        max_free = sem("max_free")
        mc_done = sem("mc_done")
        mx_done = sem("mx_done")
        nm_done = sem("nm_done")
        mrow_ready = sem("mrow_ready")
        st_full = sem("st_full")
        exp_done = sem("exp_done")
        masked = sem("masked")
        vs_ready = sem("vs_ready")
        pv_done = sem("pv_done")
        ev_done = sem("ev_done")
        ln_done = sem("ln_done")
        rb_done = sem("rb_done")
        wy_done = sem("wy_done")
        y_ready = [sem(f"y_ready{p}") for p in range(2)]
        ysum_done = sem("ysum_done")
        bn_done = sem("bn_done")
        bnag_done = sem("bnag_done")
        gl_done = sem("gl_done")
        gr_done = sem("gr_done")
        ga_done = sem("ga_done")
        gt_done = sem("gt_done")
        gb_done = sem("gb_done")
        yn_done = sem("yn_done")
        out_full = sem("out_full")
        z_done = sem("z_done")
        mean_full = sem("mean_full")
        cen_done = sem("cen_done")
        sq_done = sem("sq_done")
        var_full = sem("var_full")
        lv_done = sem("lv_done")
        rs_done = sem("rs_done")
        norm_done = sem("norm_done")
        stored = sem("stored")

        wl_ready = sem("wl_ready")
        wf_ready = sem("wf_ready")
        tab_ready = sem("tab_ready")
        k2_ready = sem("k2_ready")
        tab_done = sem("tab_done")
        xin_ready = sem("xin_ready")
        xs_ready = sem("xs_ready")
        xw_ready = sem("xw_ready")
        qk_full = sem("qk_full")
        v_full = sem("v_full")
        vt_done = sem("vt_done")
        sqw_done = sem("sqw_done")
        ssq_done = sem("ssq_done")
        ssc_done = sem("ssc_done")
        lnq_done = sem("lnq_done")
        rn_done = sem("rn_done")
        nt_done = sem("nt_done")
        ra_done = sem("ra_done")
        rsum_done = sem("rsum_done")
        rot_done = sem("rot_done")
        tq_full = sem("tq_full")
        tq_read = sem("tq_read")
        s_full = sem("s_full")
        s_read = sem("s_read")
        e_done = sem("e_done")
        rc_done = sem("rc_done")
        p_ready = sem("p_ready")
        t_full = sem("t_full")
        t_read = sem("t_read")
        o_full = sem("o_full")
        o_read = sem("o_read")
        wo_full = sem("wo_full")
        xm_done = sem("xm_done")
        fm_full = sem("fm_full")
        fc_done = sem("fc_done")
        fs_done = sem("fs_done")
        fv_full = sem("fv_full")
        fl_done = sem("fl_done")
        fr_done = sem("fr_done")
        fn_done = sem("fn_done")
        hn_done = sem("hn_done")
        g_full = sem("g_full")
        a_full = sem("a_full")
        ge_done = sem("ge_done")
        hh_done = sem("hh_done")
        w2_full = sem("w2_full")
        xo_done = sem("xo_done")
        storedb = sem("storedb")
        z_ready = [sem(f"z_ready{i}") for i in range(4)]
        zsum_done = sem("zsum_done")
        storedc = [sem(f"storedc{i}") for i in range(4)]
        sp_passed = sem("sp_passed")
        pe_passed = sem("pe_passed")
        dve_passed = sem("dve_passed")
        pool_passed = sem("pool_passed")

        TENSORS_A, TENSORS_ATTENTION, TENSORS_FFN = 6, 2, 6
        block = ctx.enter_context(nc.Block())

        @block.sync
        def _(sp):
            sp.dma_start(wqk[:], d["wqk"]).then_inc(w_ready, 16)
            sp.dma_start(wv[:], d["wv"]).then_inc(w_ready, 16)
            sp.dma_start(lam_in[:], d["lam"]).then_inc(w_ready, 16)
            sp.dma_start(gnp[:], d["gnp"]).then_inc(w_ready, 16)
            sp.dma_start(identf[:], d["identf"]).then_inc(w_ready, 16)
            sp.dma_start(wc[:], d["wc"]).then_inc(w_ready, 16)

            def load_x(b):
                sp.wait_ge(z_done, done(b * 4))
                sp.dma_start(xt[:], d["x"][bass.ds(b, 1)].rearrange("a c p t -> p (a c) t")).then_inc(x_ready, 16)

            def sequence(b, more):
                def operands(h):
                    u, c, p0 = h % UNROLL, h // 8, HS * (h % 8)
                    sp.wait_ge(st_full, done((b * 16 + h - 3) * 16))
                    sp.sem_inc(sp_passed, 1)
                    for t, parts, n in ((qt, Q_PARTS, 0), (kt, K_PARTS, 2)):
                        sp.wait_ge(low_done, done(b * 16 + 8 * c + 4 + 2 * n))
                        for s in range(6):
                            sp.dma_start(t[HS * s:HS * (s + 1), u, :, :],
                                         part[p0:p0 + HS, parts[s], n:n + 2, c, :]).then_inc(op_ready[u], 16)

                def max_rows(h):
                    slot = SLOTS - 1 if h == 0 else AHEAD + (h - 1) * SLOTS + (T_AT if h < HEADS - 1 else 0)
                    sp.wait_ge(max_free, done(b * HEADS * SLOTS + slot + 1))
                    for a in range(2):
                        sp.dma_start(qt[KDIM + a:KDIM + a + 1, h % UNROLL, :, :].rearrange("p i (k q) -> p (i k) q", q=P),
                                     mt[16 * a:16 * a + 16, :]).then_inc(mrow_ready, 16)

                def values_out(h):
                    sp.wait_ge(wy_done, done(b * 16 + h + 1))
                    if h == 0:
                        sp.wait_ge(norm_done, done(b * 2))
                        sp.wait_ge(stored, sent(b * 2))
                    for a, t in ((0, ya), (1, yb)):
                        sp.dma_start(t[VC * (h % 4):VC * (h % 4 + 1), h // 4, :],
                                     wy[32 * a:32 * a + 32, h % 2, :]).then_inc(y_ready[h % 2], 16)

                for h in range(3):
                    operands(h)
                max_rows(0)
                for h in range(HEADS):
                    if h + 3 < HEADS:
                        operands(h + 3)
                    if h + 1 < HEADS:
                        max_rows(h + 1)
                    if h:
                        values_out(h - 1)
                values_out(HEADS - 1)
                if more:
                    load_x(b + 1)
                for half in range(2):
                    sp.wait_ge(norm_done, done(b * 2 + half + 1))
                    sp.dma_start(d["sx"][bass.ds(b, 1), :, :, half * 512:half * 512 + 512].rearrange("a c p t -> p (a c) t"),
                                 z[:, :, half * 512:half * 512 + 512]).then_inc(stored, 16)

            load_x(0)
            with sp.Fori(0, nb - 1) as b:
                sequence(b, True)
            sequence(nb - 1, False)
            sp.wait_ge(stored, sent(nb * 2))

            def weights(l, tiles, signal):
                for t, name in tiles:
                    axes = " ".join("ijkm"[:len(t.shape) - 1])
                    sizes = {x: n for x, n in zip("jkm", t.shape[2:])}
                    src = d[name][bass.ds(l, 1)].rearrange("a p n -> p (a n)").rearrange(f"p ({axes}) -> p {axes}", **sizes)
                    sp.dma_start(t[:], src).then_inc(signal, 16)

            attention_tiles = ((wqkv, "wqkv"), (scl, "scl"))
            ffn_tiles = ((wo, "wo"), (w1, "w1"), (w2, "w2"), (lnp, "lnp"), (b1, "b1"), (b2, "b2"))

            def load(lb):
                sp.wait_ge(xs_ready, done(lb))
                sp.wait_ge(storedb, sent(lb * 2 - 2))
                sp.dma_start(xin[:], d["sx"][bass.ds(lb, 1)].rearrange("a c p t -> p (a c) t")).then_inc(xin_ready, 16)

            def store(lb):
                for half in range(2):
                    sp.wait_ge(xo_done, done(lb * 4 + 2 * half + 2))
                    sp.dma_start(d["sx"][bass.ds(lb + nb, 1), :, :, half * 512:half * 512 + 512].rearrange("a c p t -> p (a c) t"),
                                 xo[:, :, half * 512:half * 512 + 512]).then_inc(storedb, 16)

            def layer(l, more):
                with sp.Fori(0, nb - 1) as b:
                    load(l * nb + b + 1)
                    store(l * nb + b)
                if more:
                    sp.wait_ge(v_full, done((l + 1) * nb * WIN))
                    sp.wait_ge(ra_done, done((l + 1) * nb * WIN * 3))
                    weights(l + 1, attention_tiles, wl_ready)
                    load((l + 1) * nb)
                store(l * nb + nb - 1)
                if more:
                    weights(l + 1, ffn_tiles, wf_ready)

            load(0)
            weights(0, attention_tiles, wl_ready)
            sp.dma_start(tabc[:], d["tabc"]).then_inc(tab_ready, 16)
            weights(0, ffn_tiles, wf_ready)
            with sp.Fori(0, LAYERS - 1) as l:
                layer(l, True)
            layer(LAYERS - 1, False)
            sp.wait_ge(storedb, sent(LAYERS * nb * 2))

            def load_unit(q, i):
                z, x, half = units[i]
                sp.wait_ge(storedc[i], sent(q))
                for t, first in ((z, LAYERS * nb), (x, 0)):
                    src = d["sx"][bass.ds(q * 2 + (first + i // 2), 1), :, :, half * 512:half * 512 + 512]
                    sp.dma_start(t[:, :, half * 512:half * 512 + 512],
                                 src.rearrange("a c p t -> p (a c) t")).then_inc(z_ready[i], 16)

            def store_unit(q, i):
                z, x, half = units[i]
                sp.wait_ge(norm_done, done(nb * 2 + q * 4 + (i + 1)))
                sp.sem_inc(sp_passed, 1)
                out = d["out"][bass.ds(q * 2 + i // 2, 1), :, :, half * 512:half * 512 + 512]
                sp.dma_start(out.rearrange("a c p t -> p (a c) t"),
                             z[:, :, half * 512:half * 512 + 512]).then_inc(storedc[i], 16)

            for i in range(3):
                load_unit(0, i)
            with sp.Fori(0, nb // 2 - 1) as q:
                for i in range(4):
                    store_unit(q, i)
                    load_unit(q + (i + 3) // 4, (i + 3) % 4)
            for i in range(4):
                store_unit(nb // 2 - 1, i)
                if i == 0:
                    load_unit(nb // 2 - 1, 3)
            for i in range(4):
                sp.wait_ge(storedc[i], sent(nb // 2))

        @block.tensor
        def _(pe):
            pe.wait_ge(w_ready, sent(TENSORS_A))
            pe.wait_ge(const_ready, done(8))
            pe.wait_ge(ident_ready, done(1))

            def mean(src, half):
                for c in range(2):
                    mmi = pe.matmul(ps[:, 4 + half, :], mean_w[:], src[:, c, half * 512:half * 512 + 512],
                                    start=c == 0, stop=c == 1)
                mmi.then_inc(mean_full, 1)

            def variances(k):
                for half in range(2):
                    pe.wait_ge(sq_done, done(k * 2 + half + 1))
                    for c in range(2):
                        mmi = pe.matmul(ps[:, 6 + half, :], mean_w[:], sq[:, c, :], start=c == 0, stop=c == 1)
                    mmi.then_inc(var_full, 1)

            with pe.Fori(0, nb) as b:
                h0 = pe.snap(b * HEADS)

                pe.wait_ge(x_ready, sent(b + 1))
                def project(s):
                    k = s if s < 8 else s - 8
                    if s >= 4:
                        o = s - 4
                        if 8 <= o < 16:
                            pe.wait_ge(v_done, done(b * 8 + o - 8 + 1))
                        else:
                            pe.wait_ge(rest_done, done(b * 16 + (o if o < 8 else o - 8) + 1))
                    for kc in range(2):
                        if 8 <= s < 16:
                            blk = s - 8
                            mmi = pe.matmul(ps[:, s % 4, :], xt[:, kc, blk * P:(blk + 1) * P], wv[:, kc, :],
                                            start=kc == 0, stop=kc == 1)
                        else:
                            c, n, half = k // 8, k % 8 // 2, k % 2
                            mmi = pe.matmul(ps[:, s % 4, :], wqk[:, kc, n, c, :], xt[:, kc, half * 512:half * 512 + 512],
                                            start=kc == 0, stop=kc == 1)
                    mmi.then_inc(proj_full, 1)

                def piece(g, u, k, slot, parity):
                    r, c0, w, _ = PIECES[k % 12]
                    i = k // 12
                    if k == 0:
                        pe.wait_ge(op_ready[u], sent((g - u) * 3 + 12))
                    pe.wait_ge(max_free, done(slot - 1))
                    pe.matmul(ps[:, bank_of(parity), 0:w], qt[0:KDIM, u, i, r * P:(r + 1) * P],
                              kt[0:KDIM, u, i, c0:c0 + w], start=True, stop=True).then_inc(max_full, 1)

                def max_transpose(g, slot, parity):
                    pe.wait_ge(nm_done, done(g + 1))
                    pe.wait_ge(max_free, done(slot - 1))
                    pe.transpose(psb[0:32, bank_of(parity), 0:P], nm[:, :, :, :].rearrange("p a i k -> p (a i k)"),
                                 ident_b[:]).then_inc(max_full, 1)

                def scores(g, u, kb, i):
                    if kb == 0 and i == 0:
                        pe.wait_ge(mrow_ready, sent(2 * g + 2))
                    pe.wait_ge(exp_done, done(g * 16 + 2 * kb + i - 1))
                    for half, lo, hi in halves(kb):
                        mmi = pe.matmul(ps[:, 2 * i + half, lo - half * 512:hi - half * 512],
                                        kt[0:KALL, u, i, kb * P:(kb + 1) * P], qt[0:KALL, u, i, lo:hi],
                                        start=True, stop=True)
                    mmi.then_inc(st_full, 1)

                def values(g, u, kb, n):
                    half, lo, hi = halves(kb)[n]
                    if kb == 0:
                        pe.wait_ge(ev_done, done(g * 2 + (half - 1)))
                    if n == 0:
                        if kb == 0:
                            pe.wait_ge(vs_ready, done(g + 1))
                        pe.wait_ge(masked, done(g * 8 + kb + 1))
                    for q in range(4):
                        i = q % 2
                        w = vs[:, u % 2, kb, i, :] if q < 2 else ones[:]
                        mmi = pe.matmul(ps[32 * q:32 * q + 32, 4 + half, lo - half * 512:hi - half * 512], w,
                                        pt[:, kb % 2, i, lo:hi], start=kb == 0, stop=kb == 4 * half + 3)
                    if n == len(halves(kb)) - 1:
                        mmi.then_inc(pv_done, 1)

                def group(g0, slots, last):
                    for u in range(UNROLL):
                        g = g0 + u
                        nxt, un = g + 1, (u + 1) % UNROLL
                        one = not (last and u == UNROLL - 1)
                        two = not (last and u >= UNROLL - 2)
                        slot, parity, k = slots + u * SLOTS, 1 + u, 0
                        for kb in range(8):
                            steps = [(values, (g, u, kb, n)) for n in range(len(halves(kb)))]
                            if kb < 7:
                                steps = [(scores, (g, u, kb + 1, 0)), (scores, (g, u, kb + 1, 1))] + steps
                            elif one:
                                steps = [(scores, (nxt, un, 0, 0)), (scores, (nxt, un, 0, 1))] + steps
                            if one and not two and kb == 1:
                                max_transpose(nxt, slot, parity)
                            for n, (step, args) in enumerate(steps):
                                step(*args)
                                while two and k < sum(BESIDE[:kb]) + BESIDE[kb] * (n + 1) // len(steps):
                                    if k == T_AT:
                                        max_transpose(nxt, slot + k, parity + k)
                                    piece(g + 2, (u + 2) % UNROLL, k, slot + slot_of(k), parity + slot_of(k))
                                    k += 1

                first = pe.snap(h0 * SLOTS)
                for s in range(16):
                    project(s)
                pe.wait_ge(norm_done, done(b * 2))
                for k in range(24):
                    piece(h0, 0, k, first + k, k)
                    if k % 8 == 5:
                        project(16 + k // 8)
                max_transpose(h0, first + 24, 24)
                for n in range(8):
                    for k in range(3 * n, 3 * n + 3):
                        piece(h0 + 1, 1, k, first + (SLOTS + k), SLOTS + k)
                    if 19 + n < QKV_SLOTS:
                        project(19 + n)
                scores(h0, 0, 0, 0)
                scores(h0, 0, 0, 1)
                with pe.Fori(0, HEADS // UNROLL - 1) as j:
                    g0 = pe.snap(b * HEADS + j * UNROLL)
                    group(g0, pe.snap(g0 * SLOTS + AHEAD), False)
                g0 = pe.snap(b * HEADS + HEADS - UNROLL)
                group(g0, pe.snap(g0 * SLOTS + AHEAD), True)

                pe.wait_ge(exp_done, done(h0 * 16 + HEADS * 16))
                tiles = [(0, 0), (1, 0), (0, 1), (1, 1)]

                def project_out(n, fs):
                    oc, half = tiles[n]
                    for f in fs:
                        mmi = pe.matmul(ps[:, n, :], wc[:, f, oc * P:(oc + 1) * P],
                                        ya[:, f, half * 512:half * 512 + 512], start=f == 0, stop=f == 3)
                    return mmi

                pe.wait_ge(yn_done, done(b * 4 + 3))
                for n in range(4):
                    project_out(n, range(3))
                pe.wait_ge(yn_done, done(b * 4 + 4))
                for n in range(4):
                    project_out(n, [3]).then_inc(out_full, 1)
                    if n == 2:
                        pe.wait_ge(z_done, done(b * 4 + 2))
                        mean(z, 0)
                pe.wait_ge(z_done, done(b * 4 + 4))
                mean(z, 1)
                variances(b)

            with pe.Fori(0, LAYERS) as l:
                pe.wait_ge(k2_ready, done(5))
                pe.wait_ge(wl_ready, sent((l + 1) * TENSORS_ATTENTION))
                pe.sem_inc(pe_passed, 1)
                def project(par, n):
                    for kc in range(2):
                        mmi = pe.matmul(ps[:, n, :], xw[:, par, kc, :], wqkv[:, kc, n * 512:n * 512 + 512],
                                        start=kc == 0, stop=kc == 1)
                    return mmi

                def queries_keys(W, par, n=2, at=2, before=0):
                    pe.wait_ge(xw_ready, done(W + 1))
                    if at < 2:
                        pe.wait_ge(hh_done, done(before * 12))
                    else:
                        pe.wait_ge(ra_done, done(W * 3))
                    project(par, 0)
                    if n == 2:
                        keys(par)

                def keys(par):
                    project(par, 1).then_inc(qk_full, 1)

                def values(W, par):
                    pe.wait_ge(vt_done, done(W))
                    project(par, 2).then_inc(v_full, 1)

                def transpose_qk(W, w):
                    pe.wait_ge(rot_done, done(W + 1))
                    pe.wait_ge(t_read, done(keys_slot(W, w)))
                    for hp in range(4):
                        mmi = pe.transpose(ps[:, 6, hp * P:(hp + 1) * P],
                                           rr[:, 1, 2 * hp:2 * hp + 2, :].rearrange("p h e -> p (h e)"), identf[:])
                    mmi.then_inc(t_full, 1)
                    pe.wait_ge(tq_read, done(W))
                    for hp in range(4):
                        mmi = pe.transpose(ps[:, 3, hp * P:(hp + 1) * P],
                                           rr[:, 0, 2 * hp:2 * hp + 2, :].rearrange("p h e -> p (h e)"), identf[:])
                    mmi.then_inc(tq_full, 1)

                def scores(W, w, hp):
                    first = w == 0
                    if hp == 0:
                        pe.wait_ge(t_read, done(keys_slot(W, w) + 1))
                        pe.wait_ge(tq_read, done(W + 1))
                    pe.wait_ge(s_read, done(W * 4 + hp - 1))
                    n = P if first else 256
                    for q in range(2):
                        mmi = pe.matmul(ps[:, 4 + hp % 2, q * 256:q * 256 + n], qp[:, q, hp, :],
                                        kp[:, hp, :, :].rearrange("p a k -> p (a k)")[:, 0:n], start=True, stop=True)
                    mmi.then_inc(s_full, 1)

                def transpose_p(W, w, hp):
                    slot = probs_slot(W, hp, w == WIN - 1)
                    pe.wait_ge(p_ready, done(W * 4 + hp + 1))
                    pe.wait_ge(t_read, done(slot))
                    for q in range(2):
                        for a in range(1 if w == 0 else 2):
                            mmi = pe.transpose(ps[:, 6, (2 * q + a) * P:(2 * q + a + 1) * P],
                                               sm[:, hp % 2, q, a * P:(a + 1) * P], identf[:])
                    mmi.then_inc(t_full, 1)

                def weigh(W, w, hp):
                    n = 1 if w == 0 else 2
                    if hp == 0:
                        pe.wait_ge(vt_done, done(W + 1))
                        pe.wait_ge(o_read, done(W))
                    pe.wait_ge(t_read, done(probs_slot(W, hp, w == WIN - 1) + 1))
                    for a in range(n):
                        for q in range(2):
                            mmi = pe.matmul(ps[64 * q:64 * q + 64, 7, hp * P:(hp + 1) * P],
                                            vt[:, a, (2 * hp + q) * LD:(2 * hp + q + 1) * LD],
                                            ptw[:, hp % 2, 2 * q + a, :], start=a == 0, stop=a == n - 1)
                    mmi.then_inc(o_full, 1)

                def attend(W, w, lb=None):
                    par, more = w % 2, w < WIN - 1
                    values(W, par)
                    transpose_p(W, w, 0)
                    scores(W, w, 2)
                    weigh(W, w, 0)
                    transpose_p(W, w, 1)
                    if w < WIN - 2:
                        queries_keys(W + 2, par, n=1)
                    elif w == WIN - 2:
                        attention_out(lb, 0, 0)
                    else:
                        mean(lb, 0, 0)
                    scores(W, w, 3)
                    weigh(W, w, 1)
                    transpose_p(W, w, 2)
                    if w < WIN - 2:
                        keys(par)
                    if more:
                        transpose_qk(W + 1, w + 1)
                    weigh(W, w, 2)
                    transpose_p(W, w, 3)
                    if more:
                        scores(W + 1, w + 1, 0)
                    else:
                        variance(lb, 0, 1)
                    weigh(W, w, 3)
                    if more:
                        scores(W + 1, w + 1, 1)

                def attention_out(lb, half, bank):
                    pe.wait_ge(wf_ready, sent((l + 1) * TENSORS_FFN))
                    pe.wait_ge(o_read, done(lb * WIN + 4 * half + 4))
                    if half == 0:
                        pe.wait_ge(ra_done, done((lb + 1) * WIN * 3))
                    else:
                        pe.wait_ge(t_read, done((lb + 1) * WIN * 5))
                    for oc in range(2):
                        for f in range(4):
                            mmi = pe.matmul(ps[:, bank + oc, :], wo[:, f, oc * P:(oc + 1) * P],
                                            ot[:, f, half * 512:half * 512 + 512], start=f == 0, stop=f == 3)
                        mmi.then_inc(wo_full, 1)

                def mean(lb, half, bank):
                    pe.wait_ge(xm_done, done(lb * 4 + 2 * half + 2))
                    if half:
                        pe.wait_ge(s_read, done((lb + 1) * WIN * 4))
                    for kc in range(2):
                        mmi = pe.matmul(ps[:, bank, :], mean_w[:],
                                        xm[:, kc, 1 - kc + half * 512:1 - kc + half * 512 + 512],
                                        start=kc == 0, stop=kc == 1)
                    mmi.then_inc(fm_full, 1)

                def variance(lb, half, bank):
                    pe.wait_ge(fs_done, done(lb * 2 + half + 1))
                    for kc in range(2):
                        mmi = pe.matmul(ps[:, bank, :], mean_w[:], sqf[:, kc, :], start=kc == 0, stop=kc == 1)
                    mmi.then_inc(fv_full, 1)

                def hidden(lb, k):
                    half, j = k // HB, k % HB
                    if j == 0:
                        pe.wait_ge(hn_done, done(lb * 4 + 2 * half + 2))
                    if k == 0:
                        pe.wait_ge(vt_done, done((lb + 1) * WIN))
                        pe.wait_ge(tq_read, done((lb + 1) * WIN))
                    for a, (full, free) in enumerate(((a_full, hh_done), (g_full, ge_done))):
                        if k >= 2:
                            pe.wait_ge(free, done(lb * 12 + k - 1))
                        for kc in range(2):
                            mmi = pe.matmul(ps[0:HP, 2 * a + k % 2, :], w1[:, kc, a, j, :],
                                            cn[:, kc, half * 512:half * 512 + 512], start=kc == 0, stop=kc == 1)
                        mmi.then_inc(full, 1)

                def ffn_out(lb, half):
                    pe.wait_ge(hh_done, done(lb * 12 + (half + 1) * HB))
                    for oc in range(2):
                        for j in range(HB):
                            mmi = pe.matmul(ps[:, 4 + 2 * half + oc, :], w2[:, j, oc * P:(oc + 1) * P], hh[:, half, j, :],
                                            start=j == 0, stop=j == HB - 1)
                        mmi.then_inc(w2_full, 1)

                def start_1(lb):
                    queries_keys(lb * WIN, 0, at=0, before=lb)

                def start_2(lb):
                    W0 = lb * WIN
                    pe.wait_ge(ra_done, done(W0 * 3 + 3))
                    queries_keys(W0 + 1, 1, at=1, before=lb)
                    pe.wait_ge(xo_done, done(lb * 4))
                    transpose_qk(W0, 0)
                    scores(W0, 0, 0)
                    scores(W0, 0, 1)

                def sequence(lb, more):
                    W0 = pe.snap(lb * WIN)
                    attend(W0, 0)
                    with pe.Fori(0, 2) as j:
                        W1 = pe.snap(W0 + j * 2 + 1)
                        attend(W1, 1)
                        attend(W1 + 1, 2)
                    for w in (5, 6, 7):
                        attend(W0 + w, w, lb)
                    hidden(lb, 0)
                    hidden(lb, 1)
                    attention_out(lb, 1, 6)
                    hidden(lb, 2)
                    mean(lb, 1, 4)
                    hidden(lb, 3)
                    variance(lb, 1, 5)
                    for k in range(4, 2 * HB):
                        hidden(lb, k)
                    ffn_out(lb, 0)
                    if more:
                        start_1(lb + 1)
                    ffn_out(lb, 1)
                    if more:
                        start_2(lb + 1)

                start_1(l * nb)
                start_2(l * nb)
                with pe.Fori(0, nb - 1) as b:
                    sequence(pe.snap(l * nb + b), True)
                sequence(pe.snap(l * nb + (nb - 1)), False)

            def mean_unit(n, i):
                z, _, half = units[i]
                pe.wait_ge(zsum_done, done(n + 1))
                pe.wait_ge(cen_done, done(nb * 2 + n - 1))
                for c in range(2):
                    mmi = pe.matmul(ps[:, 4 + i % 2, :], mean_w[:], z[:, c, half * 512:half * 512 + 512],
                                    start=c == 0, stop=c == 1)
                mmi.then_inc(mean_full, 1)

            def variance_unit(n, i):
                pe.wait_ge(sq_done, done(nb * 2 + n + 1))
                pe.wait_ge(lv_done, done(nb * 2 + n - 1))
                for c in range(2):
                    mmi = pe.matmul(ps[:, 6 + i % 2, :], mean_w[:], sq[:, c, :], start=c == 0, stop=c == 1)
                mmi.then_inc(var_full, 1)

            def four(n, first):
                for i in range(4):
                    mean_unit(n + i, i)
                    if not (first and i == 0):
                        variance_unit(n + (i - 1), (i + 3) % 4)

            four(0, True)
            with pe.Fori(1, nb // 2) as q:
                four(pe.snap(q * 4), False)
            variance_unit(nb * 2 - 1, 3)

        @block.scalar
        def _(act):
            act.wait_ge(w_ready, sent(TENSORS_A))
            act.wait_ge(const_ready, done(8))
            act.wait_ge(lam_ready, done(1))
            act.activation(lam_t[:, :, :], lam_t[:, :, :], ACT.Exp, scale=-1.0).then_inc(lam_ready, 1)

            def feature_norm(k, src):
                for half in range(2):
                    act.wait_ge(cen_done, done(k * 2 + half + 1))
                    act.wait_ge(var_full, done(k * 2 + half))
                    act.activation(sq[:, :, :], src[:, :, half * 512:half * 512 + 512], ACT.Square).then_inc(sq_done, 1)
                    act.wait_ge(var_full, done(k * 2 + half + 1))
                    act.wait_ge(norm_done, done(k * 2 + half))
                    act.activation(rl[:, :], ps[:, 6 + half, :], ACT.Ln, bias=eps_c[:, 0:1]).then_inc(lv_done, 1)
                    act.wait_ge(lv_done, done(k * 2 + half + 1))
                    act.activation(rl[:, :], rl[:, :], ACT.Exp, scale=-0.5).then_inc(rs_done, 1)

            act.preload_act_table_set("natural_log_exp_and_others")
            with act.Fori(0, nb) as b:
                h0 = act.snap(b * HEADS)

                def middle(k):
                    act.wait_ge(rest_done, done(b * 16 + k + 1))
                    c, n, half = k // 8, k % 8 // 2, k % 2
                    act.activation(part[:, 1, n, c, half * 512:half * 512 + 512], rest[:, k % 2, :],
                                   ACT.Copy).then_inc(mid_done, 1)

                for s in range(QKV_SLOTS):
                    act.wait_ge(proj_full, done(b * QKV_SLOTS + s + 1))
                    if 8 <= s < 16:
                        if s == 8:
                            middle(7)
                        act.activation(va[:, s - 8, :], ps[:, s % 4, :], ACT.Copy).then_inc(v_done, 1)
                    else:
                        k = s if s < 8 else s - 8
                        c, n, half = k // 8, k % 8 // 2, k % 2
                        act.activation(part[:, 0, n, c, half * 512:half * 512 + 512], ps[:, s % 4, :],
                                       ACT.Copy).then_inc(high_done, 1)
                        if k % 8:
                            middle(k - 1)
                middle(15)

                def exps(g, kb):
                    for i in range(2):
                        act.wait_ge(st_full, done(g * 16 + 2 * kb + i + 1))
                        if i == 0:
                            act.wait_ge(pv_done, done(g * 8 + kb - 1))
                        act.activation(pt[:, kb % 2, i, kb * P:1024],
                                       ps[:, 2 * i:2 * i + 2, :].rearrange("p a q -> p (a q)")[:, kb * P:1024],
                                       ACT.Exp, scale=SCALE).then_inc(exp_done, 1)

                def copy_out(g, half):
                    act.wait_ge(pv_done, done(g * 8 + 4 * half + 4))
                    if half == 0:
                        act.wait_ge(wy_done, done(g))
                    act.activation(ev[:, half * 512:half * 512 + 512], ps[:, 4 + half, :], ACT.Copy).then_inc(ev_done, 1)

                def invert(g):
                    act.wait_ge(ev_done, done(g * 2 + 2))
                    act.activation(rb[:, :], ev[64:128, :], ACT.Ln).then_inc(ln_done, 1)
                    act.wait_ge(ln_done, done(g + 1))
                    act.activation(rb[:, :], rb[:, :], ACT.Exp, scale=-1.0).then_inc(rb_done, 1)

                def group(g0, first, last):
                    for u in range(UNROLL):
                        g = g0 + u
                        for kb in range(8):
                            exps(g, kb)
                            if kb == 5:
                                copy_out(g, 0)
                            if kb == 0 and not (first and u == 0):
                                copy_out(g - 1, 1)
                            if kb == 1 and not (first and u == 0):
                                invert(g - 1)
                            if last and u == UNROLL - 1 and kb == 2:
                                over_time(0)

                def over_time(n):
                    v = gl[:, 3 * n:3 + n]
                    act.wait_ge(bnag_done, done(b * 4 + 3 + n))
                    act.activation(v, mv[:, 3 * n:3 + n, 1], ACT.Ln, bias=eps_c[:, 0:1]).then_inc(gl_done, 1)
                    act.wait_ge(gl_done, done(b * 2 + n + 1))
                    act.activation(v, v, ACT.Exp, scale=-0.5).then_inc(gr_done, 1)

                group(h0, True, False)
                with act.Fori(1, HEADS // UNROLL - 1) as j:
                    group(act.snap(b * HEADS + j * UNROLL), False, False)
                group(act.snap(b * HEADS + HEADS - UNROLL), False, True)
                g = act.snap(b * HEADS + HEADS - 1)
                copy_out(g, 1)
                invert(g)

                over_time(1)
                feature_norm(b, z)

            with act.Fori(0, LAYERS) as l:
                act.preload_act_table_set("natural_log_exp_and_others")
                act.wait_ge(wl_ready, sent((l + 1) * TENSORS_ATTENTION))
                act.wait_ge(k2_ready, done(5))

                def squares(W):
                    act.wait_ge(qk_full, done(W + 1))
                    act.activation(sqw[:, :], ps[:, 0:2, :].rearrange("p a q -> p (a q)"), ACT.Square).then_inc(sqw_done, 1)

                def inverse_norms(W):
                    act.wait_ge(ssc_done, done(W + 1))
                    act.activation(lnn[:, :], rn[:, :], ACT.Ln).then_inc(lnq_done, 1)
                    act.wait_ge(lnq_done, done(W + 1))
                    act.wait_ge(rot_done, done(W))
                    act.activation(rn2[:, :], lnn[:, :], ACT.Exp, scale=-0.5).then_inc(rn_done, 1)

                def values(W, par):
                    act.wait_ge(v_full, done(W + 1))
                    act.wait_ge(o_full, done(W * 4))
                    act.activation(vt[:, par, :], ps[:, 2, :], ACT.Copy).then_inc(vt_done, 1)

                def place_qk(W, w):
                    act.wait_ge(t_full, done(keys_slot(W, w) + 1))
                    act.activation(kp[:, :, w % 2, :], ps[:, 6, :].rearrange("p (a k) -> p a k", a=4), ACT.Copy).then_inc(t_read, 1)
                    act.wait_ge(tq_full, done(W + 1))
                    for q in range(2):
                        rows = slice(64 * q, 64 * q + 64)
                        i = act.activation(qp[rows, q, :, :], ps[rows, 3, :].rearrange("p (a k) -> p a k", a=4), ACT.Copy)
                    i.then_inc(tq_read, 1)

                def exps(W, w, hp):
                    act.wait_ge(s_read, done(W * 4 + hp + 1))
                    n = P if w == 0 else 256
                    for q in range(2):
                        i = act.activation(sm[:, hp % 2, q, 0:n], sm[:, hp % 2, q, 0:n], ACT.Exp, scale=-1.0,
                                           bias=mxw[:, hp, q:q + 1], accum_out=sumw[:, hp, q:q + 1])
                    i.then_inc(e_done, 1)

                def place_p(W, w, hp):
                    act.wait_ge(t_full, done(probs_slot(W, hp, w == WIN - 1) + 1))
                    act.wait_ge(o_full, done(W * 4 + hp - 1))
                    n = 1 if w == 0 else 2
                    act.activation(ptw[:, hp % 2, :, :].rearrange("p (q a) k -> p q a k", q=2)[:, :, 0:n, :],
                                   ps[:, 6, :].rearrange("p (q a k) -> p q a k", q=2, a=2)[:, :, 0:n, :],
                                   ACT.Copy).then_inc(t_read, 1)

                def attend(W, w, lb=None):
                    more = w < WIN - 1
                    exps(W, w, 0)
                    exps(W, w, 1)
                    values(W, w % 2)
                    place_p(W, w, 0)
                    exps(W, w, 2)
                    place_p(W, w, 1)
                    place_p(W, w, 2)
                    exps(W, w, 3)
                    if w < WIN - 2:
                        squares(W + 2)
                    if more:
                        place_qk(W + 1, w + 1)
                    else:
                        squared_deviations(lb, 0)
                    place_p(W, w, 3)
                    if w < WIN - 2:
                        inverse_norms(W + 2)

                def squared_deviations(lb, half):
                    act.wait_ge(fc_done, done(lb * 4 + 2 * half + 2))
                    act.wait_ge(fv_full, done(lb * 2 + half))
                    act.activation(sqf[:, :, :], cn[:, :, half * 512:half * 512 + 512], ACT.Square).then_inc(fs_done, 1)

                def inverse_deviation(lb, half, bank):
                    act.wait_ge(fv_full, done(lb * 2 + half + 1))
                    act.wait_ge(fn_done, done(lb * 2 + half))
                    act.activation(rlf[:, :], ps[:, bank, :], ACT.Ln, bias=eps_c[:, 0:1]).then_inc(fl_done, 1)
                    act.wait_ge(fl_done, done(lb * 2 + half + 1))
                    act.activation(rlf[:, :], rlf[:, :], ACT.Exp, scale=-0.5).then_inc(fr_done, 1)

                def scale_bias(lb, half):
                    act.wait_ge(fn_done, done(lb * 2 + half + 1))
                    for kc in range(2):
                        act.activation(cn[:, kc, half * 512:half * 512 + 512], cn[:, kc, half * 512:half * 512 + 512],
                                       ACT.Identity, scale=lnp[:, 0, kc:kc + 1], bias=lnp[:, 1, kc:kc + 1]).then_inc(hn_done, 1)

                def gate(lb, k):
                    act.wait_ge(g_full, done(lb * 12 + k + 1))
                    act.wait_ge(hh_done, done(lb * 12 + k - 1))
                    act.activation(ge[:, k % 2, :], ps[0:HP, 2 + k % 2, :], ACT.Gelu,
                                   bias=b1[:, 1, k % HB:k % HB + 1]).then_inc(ge_done, 1)

                def start(lb):
                    W0 = lb * WIN
                    squares(W0)
                    inverse_norms(W0)
                    squares(W0 + 1)
                    place_qk(W0, 0)
                    inverse_norms(W0 + 1)

                def sequence(lb, more):
                    W0 = act.snap(lb * WIN)
                    attend(W0, 0)
                    with act.Fori(0, 2) as j:
                        W1 = act.snap(W0 + j * 2 + 1)
                        attend(W1, 1)
                        attend(W1 + 1, 2)
                    for w in (5, 6, 7):
                        attend(W0 + w, w, lb)
                    act.wait_ge(wf_ready, sent((l + 1) * TENSORS_FFN))
                    inverse_deviation(lb, 0, 1)
                    scale_bias(lb, 0)
                    act.preload_act_table_set("gelu_and_others")
                    gate(lb, 0)
                    gate(lb, 1)
                    gate(lb, 2)
                    squared_deviations(lb, 1)
                    gate(lb, 3)
                    act.preload_act_table_set("natural_log_exp_and_others")
                    inverse_deviation(lb, 1, 5)
                    scale_bias(lb, 1)
                    act.preload_act_table_set("gelu_and_others")
                    for k in range(4, 2 * HB):
                        gate(lb, k)
                    act.preload_act_table_set("natural_log_exp_and_others")
                    if more:
                        start(lb + 1)

                start(l * nb)
                with act.Fori(0, nb - 1) as b:
                    sequence(act.snap(l * nb + b), True)
                sequence(act.snap(l * nb + (nb - 1)), False)

            act.preload_act_table_set("natural_log_exp_and_others")

            def unit(n, i):
                z, _, half = units[i]
                r = (rl, rlf)[i % 2]
                act.wait_ge(cen_done, done(nb * 2 + n + 1))
                act.wait_ge(var_full, done(nb * 2 + n))
                act.activation(sq[:, :, :], z[:, :, half * 512:half * 512 + 512], ACT.Square).then_inc(sq_done, 1)
                act.wait_ge(var_full, done(nb * 2 + n + 1))
                act.wait_ge(norm_done, done(nb * 2 + n - 1))
                act.activation(r[:, :], ps[:, 6 + i % 2, :], ACT.Ln, bias=eps_c[:, 0:1]).then_inc(lv_done, 1)
                act.wait_ge(lv_done, done(nb * 2 + n + 1))
                act.activation(r[:, :], r[:, :], ACT.Exp, scale=-0.5).then_inc(rs_done, 1)

            with act.Fori(0, nb // 2) as q:
                for i in range(4):
                    unit(q * 4 + i, i)

        @block.vector
        def _(dve):
            dve.memset(mc[:, :, :, :], NEG).then_inc(const_ready, 1)
            dve.memset(kt[96:128, :, :, :], -1.0).then_inc(const_ready, 1)
            dve.wait_ge(w_ready, sent(TENSORS_A))
            dve.tensor_copy(ident_b[:], identf[:]).then_inc(ident_ready, 1)
            dve.tensor_tensor(lam_t[:, :, :], lam_in[:, 0:2, :], lam_in[:, 2:4, :], ALU.mult).then_inc(lam_ready, 1)
            dve.wait_ge(lam_ready, done(2))
            dve.tensor_scalar(lam_t[:, :, :], lam_t[:, :, :], 1.0, None, ALU.add).then_inc(lam_ready, 1)
            dve.wait_ge(lam_ready, done(3))
            dve.reciprocal(lam_t[:, :, :], lam_t[:, :, :]).then_inc(lam_ready, 1)
            dve.wait_ge(lam_ready, done(4))
            dve.tensor_tensor(lam_t[:, 0, :], lam_t[:, 1, :], lam_t[:, 0, :], ALU.subtract).then_inc(lam_ready, 1)
            dve.wait_ge(lam_ready, done(5))
            dve.tensor_scalar(nlam[:, :, :], lam_t[:, 0, :].unsqueeze(2).broadcast_to([P, HEADS, VC]),
                              -LAMBDA_INIT, None, ALU.add).then_inc(lam_ready, 1)
            dve.tensor_tensor(gsc[:, :], gnp[:, 0:2], gnp[:, 2:3].broadcast_to([P, 2]), ALU.mult).then_inc(lam_ready, 1)
            dve.wait_ge(lam_ready, done(7))
            dve.tensor_scalar(gsc[:, :], gsc[:, :], 1.0 - LAMBDA_INIT, None, ALU.mult).then_inc(lam_ready, 1)
            dve.wait_ge(lam_ready, done(8))
            dve.wait_ge(const_ready, done(8))

            def feature_norm(k, src):
                for half in range(2):
                    zh = src[:, :, half * 512:half * 512 + 512]
                    dve.wait_ge(mean_full, done(k * 2 + half + 1))
                    dve.tensor_tensor(zh, zh, ps[:, 4 + half, :].unsqueeze(1).broadcast_to([P, 2, 512]),
                                      ALU.subtract).then_inc(cen_done, 1)
                for half in range(2):
                    zh = src[:, :, half * 512:half * 512 + 512]
                    dve.wait_ge(rs_done, done(k * 2 + half + 1))
                    dve.tensor_tensor(zh, zh, rl[:, :].unsqueeze(1).broadcast_to([P, 2, 512]),
                                      ALU.mult).then_inc(norm_done, 1)

            with dve.Fori(0, nb) as b:
                h0 = dve.snap(b * HEADS)
                def residual(k):
                    s = k if k < 8 else k + 8
                    c, n, half = k // 8, k % 8 // 2, k % 2
                    dve.wait_ge(high_done, done(b * 16 + k + 1))
                    dve.wait_ge(low_done, done(b * 16 + k - 1))
                    dve.tensor_tensor(rest[:, k % 2, :], ps[:, s % 4, :], part[:, 0, n, c, half * 512:half * 512 + 512],
                                      ALU.subtract).then_inc(rest_done, 1)

                def piece(g, k, slot, parity):
                    r, c0, w, diag = PIECES[k % 12]
                    i, bank = k // 12, bank_of(parity)
                    dve.wait_ge(max_full, done(slot + 1))
                    if k == 0:
                        dve.wait_ge(mx_done, done(g))
                    into = mc[:, i, c0 // 512, r:r + 1]
                    if diag:
                        dve.wait_ge(max_free, done(slot - 1))
                        dve.sem_inc(dve_passed, 1)
                        ins = dve.tensor_tensor_reduce(out=junk[:, bank - 6, 0:w], in0=ps[:, bank, 0:w],
                                                       in1=causal[:, 512 - w:512], scale=1.0, scalar=NEG,
                                                       op0=ALU.add, op1=ALU.max, accum_out=into)
                    else:
                        ins = dve.reduce_max(into, ps[:, bank, 0:w], AX_X)
                    ins.then_inc(max_free, 1)

                def two_parts(g, slot):
                    dve.wait_ge(max_free, done(slot + 1))
                    dve.tensor_tensor(mm[:, :, :], mc[:, :, 0, :], mc[:, :, 1, :], ALU.max).then_inc(mx_done, 1)
                    dve.wait_ge(mx_done, done(g + 1))
                    dve.tensor_copy(nm[:, 0, :, :], mm[:, :, :]).then_inc(mc_done, 1)
                    dve.wait_ge(mc_done, done(g + 1))
                    dve.tensor_tensor(nm[:, 1, :, :], mm[:, :, :], nm[:, 0, :, :], ALU.subtract).then_inc(nm_done, 1)

                def copy_maxima(g, slot, parity):
                    dve.wait_ge(max_full, done(slot + 1))
                    dve.wait_ge(mrow_ready, sent(2 * g))
                    dve.tensor_copy(mt[:, :], psb[0:32, bank_of(parity), 0:P]).then_inc(max_free, 1)

                def normalise(g, u):
                    dve.wait_ge(rb_done, done(g + 1))
                    dve.wait_ge(y_ready[u % 2], sent(g - u % 2))
                    dve.tensor_tensor(wy[:, u % 2, :], ev[0:64, :], rb[:, :], ALU.mult).then_inc(wy_done, 1)

                first = dve.snap(h0 * SLOTS)
                for k in range(8):
                    residual(k)
                for k in range(24):
                    piece(h0, k, first + k, k)
                two_parts(h0, first + 23)
                for n in range(8):
                    residual(8 + n)
                    if n == 0:
                        copy_maxima(h0, first + 24, 24)
                    for k in range(3 * n, 3 * n + 3):
                        piece(h0 + 1, k, first + (SLOTS + k), SLOTS + k)
                two_parts(h0 + 1, first + (SLOTS + 23))

                def statistics(j):
                    dve.tensor_tensor(ya[:, j, :], ya[:, j, :], yb[:, j, :], ALU.add).then_inc(ysum_done, 1)
                    dve.wait_ge(ysum_done, done(b * 4 + j + 1))
                    for half in range(2):
                        dve.bn_stats(bs[:, j, half, :], ya[:, j, half * 512:half * 512 + 512]).then_inc(bn_done, 1)
                    dve.wait_ge(bn_done, done(b * 8 + 2 * j + 2))
                    dve.sem_inc(dve_passed, 1)
                    dve.bn_aggr(mv[:, j, :], bs[:, j, :, :].rearrange("p a s -> p (a s)")).then_inc(bnag_done, 1)

                def over_time(n):
                    of = slice(3 * n, 3 + n)
                    dve.wait_ge(gr_done, done(b * 2 + n + 1))
                    dve.tensor_scalar(ga[:, of], gl[:, of], gsc[:, 0:1], None, ALU.mult).then_inc(ga_done, 1)
                    dve.wait_ge(ga_done, done(b * 2 + n + 1))
                    dve.tensor_tensor(gb[:, of], mv[:, of, 0], ga[:, of], ALU.mult).then_inc(gt_done, 1)
                    dve.wait_ge(gt_done, done(b * 2 + n + 1))
                    dve.tensor_scalar(gb[:, of], gb[:, of], -1.0, gsc[:, 1:2], ALU.mult, ALU.add).then_inc(gb_done, 1)
                    dve.wait_ge(gb_done, done(b * 2 + n + 1))
                    for j in range(3 * n, 3 + n):
                        dve.tensor_scalar(ya[:, j, :], ya[:, j, :], ga[:, j:j + 1], gb[:, j:j + 1],
                                          ALU.mult, ALU.add).then_inc(yn_done, 1)

                def heads(g0, slots, first, last):
                    for u in range(UNROLL):
                        g = g0 + u
                        slot, parity = slots + u * SLOTS, 1 + u
                        if not (last and u >= UNROLL - 2):
                            for k in range(24):
                                if k == T_AT:
                                    copy_maxima(g + 1, slot + k, parity + k)
                                if k == T_AT + 1 and not (first and u == 0):
                                    normalise(g - 1, (u + 1) % 2)
                                piece(g + 2, k, slot + slot_of(k), parity + slot_of(k))
                            two_parts(g + 2, slot + 24)
                        else:
                            if u == UNROLL - 2:
                                copy_maxima(g + 1, slot, parity)
                                dve.wait_ge(y_ready[0], sent(h0 + 14))
                                dve.wait_ge(y_ready[1], sent(h0 + 12))
                                for j in range(3):
                                    statistics(j)
                                normalise(g - 1, (u + 1) % 2)
                            else:
                                normalise(g - 1, (u + 1) % 2)
                                over_time(0)

                heads(h0, dve.snap(h0 * SLOTS + AHEAD), True, False)
                with dve.Fori(1, HEADS // UNROLL - 1) as j:
                    g0 = dve.snap(b * HEADS + j * UNROLL)
                    heads(g0, dve.snap(g0 * SLOTS + AHEAD), False, False)
                g0 = dve.snap(b * HEADS + HEADS - UNROLL)
                heads(g0, dve.snap(g0 * SLOTS + AHEAD), False, True)
                normalise(g0 + UNROLL - 1, 1)

                for p in range(2):
                    dve.wait_ge(y_ready[p], sent((b + 1) * HEADS))
                statistics(3)
                over_time(1)
                for n, (oc, half) in enumerate([(0, 0), (1, 0), (0, 1), (1, 1)]):
                    dve.wait_ge(out_full, done(b * 4 + n + 1))
                    dve.tensor_tensor(z[:, oc, half * 512:half * 512 + 512], ps[:, n, :],
                                      xt[:, oc, half * 512:half * 512 + 512], ALU.add).then_inc(z_done, 1)
                feature_norm(b, z)

            with dve.Fori(0, LAYERS) as l:
                dve.wait_ge(wl_ready, sent((l + 1) * TENSORS_ATTENTION))
                dve.wait_ge(k2_ready, done(5))
                dve.wait_ge(tab_ready, sent(1))
                dve.tensor_tensor(tab[:, :, :, :].rearrange("p w a e -> p w (a e)"), tabc[:, :, :, :].rearrange("p w a e -> p w (a e)"),
                                  scl[:, :, :].rearrange("p a e -> p (a e)").unsqueeze(1).broadcast_to([P, WIN, 4 * LD]),
                                  ALU.mult).then_inc(tab_done, 1)
                dve.wait_ge(tab_done, done(l + 1))
                dve.sem_inc(dve_passed, 1)
                def norms(W):
                    dve.wait_ge(sqw_done, done(W + 1))
                    dve.wait_ge(rot_done, done(W))
                    dve.reduce_sum(rn[:, :], sqw[:, :].rearrange("p (h e) -> p h e", e=LD), AX_X).then_inc(ssq_done, 1)
                    dve.wait_ge(ssq_done, done(W + 1))
                    dve.tensor_scalar(rn[:, :], rn[:, :], 1e-24, float(2 ** (2 * NORM_SHIFT)),
                                      ALU.max, ALU.mult).then_inc(ssc_done, 1)

                def rotate(w, W, k):
                    src = ps[:, 0:2, :].rearrange("p a (h e) -> p a h e", e=LD)
                    t = tab[:, bass.ds(w, 1), :, :].rearrange("p w (a s) e -> p (w a) s e", s=2)
                    if k == 0:
                        dve.wait_ge(rsum_done, done(W))
                        dve.wait_ge(sqw_done, done(W + 1))
                        dve.tensor_tensor(ra[:, :, :, :], src, t[:, :, 0:1, :].broadcast_to([P, 2, LHEADS, LD]),
                                          ALU.mult).then_inc(ra_done, 1)
                    else:
                        if k == 1:
                            dve.wait_ge(tq_full, done(W))
                        lo, frm = (0, 32) if k == 1 else (32, 0)
                        dve.tensor_tensor(rr[:, :, :, lo:lo + 32], src[:, :, :, frm:frm + 32],
                                          t[:, :, 1:2, lo:lo + 32].broadcast_to([P, 2, LHEADS, 32]),
                                          ALU.mult).then_inc(ra_done, 1)

                def largest(W, w, hp):
                    dve.wait_ge(s_full, done(W * 4 + hp + 1))
                    dve.wait_ge(t_full, done(W * 5 + (-1, 1, 2, 3)[hp]))
                    dve.sem_inc(dve_passed, 1)
                    n = P if w == 0 else 256
                    for q in range(2):
                        i = dve.tensor_tensor_reduce(out=sm[:, hp % 2, q, 0:n], in0=ps[:, 4 + hp % 2, q * 256:q * 256 + n],
                                                     in1=window[:, w % 2, 0:n], scale=-1.0, scalar=-NEG,
                                                     op0=ALU.add, op1=ALU.min, accum_out=mxw[:, hp, q:q + 1])
                    i.then_inc(s_read, 1)

                def normalise(W, w, hp):
                    dve.wait_ge(e_done, done(W * 4 + hp + 1))
                    dve.reciprocal(sumw[:, hp, :], sumw[:, hp, :]).then_inc(rc_done, 1)
                    dve.wait_ge(rc_done, done(W * 4 + hp + 1))
                    n = P if w == 0 else 256
                    for q in range(2):
                        i = dve.tensor_scalar(sm[:, hp % 2, q, 0:n], sm[:, hp % 2, q, 0:n], sumw[:, hp, q:q + 1], None, ALU.mult)
                    i.then_inc(p_ready, 1)

                def attend(W, w, at, lb=None):
                    largest(W, w, 1)
                    normalise(W, w, 0)
                    normalise(W, w, 1)
                    largest(W, w, 2)
                    normalise(W, w, 2)
                    largest(W, w, 3)
                    if w == WIN - 1:
                        centre(lb, 0, 0)
                    normalise(W, w, 3)
                    if w < WIN - 2:
                        norms(W + 2)
                    if w < WIN - 2:
                        for k in range(3):
                            rotate(at + 2, W + 2, k)
                    elif w == WIN - 2:
                        residual(lb, 0, 0)
                    if w < WIN - 1:
                        largest(W + 1, w + 1, 0)
                    dve.wait_ge(o_full, done(W * 4 + 4))
                    dve.tensor_copy(ot[:, :, bass.ds(at * P, P)], ps[:, 7, :].rearrange("p (a q) -> p a q", a=4)).then_inc(o_read, 1)

                def residual(lb, half, bank):
                    for oc in range(2):
                        at = slice(1 + half * 512, 1 + half * 512 + 512)
                        dve.wait_ge(wo_full, done(lb * 4 + 2 * half + oc + 1))
                        dve.tensor_tensor(xm[:, oc, at], ps[:, bank + oc, :], xs[:, oc, at], ALU.add).then_inc(xm_done, 1)

                def centre(lb, half, bank):
                    dve.wait_ge(xm_done, done(lb * 4 + 2 * half + 2))
                    dve.wait_ge(fm_full, done(lb * 2 + half + 1))
                    for kc in range(2):
                        dve.tensor_tensor(cn[:, kc, half * 512:half * 512 + 512],
                                          xm[:, kc, 1 - kc + half * 512:1 - kc + half * 512 + 512],
                                          ps[:, bank, :], ALU.subtract).then_inc(fc_done, 1)

                def divide(lb, half):
                    ch = cn[:, :, half * 512:half * 512 + 512]
                    dve.wait_ge(fr_done, done(lb * 2 + half + 1))
                    dve.tensor_tensor(ch, ch, rlf[:, :].unsqueeze(1).broadcast_to([P, 2, 512]), ALU.mult).then_inc(fn_done, 1)

                def gated(lb, k):
                    dve.wait_ge(a_full, done(lb * 12 + k + 1))
                    dve.wait_ge(ge_done, done(lb * 12 + k + 1))
                    dve.scalar_tensor_tensor(hh[:, k // HB, k % HB, :], ps[0:HP, k % 2, :], b1[:, 0, k % HB:k % HB + 1],
                                             ge[:, k % 2, :], ALU.add, ALU.mult).then_inc(hh_done, 1)

                def output(lb, half):
                    dve.wait_ge(storedb, sent(lb * 2))
                    for oc in range(2):
                        dve.wait_ge(w2_full, done(lb * 4 + half * 2 + oc + 1))
                        dve.scalar_tensor_tensor(xo[:, oc, half * 512:half * 512 + 512], ps[:, 4 + 2 * half + oc, :],
                                                 b2[:, oc:oc + 1], xm[:, oc, 1 + half * 512:1 + half * 512 + 512],
                                                 ALU.add, ALU.add).then_inc(xo_done, 1)

                def start_1(lb):
                    for k in range(3):
                        rotate(0, lb * WIN, k)
                    norms(lb * WIN)

                def start_2(lb):
                    W0 = lb * WIN
                    rotate(1, W0 + 1, 0)
                    norms(W0 + 1)
                    rotate(1, W0 + 1, 1)
                    rotate(1, W0 + 1, 2)
                    largest(W0, 0, 0)

                def sequence(lb, more):
                    W0 = dve.snap(lb * WIN)
                    attend(W0, 0, 0)
                    with dve.Fori(0, 2) as j:
                        odd = dve.snap(j * 2 + 1)
                        W1 = dve.snap(W0 + odd)
                        attend(W1, 1, odd)
                        attend(W1 + 1, 2, odd + 1)
                    for w in (5, 6, 7):
                        attend(W0 + w, w, w, lb)
                    divide(lb, 0)
                    gated(lb, 0)
                    gated(lb, 1)
                    residual(lb, 1, 6)
                    gated(lb, 2)
                    centre(lb, 1, 4)
                    gated(lb, 3)
                    divide(lb, 1)
                    for k in range(4, 2 * HB):
                        gated(lb, k)
                    output(lb, 0)
                    if more:
                        start_1(lb + 1)
                    output(lb, 1)
                    if more:
                        start_2(lb + 1)
                    else:
                        dve.wait_ge(xo_done, done(lb * 4 + 4))

                start_1(l * nb)
                start_2(l * nb)
                with dve.Fori(0, nb - 1) as b:
                    sequence(dve.snap(l * nb + b), True)
                sequence(dve.snap(l * nb + (nb - 1)), False)

            def add_unit(n, q, i):
                z, x, half = units[i]
                h = slice(half * 512, half * 512 + 512)
                dve.wait_ge(z_ready[i], sent(q * 2 + 2))
                dve.tensor_tensor(z[:, :, h], z[:, :, h], x[:, :, h], ALU.add).then_inc(zsum_done, 1)

            def centre_unit(n, i):
                z, _, half = units[i]
                zh = z[:, :, half * 512:half * 512 + 512]
                dve.wait_ge(mean_full, done(nb * 2 + n + 1))
                dve.tensor_tensor(zh, zh, ps[:, 4 + i % 2, :].unsqueeze(1).broadcast_to([P, 2, 512]),
                                  ALU.subtract).then_inc(cen_done, 1)

            def divide_unit(n, i):
                z, _, half = units[i]
                zh = z[:, :, half * 512:half * 512 + 512]
                dve.wait_ge(rs_done, done(nb * 2 + n + 1))
                dve.tensor_tensor(zh, zh, (rl, rlf)[i % 2][:, :].unsqueeze(1).broadcast_to([P, 2, 512]),
                                  ALU.mult).then_inc(norm_done, 1)

            def four(n, q, first):
                for i in range(4):
                    if not (first and i == 0):
                        centre_unit(n + (i - 1), (i + 3) % 4)
                    add_unit(n + i, q, i)
                    if not (first and i < 2):
                        divide_unit(n + (i - 2), (i + 2) % 4)

            four(0, 0, True)
            with dve.Fori(1, nb // 2) as q:
                four(dve.snap(q * 4), q, False)
            centre_unit(nb * 2 - 1, 3)
            divide_unit(nb * 2 - 2, 2)
            divide_unit(nb * 2 - 1, 3)

        @block.gpsimd
        def _(pool):
            for s in counters:
                pool.sem_inc(s, START)
            pool.memset(ones[:], 1.0).then_inc(const_ready, 1)
            pool.memset(mean_w[:], 1.0 / 256).then_inc(const_ready, 1)
            pool.memset(eps_c[:], EPS).then_inc(const_ready, 1)
            pool.memset(causal[:], 0.0).then_inc(const_ready, 1)
            pool.memset(junk[:], 0.0).then_inc(const_ready, 1)
            pool.wait_ge(const_ready, done(7))
            pool.affine_select(out=causal[:], in_=causal[:], compare_op=ALU.is_ge, fill=NEG, base=512 - P,
                               pattern=[[-1, 512]], channel_multiplier=1).then_inc(const_ready, 1)
            pool.wait_ge(lam_ready, done(8))
            with pool.Fori(0, nb) as b:
                h0 = pool.snap(b * HEADS)
                def low_parts(k):
                    c, n, half = k // 8, k % 8 // 2, k % 2
                    pool.wait_ge(mid_done, done(b * 16 + k + 1))
                    pool.tensor_tensor(part[:, 2, n, c, half * 512:half * 512 + 512], rest[:, k % 2, :],
                                       part[:, 1, n, c, half * 512:half * 512 + 512], ALU.subtract).then_inc(low_done, 1)

                def place_values(g, h, par, i):
                    v = va[:, :, bass.ds(h * VC, VC)]
                    if i == 0:
                        pool.wait_ge(pv_done, done((g - 1) * 8))
                        pool.sem_inc(pool_passed, 1)
                        pool.tensor_copy(vs[:, par, :, 0, :], v)
                    else:
                        pool.tensor_tensor(vs[:, par, :, 1, :], v, nlam[:, bass.ds(h, 1), :].broadcast_to([P, 8, VC]),
                                           ALU.mult).then_inc(vs_ready, 1)

                for k in range(8):
                    low_parts(k)
                pool.wait_ge(v_done, done(b * 8 + 8))
                place_values(h0, 0, 0, 0)
                place_values(h0, 0, 0, 1)
                for k in range(8, 16):
                    low_parts(k)

                def heads(g0, hh, last):
                    for u in range(UNROLL):
                        g = g0 + u
                        for kb in range(8):
                            pool.wait_ge(exp_done, done(g * 16 + 2 * kb + 2))
                            pool.sem_inc(pool_passed, 1)
                            diag = pt[:, kb % 2, :, kb * P:(kb + 1) * P]
                            pool.affine_select(out=diag, in_=diag, compare_op=ALU.is_ge, fill=0.0, base=0,
                                               pattern=[[0, 2], [1, P]], channel_multiplier=-1).then_inc(masked, 1)
                            if kb < 2 and not (last and u == UNROLL - 1):
                                place_values(g + 1, hh + u + 1, (u + 1) % 2, kb)

                with pool.Fori(0, HEADS // UNROLL - 1) as j:
                    heads(pool.snap(b * HEADS + j * UNROLL), pool.snap(j * UNROLL), False)
                heads(pool.snap(b * HEADS + HEADS - UNROLL), HEADS - UNROLL, True)

            pool.wait_ge(stored, sent(nb * 2))
            pool.memset(window[:], 0.0).then_inc(k2_ready, 1)
            pool.memset(qp[:], 0.0).then_inc(k2_ready, 1)
            pool.memset(xs[:, :, 0:1], 0.0).then_inc(k2_ready, 1)
            pool.memset(xm[:, :, 0:1], 0.0).then_inc(k2_ready, 1)
            pool.wait_ge(k2_ready, done(4))
            for par in range(2):
                own, prev = window[:, par, par * P:(par + 1) * P], window[:, par, (1 - par) * P:(2 - par) * P]
                pool.affine_select(out=own, in_=own, compare_op=ALU.is_ge, fill=NEG, base=0,
                                   pattern=[[-1, P]], channel_multiplier=1)
                i = pool.affine_select(out=prev, in_=prev, compare_op=ALU.is_ge, fill=NEG, base=0,
                                       pattern=[[1, P]], channel_multiplier=-1)
            i.then_inc(k2_ready, 1)
            with pool.Fori(0, LAYERS) as l:
                with pool.Fori(0, nb) as b:
                    W0 = pool.snap((l * nb + b) * WIN)

                    def combine(W):
                        pool.wait_ge(rn_done, done(W + 1))
                        pool.tensor_tensor(nt[:, :], rn2[:, :], rn2[:, :], ALU.mult).then_inc(nt_done, 1)
                        pool.wait_ge(nt_done, done(W * 4 + 1))
                        pool.tensor_tensor(nt[:, :], nt[:, :], rn[:, :], ALU.mult).then_inc(nt_done, 1)
                        pool.wait_ge(nt_done, done(W * 4 + 2))
                        pool.sem_inc(pool_passed, 1)
                        pool.tensor_scalar(nt[:, :], nt[:, :], -0.5, 1.5, ALU.mult, ALU.add).then_inc(nt_done, 1)
                        pool.wait_ge(nt_done, done(W * 4 + 3))
                        pool.tensor_tensor(nt[:, :], nt[:, :], rn2[:, :], ALU.mult).then_inc(nt_done, 1)
                        pool.wait_ge(nt_done, done(W * 4 + 4))
                        pool.wait_ge(ra_done, done(W * 3 + 3))
                        flat = lambda t: t[:, :, :, :].rearrange("p a h e -> p (a h e)")
                        pool.tensor_tensor(flat(rr), flat(ra), flat(rr), ALU.add).then_inc(rsum_done, 1)
                        pool.wait_ge(rsum_done, done(W + 1))
                        r3 = rr[:, :, :, :].rearrange("p a h e -> p (a h) e")
                        pool.tensor_tensor(r3, r3, nt[:, :].unsqueeze(2).broadcast_to([P, 2 * LHEADS, LD]),
                                           ALU.mult).then_inc(rot_done, 1)

                    def tokens(w, W, par):
                        pool.wait_ge(v_full, done(W - 1))
                        pool.sem_inc(pool_passed, 1)
                        for kc in range(2):
                            i = pool.tensor_copy(xw[:, par, kc, :], xs[:, kc, bass.ds(w * P + (1 - kc), P)])
                        i.then_inc(xw_ready, 1)

                    pool.wait_ge(xin_ready, sent(l * nb + b + 1))
                    pool.wait_ge(xm_done, done((l * nb + b) * 4))
                    pool.sem_inc(pool_passed, 1)
                    pool.tensor_copy(xs[:, :, 1:1025], xin[:, :, :]).then_inc(xs_ready, 1)
                    pool.wait_ge(xs_ready, done(l * nb + b + 1))
                    tokens(0, W0, 0)
                    tokens(1, W0 + 1, 1)
                    combine(W0)
                    with pool.Fori(0, WIN // 2 - 1) as j:
                        w = pool.snap(j * 2)
                        W = pool.snap(W0 + w)
                        for par in range(2):
                            combine(W + (par + 1))
                            tokens(w + (par + 2), W + (par + 2), par)
                    combine(W0 + (WIN - 1))


def rotary_tables(np):
    f = np.float32
    n = WIN * P
    half = np.arange(0, LD, 2, dtype=f)
    inv = f(1.0) / f(10000.0) ** (half / f(LD))
    t = np.arange(n, dtype=f)
    ang = t[:, None] * inv[None, :]
    base = (half + f(0.4 * LD)) / f(1.4 * LD)
    decay = base[None, :].astype(f) ** ((t - n // 2) / f(64.0))[:, None]
    cos, sin = np.cos(ang), np.sin(ang)
    up = f(2.0 ** NORM_SHIFT)
    rows = [np.concatenate([cos, cos], 1) * np.concatenate([decay, decay], 1) * f(8.0) * up,
            np.concatenate([-sin, sin], 1) * np.concatenate([decay, decay], 1) * f(8.0) * up,
            np.concatenate([cos, cos], 1) / np.concatenate([decay, decay], 1) * up,
            np.concatenate([-sin, sin], 1) / np.concatenate([decay, decay], 1) * up]
    tab = np.stack(rows, 1).astype(f)
    return tab.reshape(WIN, P, 4, LD).transpose(1, 0, 2, 3)


def layouts(inp):
    import numpy as np

    f = {k.removeprefix("L0_"): np.asarray(v) for k, v in inp.items()}
    out = {}
    nb = f["attn_x"].shape[0]
    out["x"] = f["attn_x"].transpose(0, 2, 1).reshape(nb, 2, P, 1024)
    w = np.stack([f["attn_" + n].T for n in ("Wq1", "Wq2", "Wk1", "Wk2")])
    out["wqk"] = w.reshape(4, 2, P, 2, P).transpose(2, 1, 0, 3, 4)
    out["wv"] = f["attn_Wv"].T.reshape(2, P, 512).transpose(1, 0, 2)
    out["wc"] = f["attn_Wc"].T.reshape(4, P, 256).transpose(1, 0, 2)
    out["gnp"] = np.stack([np.tile(f["attn_" + n], 4) for n in ("gn_w", "gn_b", "gamma")], 1)
    lam = np.stack([f["attn_" + n].reshape(HEADS) for n in ("lq1", "lq2", "lk1", "lk2")])
    out["lam"] = np.broadcast_to(lam, (P, 4, HEADS))
    out["identf"] = np.eye(P, dtype=np.float32)

    flat = lambda a: a.reshape(LAYERS, a.shape[1], -1)
    out["wqkv"] = flat(f["ffn_wqkv"].reshape(LAYERS, 2, P, 1536).transpose(0, 2, 1, 3))
    out["wo"] = flat(f["ffn_wo"].reshape(LAYERS, 4, P, 256).transpose(0, 2, 1, 3))
    pad = HB * HP - HID
    w1 = f["ffn_w1"].reshape(LAYERS, 2, P, 2, HID)
    w1 = np.pad(w1, [(0, 0)] * 4 + [(0, pad)])
    out["w1"] = flat(w1.reshape(LAYERS, 2, P, 2, HB, HP).transpose(0, 2, 1, 3, 4, 5))
    w2 = np.pad(f["ffn_w2"], [(0, 0), (0, pad), (0, 0)])
    out["w2"] = flat(w2.reshape(LAYERS, HB, HP, 256).transpose(0, 2, 1, 3))
    b1 = np.pad(f["ffn_b1"].reshape(LAYERS, 2, HID), [(0, 0), (0, 0), (0, pad)])
    out["b1"] = flat(b1.reshape(LAYERS, 2, HB, HP).transpose(0, 3, 1, 2))
    out["b2"] = flat(f["ffn_b2"].reshape(LAYERS, 2, P).transpose(0, 2, 1))
    ln = np.stack([f["ffn_ln_g"], f["ffn_ln_b"]], 1).reshape(LAYERS, 2, 2, P)
    out["lnp"] = flat(ln.transpose(0, 3, 1, 2))
    qs, ks = f["ffn_q_scale"], f["ffn_k_scale"]
    scl = np.stack([qs, np.roll(qs, 32, 1), ks, np.roll(ks, 32, 1)], 1)
    out["scl"] = flat(np.broadcast_to(scl[:, None], (LAYERS, P, 4, LD)))
    out["tabc"] = rotary_tables(np)
    return {k: np.ascontiguousarray(v) for k, v in out.items()}

_INS = ["x", "wqk", "wv", "wc", "gnp", "lam", "identf", "wqkv", "wo", "w1", "w2", "b1", "b2", "lnp", "scl", "tabc"]


def kernel(**inputs):
    import numpy as _np
    import concourse.bacc as _bacc
    from concourse import mybir as _mybir
    from concourse.bass_utils import run_bass_kernel_spmd as _run

    nc = _bacc.Bacc("TRN2", target_bir_lowering=False, num_devices=1)
    laid = layouts(inputs)
    nb = laid["x"].shape[0]
    arrays, d = {}, {}
    for name in _INS:
        a = laid[name]
        arrays[f"in_{name}"] = a
        d[name] = nc.dram_tensor(f"in_{name}", a.shape, _mybir.dt.from_np(a.dtype), kind="ExternalInput").ap()
    d["sx"] = nc.dram_tensor("between_phases", (nb * (LAYERS + 1), 2, P, 1024), _mybir.dt.float32, kind="Internal").ap()
    d["out"] = nc.dram_tensor("out", (nb, 2, P, 1024), _mybir.dt.float32, kind="ExternalOutput").ap()
    program(nc, d, nb)
    r = _run(nc, [arrays], core_ids=[0])
    return r.results[0]["out"].reshape(nb, 256, 1024).transpose(0, 2, 1)
```
